# Optimizing a Trainium2 kernel written in Bass

```python
import numpy as np
import jax
import jax.numpy as jnp

def _softmax(x, axis=-1):
    return jax.nn.softmax(x, axis=axis)

def _gelu(x):
    return jax.nn.gelu(x, approximate=True)

def _silu(x):
    return jax.nn.silu(x)

def _sigmoid(x):
    return jax.nn.sigmoid(x)

def _layernorm(x, axis=-1, eps=1e-05):
    m = jnp.mean(x, axis=axis, keepdims=True)
    v = jnp.var(x, axis=axis, keepdims=True)
    return (x - m) / jnp.sqrt(v + eps)

def _scatter_add(tgt, idx, src, axis=0):
    return tgt.at[idx].add(src)

def _segment_sum(src, seg, n):
    return jax.ops.segment_sum(src, seg, n)
kernel_name = 'mk_recurrent_d2_jaxref_r8_7eb036'

def setup_inputs(seed: int=0):
    np.random.seed(seed)
    _w = jnp.asarray

    def _L0_attn_setup():
        import jax, jax.numpy as jnp
        import numpy as np
        NUM_HEADS = 16
        EPS = 1e-06

        def _phi(x):
            return jax.nn.elu(x) + 1.0
        key = jax.random.key(seed)
        ks = jax.random.split(key, 5)
        B, L, D = (4, 1024, 128)
        scale = 0.02
        return {'x': jax.random.normal(ks[0], (B, L, D), dtype=jnp.float32), 'Wq': jax.random.normal(ks[1], (D, D), dtype=jnp.float32) * scale, 'Wk': jax.random.normal(ks[2], (D, D), dtype=jnp.float32) * scale, 'Wv': jax.random.normal(ks[3], (D, D), dtype=jnp.float32) * scale, 'Wo': jax.random.normal(ks[4], (D, D), dtype=jnp.float32) * scale}
    _L0_attn_in = _L0_attn_setup()

    def _L0_ffn_setup():
        import jax, jax.numpy as jnp
        import numpy as np
        E = 8
        D = 128
        F = 512
        S, B = (256, 2)
        LN_EPS = 1e-05

        def _moe_forward(input_features, centroids, ln_g, ln_b, W1, b1, W2, b2):
            s, b, d = input_features.shape
            x = jnp.swapaxes(input_features, 0, 1).reshape(-1, d)
            logits = x.astype(jnp.float32) @ centroids.astype(jnp.float32).T
            assign = jnp.argmax(logits, axis=-1)
            onehot = jax.nn.one_hot(assign, E, dtype=x.dtype)
            disp = jnp.einsum('te,td->etd', onehot, x)
            mu = disp.mean(-1, keepdims=True)
            var = disp.var(-1, keepdims=True)
            xn = (disp - mu) * jax.lax.rsqrt(var + LN_EPS)
            xn = xn * ln_g[:, None, :] + ln_b[:, None, :]
            h = jax.nn.relu(jnp.einsum('etd,edf->etf', xn, W1) + b1[:, None, :])
            y = jnp.einsum('etf,efd->etd', h, W2) + b2[:, None, :]
            y = disp + y
            out = jnp.einsum('te,etd->td', onehot, y)
            return jnp.swapaxes(out.reshape(b, s, d), 0, 1)
        key = jax.random.key(seed)
        ks = jax.random.split(key, 8)
        scale_in = 1.0 / np.sqrt(D)
        scale_ff = 1.0 / np.sqrt(F)
        return {'input_features': jax.random.normal(ks[0], (S, B, D), dtype=jnp.float32), 'centroids': jax.random.normal(ks[1], (E, D), dtype=jnp.float32) * scale_in, 'ln_g': jnp.ones((E, D), dtype=jnp.float32), 'ln_b': jnp.zeros((E, D), dtype=jnp.float32), 'W1': jax.random.normal(ks[2], (E, D, F), dtype=jnp.float32) * scale_in, 'b1': jax.random.normal(ks[3], (E, F), dtype=jnp.float32) * 0.01, 'W2': jax.random.normal(ks[4], (E, F, D), dtype=jnp.float32) * scale_ff, 'b2': jax.random.normal(ks[5], (E, D), dtype=jnp.float32) * 0.01}
    _L0_ffn_in = _L0_ffn_setup()

    def _L1_attn_setup():
        import jax, jax.numpy as jnp
        import numpy as np
        D = 128
        H = 16
        N = D // H
        B = 4
        T = 256
        NLAYERS = 12
        LAYER_ID = 6
        EPS = 1e-05 * 64

        def _forward(x, w_r, w_k, w_v, w_g, w_o, time_maa_k, time_maa_v, time_maa_r, time_maa_g, time_decay, time_faaaa, ln_g, ln_b):
            Bs, Ts, C = x.shape
            if Ts % 32 == 0:
                Q = 32
            elif Ts % 128 == 0:
                Q = 128
            else:
                Q = Ts
            nC = Ts // Q
            xs = jnp.pad(x, ((0, 0), (1, 0), (0, 0)))[:, :-1]
            xx = xs - x
            xk = x + xx * time_maa_k
            xv = x + xx * time_maa_v
            xr = x + xx * time_maa_r
            xg = x + xx * time_maa_g
            r = (xr @ w_r.T).reshape(Bs, Ts, H, N).transpose(0, 2, 1, 3)
            k = (xk @ w_k.T).reshape(Bs, Ts, H, N).transpose(0, 2, 3, 1)
            v = (xv @ w_v.T).reshape(Bs, Ts, H, N).transpose(0, 2, 1, 3)
            g = jax.nn.silu(xg @ w_g.T)
            w = jnp.exp(-jnp.exp(time_decay))
            u = time_faaaa
            ws = (w ** Q)[None, :, None, None]
            q = jnp.arange(Q)
            wk = (w[:, None] ** (Q - 1 - q)[None, :])[None, :, None, :]
            wb = (w[:, None] ** q[None, :])[None, :, :, None]
            ii = q[:, None]
            jj = q[None, :]
            e = jnp.maximum(ii - jj - 1, 0)
            Wmat = jnp.where((jj < ii)[None], w[:, None, None] ** e[None], 0.0)
            Wmat = Wmat + jnp.eye(Q, dtype=x.dtype)[None] * u[:, None, None]
            Wmat = Wmat[None]
            rC = r.reshape(Bs, H, nC, Q, N).transpose(2, 0, 1, 3, 4)
            kC = k.reshape(Bs, H, N, nC, Q).transpose(3, 0, 1, 2, 4)
            vC = v.reshape(Bs, H, nC, Q, N).transpose(2, 0, 1, 3, 4)

            def step(state, inp):
                rr, kk, vv = inp
                y = rr @ kk * Wmat @ vv + rr @ state * wb
                state = ws * state + kk * wk @ vv
                return (state, y)
            state0 = jnp.zeros((Bs, H, N, N), x.dtype)
            _, yC = jax.lax.scan(step, state0, (rC, kC, vC))
            y = yC.transpose(1, 2, 0, 3, 4).reshape(Bs, H, Ts, N)
            y = y.transpose(0, 2, 1, 3).reshape(Bs * Ts, H, N)
            mu = y.mean(-1, keepdims=True)
            var = y.var(-1, keepdims=True)
            y = (y - mu) / jnp.sqrt(var + EPS)
            y = y.reshape(Bs, Ts, C) * ln_g + ln_b
            y = y * g
            return y @ w_o.T
        key = jax.random.key(seed)
        ks = jax.random.split(key, 6)
        r01 = LAYER_ID / (NLAYERS - 1)
        r10 = 1.0 - LAYER_ID / NLAYERS
        ddd = np.arange(D, dtype=np.float64) / D
        maa_k = (1.0 - ddd ** r10).astype(np.float32)
        maa_v = (1.0 - (ddd ** r10 + 0.3 * r01)).astype(np.float32)
        maa_r = (1.0 - ddd ** (0.5 * r10)).astype(np.float32)
        maa_g = maa_r.copy()
        hh = np.arange(H, dtype=np.float64)
        decay = (-6.0 + 5.0 * (hh / (H - 1)) ** (0.7 + 1.3 * r01)).astype(np.float32)
        faaaa = (r01 * (1.0 - hh / (H - 1))).astype(np.float32)
        s = 0.02
        return {'x': jax.random.normal(ks[0], (B, T, D), jnp.float32), 'w_r': jax.random.normal(ks[1], (D, D), jnp.float32) * s, 'w_k': jax.random.normal(ks[2], (D, D), jnp.float32) * s, 'w_v': jax.random.normal(ks[3], (D, D), jnp.float32) * s, 'w_g': jax.random.normal(ks[4], (D, D), jnp.float32) * s, 'w_o': jax.random.normal(ks[5], (D, D), jnp.float32) * s, 'time_maa_k': jnp.asarray(maa_k), 'time_maa_v': jnp.asarray(maa_v), 'time_maa_r': jnp.asarray(maa_r), 'time_maa_g': jnp.asarray(maa_g), 'time_decay': jnp.asarray(decay), 'time_faaaa': jnpp if False else jnp.asarray(faaaa), 'ln_g': jnp.ones((D,), jnp.float32), 'ln_b': jnp.zeros((D,), jnp.float32)}
    _L1_attn_in = _L1_attn_setup()

    def _L1_ffn_setup():
        import jax, jax.numpy as jnp
        import numpy as np
        from jax import lax
        D = 128
        E = 8
        F = 512
        TOP_K = 2
        key = jax.random.key(seed)
        ks = jax.random.split(key, 8)
        s = 0.02
        return {'x': jax.random.normal(ks[0], (4, 256, D), dtype=jnp.float32), 'gate_w': jax.random.normal(ks[1], (D, E), dtype=jnp.float32) * s, 'gate_b': jnp.zeros((E,), dtype=jnp.float32), 'w1': jax.random.normal(ks[2], (E, D, F), dtype=jnp.float32) * s, 'b1': jnp.zeros((E, F), dtype=jnp.float32), 'w2': jax.random.normal(ks[3], (E, F, D), dtype=jnp.float32) * s, 'b2': jnp.zeros((E, D), dtype=jnp.float32)}
    _L1_ffn_in = _L1_ffn_setup()
    _d = {'L0_attn_x': _L0_attn_in['x'], 'L0_attn_Wq': _L0_attn_in['Wq'], 'L0_attn_Wk': _L0_attn_in['Wk'], 'L0_attn_Wv': _L0_attn_in['Wv'], 'L0_attn_Wo': _L0_attn_in['Wo'], 'L0_ffn_centroids': _L0_ffn_in['centroids'], 'L0_ffn_ln_g': _L0_ffn_in['ln_g'], 'L0_ffn_ln_b': _L0_ffn_in['ln_b'], 'L0_ffn_W1': _L0_ffn_in['W1'], 'L0_ffn_b1': _L0_ffn_in['b1'], 'L0_ffn_W2': _L0_ffn_in['W2'], 'L0_ffn_b2': _L0_ffn_in['b2'], 'L1_attn_w_r': _L1_attn_in['w_r'], 'L1_attn_w_k': _L1_attn_in['w_k'], 'L1_attn_w_v': _L1_attn_in['w_v'], 'L1_attn_w_g': _L1_attn_in['w_g'], 'L1_attn_w_o': _L1_attn_in['w_o'], 'L1_attn_time_maa_k': _L1_attn_in['time_maa_k'], 'L1_attn_time_maa_v': _L1_attn_in['time_maa_v'], 'L1_attn_time_maa_r': _L1_attn_in['time_maa_r'], 'L1_attn_time_maa_g': _L1_attn_in['time_maa_g'], 'L1_attn_time_decay': _L1_attn_in['time_decay'], 'L1_attn_time_faaaa': _L1_attn_in['time_faaaa'], 'L1_attn_ln_g': _L1_attn_in['ln_g'], 'L1_attn_ln_b': _L1_attn_in['ln_b'], 'L1_ffn_gate_w': _L1_ffn_in['gate_w'], 'L1_ffn_gate_b': _L1_ffn_in['gate_b'], 'L1_ffn_w1': _L1_ffn_in['w1'], 'L1_ffn_b1': _L1_ffn_in['b1'], 'L1_ffn_w2': _L1_ffn_in['w2'], 'L1_ffn_b2': _L1_ffn_in['b2']}
    _x0 = _d['L0_attn_x']
    _d['L0_attn_x'] = jax.random.normal(jax.random.fold_in(jax.random.key(seed), 1), (32, 256, 128), dtype=_x0.dtype)
    del _x0
    return _d

def reference(L0_attn_x, L0_attn_Wq, L0_attn_Wk, L0_attn_Wv, L0_attn_Wo, L0_ffn_centroids, L0_ffn_ln_g, L0_ffn_ln_b, L0_ffn_W1, L0_ffn_b1, L0_ffn_W2, L0_ffn_b2, L1_attn_w_r, L1_attn_w_k, L1_attn_w_v, L1_attn_w_g, L1_attn_w_o, L1_attn_time_maa_k, L1_attn_time_maa_v, L1_attn_time_maa_r, L1_attn_time_maa_g, L1_attn_time_decay, L1_attn_time_faaaa, L1_attn_ln_g, L1_attn_ln_b, L1_ffn_gate_w, L1_ffn_gate_b, L1_ffn_w1, L1_ffn_b1, L1_ffn_w2, L1_ffn_b2):

    def _L0_attn_ref(x, Wq, Wk, Wv, Wo):
        import jax, jax.numpy as jnp
        import numpy as np
        NUM_HEADS = 16
        EPS = 1e-06

        def _phi(x):
            return jax.nn.elu(x) + 1.0
        B, L, D = x.shape
        H = NUM_HEADS
        dh = D // H
        Q = x @ Wq
        K = x @ Wk
        V = x @ Wv
        Qh = Q.reshape(B, L, H, dh).transpose(0, 2, 1, 3)
        Kh = K.reshape(B, L, H, dh).transpose(0, 2, 1, 3)
        Vh = V.reshape(B, L, H, dh).transpose(0, 2, 1, 3)
        Qf = _phi(Qh)
        Kf = _phi(Kh)
        Kv = jnp.einsum('bhlm,bhln->bhmn', Kf, Vh)
        K1 = jnp.sum(Kf, axis=2)
        num = jnp.einsum('bhlm,bhmn->bhln', Qf, Kv)
        den = jnp.einsum('bhlm,bhm->bhl', Qf, K1) + EPS
        out = num / den[..., None]
        out = out.transpose(0, 2, 1, 3).reshape(B, L, D)
        return out @ Wo

    def _L0_ffn_ref(input_features, centroids, ln_g, ln_b, W1, b1, W2, b2):
        import jax, jax.numpy as jnp
        import numpy as np
        E = 8
        D = 128
        F = 512
        S, B = (256, 2)
        LN_EPS = 1e-05

        def _moe_forward(input_features, centroids, ln_g, ln_b, W1, b1, W2, b2):
            s, b, d = input_features.shape
            x = jnp.swapaxes(input_features, 0, 1).reshape(-1, d)
            logits = x.astype(jnp.float32) @ centroids.astype(jnp.float32).T
            assign = jnp.argmax(logits, axis=-1)
            onehot = jax.nn.one_hot(assign, E, dtype=x.dtype)
            disp = jnp.einsum('te,td->etd', onehot, x)
            mu = disp.mean(-1, keepdims=True)
            var = disp.var(-1, keepdims=True)
            xn = (disp - mu) * jax.lax.rsqrt(var + LN_EPS)
            xn = xn * ln_g[:, None, :] + ln_b[:, None, :]
            h = jax.nn.relu(jnp.einsum('etd,edf->etf', xn, W1) + b1[:, None, :])
            y = jnp.einsum('etf,efd->etd', h, W2) + b2[:, None, :]
            y = disp + y
            out = jnp.einsum('te,etd->td', onehot, y)
            return jnp.swapaxes(out.reshape(b, s, d), 0, 1)
        return _moe_forward(input_features, centroids, ln_g, ln_b, W1, b1, W2, b2)

    def _L1_attn_ref(x, w_r, w_k, w_v, w_g, w_o, time_maa_k, time_maa_v, time_maa_r, time_maa_g, time_decay, time_faaaa, ln_g, ln_b):
        import jax, jax.numpy as jnp
        import numpy as np
        D = 128
        H = 16
        N = D // H
        B = 4
        T = 256
        NLAYERS = 12
        LAYER_ID = 6
        EPS = 1e-05 * 64

        def _forward(x, w_r, w_k, w_v, w_g, w_o, time_maa_k, time_maa_v, time_maa_r, time_maa_g, time_decay, time_faaaa, ln_g, ln_b):
            Bs, Ts, C = x.shape
            if Ts % 32 == 0:
                Q = 32
            elif Ts % 128 == 0:
                Q = 128
            else:
                Q = Ts
            nC = Ts // Q
            xs = jnp.pad(x, ((0, 0), (1, 0), (0, 0)))[:, :-1]
            xx = xs - x
            xk = x + xx * time_maa_k
            xv = x + xx * time_maa_v
            xr = x + xx * time_maa_r
            xg = x + xx * time_maa_g
            r = (xr @ w_r.T).reshape(Bs, Ts, H, N).transpose(0, 2, 1, 3)
            k = (xk @ w_k.T).reshape(Bs, Ts, H, N).transpose(0, 2, 3, 1)
            v = (xv @ w_v.T).reshape(Bs, Ts, H, N).transpose(0, 2, 1, 3)
            g = jax.nn.silu(xg @ w_g.T)
            w = jnp.exp(-jnp.exp(time_decay))
            u = time_faaaa
            ws = (w ** Q)[None, :, None, None]
            q = jnp.arange(Q)
            wk = (w[:, None] ** (Q - 1 - q)[None, :])[None, :, None, :]
            wb = (w[:, None] ** q[None, :])[None, :, :, None]
            ii = q[:, None]
            jj = q[None, :]
            e = jnp.maximum(ii - jj - 1, 0)
            Wmat = jnp.where((jj < ii)[None], w[:, None, None] ** e[None], 0.0)
            Wmat = Wmat + jnp.eye(Q, dtype=x.dtype)[None] * u[:, None, None]
            Wmat = Wmat[None]
            rC = r.reshape(Bs, H, nC, Q, N).transpose(2, 0, 1, 3, 4)
            kC = k.reshape(Bs, H, N, nC, Q).transpose(3, 0, 1, 2, 4)
            vC = v.reshape(Bs, H, nC, Q, N).transpose(2, 0, 1, 3, 4)

            def step(state, inp):
                rr, kk, vv = inp
                y = rr @ kk * Wmat @ vv + rr @ state * wb
                state = ws * state + kk * wk @ vv
                return (state, y)
            state0 = jnp.zeros((Bs, H, N, N), x.dtype)
            _, yC = jax.lax.scan(step, state0, (rC, kC, vC))
            y = yC.transpose(1, 2, 0, 3, 4).reshape(Bs, H, Ts, N)
            y = y.transpose(0, 2, 1, 3).reshape(Bs * Ts, H, N)
            mu = y.mean(-1, keepdims=True)
            var = y.var(-1, keepdims=True)
            y = (y - mu) / jnp.sqrt(var + EPS)
            y = y.reshape(Bs, Ts, C) * ln_g + ln_b
            y = y * g
            return y @ w_o.T
        return _forward(x, w_r, w_k, w_v, w_g, w_o, time_maa_k, time_maa_v, time_maa_r, time_maa_g, time_decay, time_faaaa, ln_g, ln_b)

    def _L1_ffn_ref(x, gate_w, gate_b, w1, b1, w2, b2):
        import jax, jax.numpy as jnp
        import numpy as np
        from jax import lax
        D = 128
        E = 8
        F = 512
        TOP_K = 2
        B, S, _ = x.shape
        flat = x.reshape(-1, D)
        T = flat.shape[0]
        logits = flat @ gate_w + gate_b
        topv, topi = lax.top_k(logits, TOP_K)
        topw = jax.nn.softmax(topv.astype(jnp.float32), axis=-1).astype(x.dtype)
        routing = jnp.zeros_like(logits).at[jnp.arange(T)[:, None], topi].set(topw)

        def body(acc, params):
            W1e, b1e, W2e, b2e, we = params
            h = jax.nn.gelu(flat @ W1e + b1e, approximate=False)
            out = h @ W2e + b2e
            return (acc + out * we[:, None], None)
        init = jnp.zeros_like(flat)
        final, _ = lax.scan(body, init, (w1, b1, w2, b2, routing.T))
        return final.reshape(B, S, D)
    x = L0_attn_x
    xn = _layernorm(x, axis=-1)
    s = _L0_attn_ref(xn, L0_attn_Wq, L0_attn_Wk, L0_attn_Wv, L0_attn_Wo)
    g = _silu(_L0_ffn_ref(xn, L0_ffn_centroids, L0_ffn_ln_g, L0_ffn_ln_b, L0_ffn_W1, L0_ffn_b1, L0_ffn_W2, L0_ffn_b2))
    x = x + s * g
    xn = _layernorm(x, axis=-1)
    s = _L1_attn_ref(xn, L1_attn_w_r, L1_attn_w_k, L1_attn_w_v, L1_attn_w_g, L1_attn_w_o, L1_attn_time_maa_k, L1_attn_time_maa_v, L1_attn_time_maa_r, L1_attn_time_maa_g, L1_attn_time_decay, L1_attn_time_faaaa, L1_attn_ln_g, L1_attn_ln_b)
    g = _silu(_L1_ffn_ref(xn, L1_ffn_gate_w, L1_ffn_gate_b, L1_ffn_w1, L1_ffn_b1, L1_ffn_w2, L1_ffn_b2))
    x = x + s * g
    return x

_drawn_inputs = setup_inputs


def setup_inputs(seed=0):
    import zlib

    import numpy as np

    out = dict(_drawn_inputs(seed))
    spreads = {'L0_ffn_ln_g': (1.0, 0.6),
     'L0_ffn_ln_b': (0.0, 0.8),
     'L1_attn_ln_g': (1.0, 0.6),
     'L1_attn_ln_b': (0.0, 0.8),
     'L1_ffn_gate_b': (0.0, 0.8),
     'L1_ffn_b1': (0.0, 0.8),
     'L1_ffn_b2': (0.0, 0.8)}
    factors = {'L0_attn_Wq': 8.0,
     'L0_attn_Wk': 8.0,
     'L0_attn_Wv': 8.0,
     'L0_attn_Wo': 8.0,
     'L0_ffn_centroids': 8.0,
     'L0_ffn_W1': 8.0,
     'L0_ffn_b1': 8.0,
     'L0_ffn_W2': 8.0,
     'L0_ffn_b2': 37.044,
     'L1_attn_w_r': 8.0,
     'L1_attn_w_k': 8.0,
     'L1_attn_w_v': 8.0,
     'L1_attn_w_g': 8.0,
     'L1_attn_w_o': 8.0,
     'L1_attn_time_maa_k': 8.0,
     'L1_attn_time_maa_v': 8.0,
     'L1_attn_time_maa_r': 8.0,
     'L1_attn_time_maa_g': 8.0,
     'L1_attn_time_decay': 64.0,
     'L1_attn_time_faaaa': 8.0,
     'L1_ffn_gate_w': 8.0,
     'L1_ffn_w1': 8.0,
     'L1_ffn_w2': 8.0}
    for name, (base, spread) in spreads.items():
        noise = np.random.default_rng([zlib.crc32(name.encode()), seed]).standard_normal(out[name].shape)
        drawn = base * np.exp(spread * noise) if base else spread * noise
        out[name] = jnp.asarray(drawn.astype(out[name].dtype))
    for name, factor in factors.items():
        out[name] = (out[name] * factor).astype(out[name].dtype)
    return out
```

```python
from collections import namedtuple
from contextlib import ExitStack

import concourse.bass as bass
from concourse import mybir

ALU = mybir.AluOpType
ACT = mybir.ActivationFunctionType
F32 = mybir.dt.float32
I32 = mybir.dt.int32
U32 = mybir.dt.uint32
AX = mybir.AxisListType

P = 128
B, L, D = 32, 256, 128
TOK = B * L
NT = TOK // P
GT = 4
G = NT // GT
GW = GT * P
E, F = 8, 512
FC = F // P
HEADS, HN = 16, 8
SLOT = 256
HALVES = SLOT // P
CHOICES = (1, 2)
TILES = tuple((TOK * c // SLOT + E - 1 + 1) // 2 * 2 for c in CHOICES)
MAXT = max(TILES)
THR = TOK // SLOT
LN_EPS = 1e-5
DEN_EPS = 1e-6
GN_EPS = 1e-5 * 64
HUGE = 3.0e38
ENGINES = 5
PARAMS = 16 * 24
CREDIT = 2

WORDS = 11012
C_B1 = (0, E * FC)
C_LNG = 2 * E * FC
C_LNB = C_LNG + E
C_CENT = C_LNB + E
C_MAA = C_CENT + E
C_GNG = C_MAA + 4
C_GNB = C_GNG + 1


class Steps:

    def __init__(self, sem, per=0):
        self.sem, self.per, self.base, self.n = sem, per, 0, 0

    def at(self, i):
        assert self.n in (0, self.per), (self.n, self.per)
        self.base, self.n = i * self.per, 0

    def one(self):
        self.n += 1
        return 1

    def all(self):
        return self.base + self.n


def program(nc, a, out):
    with ExitStack() as ctx:
        def sb(name, shape, dt=F32):
            return ctx.enter_context(nc.sbuf_tensor(name, shape, dt))

        def sem(name):
            return ctx.enter_context(nc.semaphore(name))

        X = sb("X", [P, NT, D])
        XN = sb("XN", [P, NT, D])
        S = sb("S", [P, NT, D])
        XN2 = sb("XN2", [P, NT, D])
        KV = [XN2[:, par * NT // 2:(par + 1) * NT // 2, :].rearrange("p a b -> p (a b)") for par in range(2)]
        TOEP = sb("TOEP", [P, HEADS, 2 * P])
        COLS = sb("COLS", [P, P])
        IDENT = sb("IDENT", [P, P])
        UPPER = sb("UPPER", [P, P])
        ONES = sb("ONES", [P, P])
        BLOCK = sb("BLOCK", [P, P])
        ZERO4 = sb("ZERO4", [P, 1])
        EPSC = sb("EPSC", [P, 3])
        IE8 = sb("IE8", [P, E])
        ITHR = sb("ITHR", [P, THR])
        ITILE = sb("ITILE", [P, MAXT])
        TD = sb("TD", [P, HEADS])
        TU = sb("TU", [P, HEADS])
        LW = sb("LW", [P, HEADS])
        GB = sb("GB", [P, E])
        GWT = sb("GWT", [P, E])
        WA = sb("WA", [P, 4, D])
        WT = sb("WT", [P, 5, D])
        B2 = sb("B2", [P, E, D])
        MX = sb("MX", [P, 2, NT])
        IDX = sb("IDX", [P, NT])
        CNT = sb("CNT", [P, 4, E])
        TE = sb("TE", [P, MAXT], I32)
        TEF = sb("TEF", [P, MAXT])
        POSF = sb("POSF", [P, NT])
        POS = sb("POS", [P, 2, NT], U32)
        WTS = sb("WTS", [P, 3, NT])
        ARENA = sb("ARENA", [P, WORDS])

        def carve():
            at = [0]

            def take(*shape):
                n = 1
                for s in shape:
                    n *= s
                v = ARENA[:, at[0]:at[0] + n]
                at[0] += n
                assert at[0] <= WORDS, at[0]
                if len(shape) == 2:
                    v = v.rearrange("p (a b) -> p a b", a=shape[0])
                if len(shape) == 3:
                    v = v.rearrange("p (a b c) -> p a b c", a=shape[0], b=shape[1])
                return v
            return take

        PS = ctx.enter_context(nc.psum_tensor("PS", [P, 8, 512], F32))
        disp = nc.dram_tensor("disp", (MAXT * SLOT, D), F32, kind="Internal").ap()
        ybuf = nc.dram_tensor("ybuf", (MAXT * SLOT, D), F32, kind="Internal").ap()

        x_dram = a["L0_attn_x"].rearrange("b (h p) d -> p (b h) d", p=P)
        out_dram = out.rearrange("b (h p) d -> p (b h) d", p=P)

        phase_done = sem("phase_done")
        passed = sem("passed")
        params_in = sem("params_in")
        b2_in = sem("b2_in")
        rows_zeroed = sem("rows_zeroed")
        consts_made = sem("consts_made")
        pool_steps = sem("pool_steps")
        set_ready = sem("set_ready")
        cols_turned = sem("cols_turned")
        cols_kept = sem("cols_kept")
        zero_filled = sem("zero_filled")
        s_zeroed = sem("s_zeroed")
        lw_made = sem("lw_made")
        exp_made = sem("exp_made")
        toep_made = sem("toep_made")
        toep_cut = sem("toep_cut")
        x_in = [sem(f"x_in{i}") for i in range(2)]
        out_done = [sem(f"out_done{i}") for i in range(2)]

        def some(layer, names):
            names = names.split()
            return namedtuple("Sems", names)(*(sem(f"{n}_{layer}") for n in names))

        LNS = [some(la, "ln_steps var_made sd_made xn_made xn_kept xn_turned xt_made logits_made lg_kept")
               for la in range(2)]
        RT = [some(la, "rt_steps onehot_made ranks_made w_exp") for la in range(2)]
        SC = [some(la, "staged sent0 sent1") for la in range(2)]
        FF = [some(la, "w1_in0 w1_in1 w2_in0 w2_in1 rows_in0 rows_in1 turned xf_made h_made "
                       "hid_made y_made b2_made par_made y_kept y_out0 y_out1") for la in range(2)]
        CB = [some(la, "pos_staged got0 got1 u_steps u_made silu_made post_steps x_made") for la in range(2)]
        AT = some("a0", "xs_in0 xs_in1 turned xt_made qkv_made ek_made eq_made v_made phi_steps phi_made "
                        "aug_made masked num_made dd_made out_steps out_made s_made s_kept")
        RW = some("a1", "xs_in0 xs_in1 turned xt_made mix_steps mixed kvr_made g_made k_kept v_kept r_kept "
                        "g_kept kv_made chunk_steps prod_made red_made gn_steps sq_in sq_made "
                        "sd_in sd_made yn_made yt_made ya_made yg_made s_made s_kept pad_zeroed")

        def pairs(eng, first, count, body):
            with eng.Fori(0, count // 2) as it:
                for u in range(2):
                    par = (first + u) % 2
                    body(it * 2 + (first + u), par, it + (first + u - par) // 2)

        def hold(eng, s, value):
            eng.wait_ge(s, value)
            eng.sem_inc(passed, 1)

        def barrier(eng, n):
            eng.drain().then_inc(phase_done, 1)
            eng.wait_ge(phase_done, ENGINES * n)

        def grp(arr, g):
            return arr[:, bass.ds(g * GT, GT), :]

        t1 = carve()
        XN_ST = [t1(GT, D) for _ in range(2)]
        XT_ST = [t1(GT, P) for _ in range(2)]
        ST = [t1(GT, 6) for _ in range(2)]
        ST2 = [t1(GT, 6) for _ in range(2)]
        SM = [t1(16, GT) for _ in range(2)]
        ROWS = t1(P)
        WNAT = t1(5, D)
        EXPO = t1(2 * P)
        LG = ARENA[:, WORDS - NT * E:WORDS].rearrange("p (t e) -> p t e", e=E)

        t2 = carve()
        RA, RB, RC, RD = [t2(NT, E) for _ in range(4)]
        RTH = t2(E, THR)
        RTT = t2(MAXT, E)
        RONE = t2(NT)
        OH = [t2(NT, E) for _ in range(2)]

        t3 = carve()
        A_XS = [t3(GT, D) for _ in range(2)]
        A_XT = [t3(GT, P) for _ in range(2)]
        A_E = t3(GT, P)
        A_E2 = t3(GT, P)
        A_KF = [t3(GT, D) for _ in range(2)]
        A_VA = [t3(GT, 2 * D) for _ in range(2)]
        A_QF = [t3(GW) for _ in range(2)]
        A_M = t3(2, 2 * D)
        A_DD = t3(GW)
        A_OT = [t3(GW) for _ in range(2)]

        t4 = carve()
        F_W1 = [t4(F) for _ in range(2)]
        F_W2 = [t4(FC, D) for _ in range(2)]
        F_D = [t4(HALVES, D) for _ in range(2)]
        F_X = [t4(SLOT) for _ in range(2)]
        F_H = [t4(FC, SLOT) for _ in range(2)]
        F_Y = [t4(HALVES, D) for _ in range(2)]
        F_PAR = [t4(FC + 2) for _ in range(2)]
        F_B2 = [t4(D) for _ in range(2)]

        t5 = carve()
        C_Y = [t5(2 * GT, D) for _ in range(2)]
        C_U = [t5(GT, D) for _ in range(2)]
        C_S = [t5(GT, D) for _ in range(2)]
        C_O = [t5(GT, D) for _ in range(2)]
        C_T = t5(GT, D)

        t6 = carve()
        R_XS = [t6(GT, D) for _ in range(2)]
        R_XT = [t6(2, L + 1) for _ in range(2)]
        R_XX = t6(GW)
        R_MIX = t6(4, GW)
        R_K, R_V = [t6(GW) for _ in range(2)]
        R_R = [t6(GW) for _ in range(2)]
        R_G = [t6(GW) for _ in range(2)]
        R_P = t6(1024)
        R_Y = t6(GW)
        R_YC = t6(GW)
        R_SQ = t6(GW)
        R_YN = t6(GT, D)
        R_SM = t6(4, 64)
        STAGE = [sb(f"STAGE{i}", [P, GT, D]) for i in range(2)]
        POS_ST = [sb(f"POS_ST{i}", [P, 2, GT], U32) for i in range(2)]

        def load_b2(sp, la):
            src = a[f"L{la}_ffn_b2"].rearrange("(o e) d -> o (e d)", o=1).to_broadcast([P, E * D])
            sp.dma_start(B2[:].rearrange("p e d -> p (e d)"), src).then_inc(b2_in, 16)

        def sp_attention_loads(sp, dst, sems, turned):
            def load(g, par, use):
                sp.wait_ge(turned, g + 1)
                sp.dma_start(dst[par], grp(XN, g)).then_inc(sems[par], 16)
            pairs(sp, 0, G, load)

        def sp_experts(sp, la):
            f = FF[la]
            w1 = a[f"L{la}_ffn_W1" if la == 0 else "L1_ffn_w1"]
            w2 = a[f"L{la}_ffn_W2" if la == 0 else "L1_ffn_w2"]

            def load(t, par, use):
                e = sp.value_load(TE[0:1, bass.ds(t, 1)], min_val=0, max_val=E - 1)
                sp.wait_ge(f.turned, t + 1)
                sp.dma_start(F_D[par], disp.rearrange("(t h p) d -> p (t h) d", h=HALVES, p=P)
                             [:, bass.ds(t * HALVES, HALVES), :]).then_inc((f.rows_in0, f.rows_in1)[par], 16)
                sp.wait_ge(f.h_made, t + 1)
                sp.dma_start(F_W1[par], w1.rearrange("e d f -> d e f")[:, bass.ds(e, 1), :]
                             .rearrange("p e f -> p (e f)")).then_inc((f.w1_in0, f.w1_in1)[par], 16)
                sp.wait_ge(f.y_made, t + 1)
                sp.dma_start(F_W2[par], w2.rearrange("e (c p) d -> p (e c) d", p=P)
                             [:, bass.ds(e * FC, FC), :]).then_inc((f.w2_in0, f.w2_in1)[par], 16)
            pairs(sp, 0, TILES[la], load)

        def pool_send(pool, la, src, extra):
            c, s = CHOICES[la], SC[la]
            sent = (s.sent0, s.sent1)

            def send(g, par, use, first=False):
                if extra:
                    extra(g, par, first)
                if not first:
                    hold(pool, sent[par], use * 16 * GT * c)
                pool.tensor_copy(STAGE[par][:], grp(src, g)).then_inc(s.staged, 1)
                pool.tensor_copy(POS_ST[par][:, 0:c, :], POS[:, 0:c, bass.ds(g * GT, GT)]).then_inc(s.staged, 1)
                hold(pool, s.staged, 2 * g + 2)
                for j in range(GT):
                    for i in range(c):
                        pool.indirect_dma_start(
                            out=disp, out_offset=bass.IndirectOffsetOnAxis(ap=POS_ST[par][:, i, j:j + 1], axis=0),
                            in_=STAGE[par][:, j, :], in_offset=None).then_inc(sent[par], 16)
            send(0, 0, 0, True)
            send(1, 1, 0, True)
            pairs(pool, 2, G - 2, send)
            for par in range(2):
                pool.wait_ge(sent[par], G // 2 * 16 * GT * c)

        def pool_store_y(pool, la):
            f = FF[la]

            def store(t, par, use):
                hold(pool, f.y_kept, t + CREDIT + 1)
                pool.dma_start(ybuf.rearrange("(t h p) d -> p (t h) d", h=HALVES, p=P)
                               [:, bass.ds(t * HALVES, HALVES), :], F_Y[par]).then_inc((f.y_out0, f.y_out1)[par], 16)
            pairs(pool, 0, TILES[la], store)
            for s in (f.y_out0, f.y_out1):
                pool.wait_ge(s, 16 * TILES[la] // 2)

        def pool_fetch_y(pool, la):
            c, b = CHOICES[la], CB[la]
            got = (b.got0, b.got1)

            def fetch(g, par, use, first=False):
                if not first:
                    hold(pool, got[par], use * 16 * GT * c)
                    hold(pool, b.u_made, g - 1)
                pool.tensor_copy(POS_ST[par][:, 0:c, :], POS[:, 0:c, bass.ds(g * GT, GT)]).then_inc(b.pos_staged, 1)
                hold(pool, b.pos_staged, g + 1)
                for i in range(c):
                    for j in range(GT):
                        pool.indirect_dma_start(
                            out=C_Y[par][:, i * GT + j, :], out_offset=None, in_=ybuf[0:TILES[la] * SLOT, :],
                            in_offset=bass.IndirectOffsetOnAxis(ap=POS_ST[par][:, i, j:j + 1], axis=0)
                        ).then_inc(got[par], 16)
            fetch(0, 0, 0, True)
            fetch(1, 1, 0, True)
            pairs(pool, 2, G - 2, fetch)

        def pe_norm(pe, la):
            s = LNS[la]
            router = COLS[:, C_CENT:C_CENT + E] if la == 0 else GWT[:]
            pe.sem_inc(s.xn_turned, CREDIT)
            pe.sem_inc(s.logits_made, CREDIT)

            def body(g, par, use):
                pe.wait_ge(s.xn_made, g + 1)
                pe.wait_ge(s.xt_made, g + 1)
                for j in range(GT):
                    last = pe.transpose(PS[:, par, j * P:(j + 1) * P], XN_ST[par][:, j, :], IDENT[:])
                last.then_inc(s.xn_turned, 1)
                pe.wait_ge(s.xt_made, g + CREDIT + 1)
                pe.wait_ge(s.lg_kept, g + 1)
                for j in range(GT):
                    last = pe.matmul(PS[:, 2 + par, j * E:(j + 1) * E], XT_ST[par][:, j, :], router,
                                     start=True, stop=True)
                last.then_inc(s.logits_made, 1)
            pairs(pe, 0, G, body)

        def pe_ranks(pe, la):
            r = RT[la]
            pe.wait_ge(r.onehot_made, 1)
            oh = RA.rearrange("p t e -> p (t e)")
            pe.matmul(PS[:, 4, :], UPPER[:], oh, start=True, stop=True)
            pe.matmul(PS[:, 5, :], ONES[:], oh, start=True, stop=True).then_inc(r.ranks_made, 1)

        def pe_linear_attention(pe):
            xs_in = (AT.xs_in0, AT.xs_in1)
            pe.sem_inc(AT.turned, CREDIT)
            pe.sem_inc(AT.s_made, CREDIT)

            def turn(g, par, use):
                pe.wait_ge(xs_in[par], 16 * (use + 1))
                pe.wait_ge(AT.xt_made, g)
                for j in range(GT):
                    last = pe.transpose(PS[:, 0, j * P:(j + 1) * P], A_XS[par][:, j, :], IDENT[:])
                last.then_inc(AT.turned, 1)

            def project(g, par):
                pe.wait_ge(AT.xt_made, g + 1)
                pe.wait_ge(AT.phi_made, g)
                pe.wait_ge(AT.v_made, g)
                for j in range(GT):
                    pe.matmul(PS[:, 2 + j // 2, (j % 2) * 2 * D:(j % 2 + 1) * 2 * D], A_XT[par][:, j, :],
                              WA[:, 1:3, :].rearrange("p a d -> p (a d)"), start=True, stop=True)
                pe.matmul(PS[:, 1, :], WA[:, 0, :], A_XT[par].rearrange("p a b -> p (a b)"),
                          start=True, stop=True).then_inc(AT.qkv_made, 1)

            def sums(g, par):
                pe.wait_ge(AT.phi_made, g + 1)
                pe.wait_ge(AT.v_made, g + 1)
                pe.wait_ge(AT.masked, g)
                for s in range(2):
                    for h in range(2):
                        last = pe.matmul(PS[:, 4, s * 2 * D:(s + 1) * 2 * D], A_KF[par][:, 2 * s + h, :],
                                         A_VA[par][:, 2 * s + h, :], start=(h == 0), stop=(h == 1))
                last.then_inc(AT.aug_made, 1)

            def apply(g, par):
                pe.wait_ge(AT.masked, g + 1)
                pe.wait_ge(AT.out_made, g)
                for i in range(2):
                    for s in range(2):
                        last = pe.matmul(PS[:, 5 + i, s * L:(s + 1) * L], A_M[:, s, i * D:(i + 1) * D],
                                         A_QF[par][:, s * L:(s + 1) * L], start=True, stop=True)
                last.then_inc(AT.num_made, 1)

            def final(g, par):
                pe.wait_ge(AT.out_made, g + 1)
                pe.wait_ge(AT.s_kept, g)
                for j in range(GT):
                    last = pe.matmul(PS[:, 7, j * D:(j + 1) * D], A_OT[par][:, j * P:(j + 1) * P], WA[:, 3, :],
                                     start=True, stop=True)
                last.then_inc(AT.s_made, 1)

            def body(g, par, use, first=False, final_group=False):
                if not final_group:
                    turn(g + 1, 1 - par, use + par)
                sums(g, par)
                if not final_group:
                    project(g + 1, 1 - par)
                apply(g, par)
                if not first:
                    final(g - 1, 1 - par)
            turn(0, 0, 0)
            project(0, 0)
            body(0, 0, 0, first=True)
            pairs(pe, 1, G - 2, body)
            body(G - 1, (G - 1) % 2, (G - 1) // 2, final_group=True)
            final(G - 1, (G - 1) % 2)

        def pe_experts(pe, la):
            f, n = FF[la], TILES[la]
            pe.sem_inc(f.turned, CREDIT)
            pe.sem_inc(f.h_made, CREDIT)
            pe.sem_inc(f.y_made, CREDIT)

            def turn(t, par, use):
                pe.wait_ge((f.rows_in0, f.rows_in1)[par], 16 * (use + 1))
                pe.wait_ge(f.xf_made, t + 1)
                for h in range(HALVES):
                    last = pe.transpose(PS[:, par, h * P:(h + 1) * P], F_D[par][:, h, :], IDENT[:])
                last.then_inc(f.turned, 1)

            def hidden(t, par, use):
                pe.wait_ge((f.w1_in0, f.w1_in1)[par], 16 * (use + 1))
                pe.wait_ge(f.xf_made, t + CREDIT + 1)
                pe.wait_ge(f.hid_made, t + 1)
                for c in range(FC):
                    last = pe.matmul(PS[:, 2 + 2 * par + c // 2, (c % 2) * SLOT:(c % 2 + 1) * SLOT],
                                     F_W1[par][:, c * P:(c + 1) * P], F_X[par], start=True, stop=True)
                last.then_inc(f.h_made, 1)

            def result(t, par, use):
                pe.wait_ge((f.w2_in0, f.w2_in1)[par], 16 * (use + 1))
                pe.wait_ge(f.hid_made, t + CREDIT + 1)
                pe.wait_ge(f.y_kept, t + 1)
                for h in range(HALVES):
                    for c in range(FC):
                        last = pe.matmul(PS[:, 6 + par, h * D:(h + 1) * D], F_H[par][:, c, h * P:(h + 1) * P],
                                         F_W2[par][:, c, :], start=(c == 0), stop=(c == FC - 1))
                last.then_inc(f.y_made, 1)

            turn(0, 0, 0)
            turn(1, 1, 0)
            hidden(0, 0, 0)

            def body(t, par, use):
                turn(t + 1, 1 - par, use + par)
                hidden(t, par, use)
                result(t - 1, 1 - par, use + par - 1)
            pairs(pe, 1, n - 2, body)
            hidden(n - 1, 1, n // 2 - 1)
            result(n - 2, 0, n // 2 - 1)
            result(n - 1, 1, n // 2 - 1)

        def pe_recurrence(pe):
            xs_in = (RW.xs_in0, RW.xs_in1)
            pe.sem_inc(RW.turned, CREDIT)

            def turn(g, par, use):
                pe.wait_ge(xs_in[par], 16 * (use + 1))
                pe.wait_ge(RW.g_kept, g)
                for j in range(GT):
                    last = pe.transpose(PS[:, 0, j * P:(j + 1) * P], R_XS[par][:, j, :], IDENT[:])
                last.then_inc(RW.turned, 1)

            def project(g):
                pe.wait_ge(RW.mixed, g + 1)
                for i in range(3):
                    for j in range(GT):
                        last = pe.matmul(PS[:, 1 + i, j * D:(j + 1) * D], R_MIX[:, i, j * P:(j + 1) * P],
                                         WT[:, i, :], start=True, stop=True)
                last.then_inc(RW.kvr_made, 1)
                pe.matmul(PS[:, 0, :], WT[:, 3, :], R_MIX[:, 3, :], start=True, stop=True).then_inc(RW.g_made, 1)

            def chunk(g, par, c):
                if c == 0:
                    pe.wait_ge(RW.kv_made, g + 1)
                pe.wait_ge(RW.prod_made, 4 * g + c + 1)
                for h in range(4):
                    kv = KV[par].rearrange("p (h t q) -> p h t q", t=GT, q=64)[:, 4 * c + h, :, :]
                    ps = PS[:, 4 + 2 * (c % 2) + h // 2, (h % 2) * 256:(h % 2 + 1) * 256]
                    pv = ps.rearrange("p (t q) -> p t q", q=64)
                    pe.matmul(pv, TOEP[:, 4 * c + h, 0:P], kv, start=True, stop=False)
                    last = pe.matmul(pv[:, 1::2, :], TOEP[:, 4 * c + h, P:2 * P], kv[:, 0::2, :],
                                     start=False, stop=True)
                last.then_inc(RW.chunk_steps, 1)

            def turn_back(g):
                pe.wait_ge(RW.yn_made, g + 1)
                for j in range(GT):
                    last = pe.transpose(PS[:, 1, j * P:(j + 1) * P], R_YN[:, j, :], IDENT[:])
                last.then_inc(RW.yt_made, 1)

            def final(g):
                pe.wait_ge(RW.yg_made, g + 1)
                for j in range(GT):
                    last = pe.matmul(PS[:, 2, j * D:(j + 1) * D], R_SQ[:, j * P:(j + 1) * P], WT[:, 4, :],
                                     start=True, stop=True)
                last.then_inc(RW.s_made, 1)

            def body(g, par, use, first=False, final_group=False):
                if not final_group:
                    turn(g + 1, 1 - par, use + par)
                if not first:
                    turn_back(g - 1)
                chunk(g, par, 0)
                if not first:
                    final(g - 1)
                chunk(g, par, 1)
                if not final_group:
                    if not first:
                        pe.wait_ge(RW.s_kept, g)
                    project(g + 1)
                chunk(g, par, 2)
                chunk(g, par, 3)
            turn(0, 0, 0)
            project(0)
            body(0, 0, 0, first=True)
            pairs(pe, 1, G - 2, body)
            body(G - 1, (G - 1) % 2, (G - 1) // 2, final_group=True)
            turn_back(G - 1)
            final(G - 1)

        def act_norm(act, la):
            s = LNS[la]
            norms = 2 if la == 0 else 1
            act.sem_inc(s.xn_kept, CREDIT)
            act.sem_inc(s.xt_made, CREDIT)

            def body(g, par, use):
                for i in range(norms):
                    act.wait_ge(s.var_made, norms * g + i + 1)
                    nc.scalar.activation(SM[par][:, 8 * i + 6, :], SM[par][:, 8 * i + 5, :], ACT.Sqrt
                                         ).then_inc(s.sd_made, 1)
                    if i == 0:
                        hold(act, s.xn_made, g + 1)
                        nc.scalar.activation(grp(XN, g), XN_ST[par], ACT.Copy).then_inc(s.xn_kept, 1)
                act.wait_ge(s.xn_turned, g + CREDIT + 1)
                act.wait_ge(s.logits_made, g + 1)
                nc.scalar.activation(XT_ST[par].rearrange("p a b -> p (a b)"), PS[:, par, :], ACT.Copy
                                     ).then_inc(s.xt_made, 1)
            pairs(act, 0, G, body)

        def act_linear_attention(act):
            def keep_turned(g, par):
                act.wait_ge(AT.turned, g + CREDIT + 1)
                nc.scalar.activation(A_XT[par].rearrange("p a b -> p (a b)"), PS[:, 0, :], ACT.Copy
                                     ).then_inc(AT.xt_made, 1)

            def exps(g, par):
                act.wait_ge(AT.qkv_made, g + 1)
                kv = PS[:, 2:4, :].rearrange("p b (j c d) -> p (b j) c d", c=2, d=D)
                nc.scalar.activation(A_E, kv[:, :, 0, :], ACT.Exp).then_inc(AT.ek_made, 1)
                nc.scalar.activation(A_VA[par][:, :, 0:D], kv[:, :, 1, :], ACT.Copy).then_inc(AT.v_made, 1)
                nc.scalar.activation(A_E2.rearrange("p a b -> p (a b)"), PS[:, 1, :], ACT.Exp
                                     ).then_inc(AT.eq_made, 1)

            def dens(g):
                act.wait_ge(AT.num_made, g + 1)
                act.wait_ge(AT.out_made, g)
                nc.scalar.activation(A_DD, PS[:, 6, :], ACT.Identity, bias=EPSC[:, 1:2]).then_inc(AT.dd_made, 1)

            def keep_s(g):
                hold(act, AT.s_made, g + CREDIT + 1)
                nc.scalar.activation(grp(S, g), PS[:, 7, :].rearrange("p (a d) -> p a d", d=D), ACT.Copy
                                     ).then_inc(AT.s_kept, 1)

            def body(g, par, use, first=False, final_group=False):
                if not final_group:
                    keep_turned(g + 1, 1 - par)
                    exps(g + 1, 1 - par)
                dens(g)
                if not first:
                    keep_s(g - 1)
            keep_turned(0, 0)
            exps(0, 0)
            body(0, 0, 0, first=True)
            pairs(act, 1, G - 2, body)
            body(G - 1, (G - 1) % 2, (G - 1) // 2, final_group=True)
            keep_s(G - 1)

        def act_experts(act, la, func):
            f = FF[la]
            act.sem_inc(f.hid_made, CREDIT)

            def body(t, par, use):
                act.wait_ge(f.h_made, t + CREDIT + 1)
                act.wait_ge(f.par_made, t + 1)
                act.wait_ge(f.y_made, t + 1)
                for c in range(FC):
                    last = nc.scalar.activation(
                        F_H[par][:, c, :], PS[:, 2 + 2 * par + c // 2, (c % 2) * SLOT:(c % 2 + 1) * SLOT],
                        func, bias=F_PAR[par][:, c:c + 1])
                last.then_inc(f.hid_made, 1)
            pairs(act, 0, TILES[la], body)

        def act_combine(act, la):
            b = CB[la]

            def body(g, par, use):
                act.wait_ge(b.u_made, g + 1)
                act.wait_ge(b.x_made, g + 1)
                nc.scalar.activation(C_S[par], C_U[par], ACT.Silu).then_inc(b.silu_made, 1)
            pairs(act, 0, G, body)

        def act_recurrence(act):
            def keep_turned(g, par):
                act.wait_ge(RW.turned, g + CREDIT + 1)
                nc.scalar.activation(R_XT[par][:, :, 1:L + 1], PS[:, 0, :].rearrange("p (s t) -> p s t", s=2),
                                     ACT.Copy).then_inc(RW.xt_made, 1)

            def keep_kvr(g, par):
                act.wait_ge(RW.kvr_made, g + 1)
                act.wait_ge(RW.kv_made, g)
                for ps, dst, s in ((1, R_K, RW.k_kept), (2, R_V, RW.v_kept), (3, R_R[par], RW.r_kept)):
                    nc.scalar.activation(dst.rearrange("p (h t n) -> p t h n", t=GT, n=HN),
                                         PS[:, ps, :].rearrange("p (t h n) -> p t h n", t=GT, n=HN),
                                         ACT.Copy).then_inc(s, 1)
                act.wait_ge(RW.g_made, g + 1)
                nc.scalar.activation(R_G[par], PS[:, 0, :], ACT.Silu).then_inc(RW.g_kept, 1)

            def squares(g):
                act.wait_ge(RW.sq_in, g + 1)
                nc.scalar.activation(R_SQ, R_YC, ACT.Square).then_inc(RW.sq_made, 1)
                act.wait_ge(RW.sd_in, g + 1)
                nc.scalar.activation(R_SM[:, 2, :], R_SM[:, 1, :], ACT.Sqrt, scale=1.0 / HN,
                                     bias=EPSC[:, 2:3]).then_inc(RW.sd_made, 1)

            def affine(g):
                act.wait_ge(RW.yt_made, g + 1)
                nc.scalar.activation(R_XX2, PS[:, 1, :], ACT.Identity, scale=COLS[:, C_GNG:C_GNG + 1],
                                     bias=COLS[:, C_GNB:C_GNB + 1]).then_inc(RW.ya_made, 1)

            def keep_s(g):
                hold(act, RW.s_made, g + 1)
                nc.scalar.activation(grp(S, g), PS[:, 2, :].rearrange("p (a d) -> p a d", d=D), ACT.Copy
                                     ).then_inc(RW.s_kept, 1)

            def body(g, par, use, first=False, final_group=False):
                if not final_group:
                    keep_turned(g + 1, 1 - par)
                if not first:
                    affine(g - 1)
                    keep_s(g - 1)
                if not final_group:
                    keep_kvr(g + 1, 1 - par)
                squares(g)
            keep_turned(0, 0)
            keep_kvr(0, 0)
            body(0, 0, 0, first=True)
            pairs(act, 1, G - 2, body)
            body(G - 1, (G - 1) % 2, (G - 1) // 2, final_group=True)
            affine(G - 1)
            keep_s(G - 1)

        R_XX2 = R_YC

        def dve_norm(v, la):
            s = LNS[la]
            k = Steps(s.ln_steps, 17 if la == 0 else 8)
            v.sem_inc(s.lg_kept, CREDIT)

            def moments(src, st, sm, i):
                for j in range(GT):
                    last = v.bn_stats(st[:, j, :], src(j))
                last.then_inc(s.ln_steps, k.one())
                v.wait_ge(s.ln_steps, k.all())
                v.tensor_tensor(sm[:, 0, :], st[:, :, 1], st[:, :, 4], ALU.add).then_inc(s.ln_steps, k.one())
                v.tensor_tensor(sm[:, 1, :], st[:, :, 1], st[:, :, 4], ALU.subtract).then_inc(s.ln_steps, k.one())
                v.tensor_tensor(sm[:, 2, :], st[:, :, 2], st[:, :, 5], ALU.add).then_inc(s.ln_steps, k.one())
                v.wait_ge(s.ln_steps, k.all())
                v.scalar_tensor_tensor(out=sm[:, 3, :], in0=sm[:, 1, :], scalar=D / 4.0, in1=sm[:, 1, :],
                                       op0=ALU.mult, op1=ALU.mult).then_inc(s.ln_steps, k.one())
                v.tensor_scalar(sm[:, 0, :], sm[:, 0, :], 0.5, None, ALU.mult).then_inc(s.ln_steps, k.one())
                v.wait_ge(s.ln_steps, k.all())
                v.tensor_tensor(sm[:, 4, :], sm[:, 2, :], sm[:, 3, :], ALU.add).then_inc(s.ln_steps, k.one())
                v.wait_ge(s.ln_steps, k.all())
                v.tensor_scalar(sm[:, 5, :], sm[:, 4, :], 1.0 / D, LN_EPS, ALU.mult, ALU.add
                                ).then_inc(s.var_made, 1)

            def norm(g, par, use):
                k.at(g)
                if la == 0:
                    v.wait_ge(x_in[par], 16 * (use + 1))
                v.wait_ge(s.xn_kept, g + 1)
                v.wait_ge(s.xn_turned, g + 1)
                norms = 2 if la == 0 else 1
                moments(lambda j: X[:, bass.ds(g * GT + j, 1), :].rearrange("p a d -> p (a d)"), ST[par], SM[par], 0)
                v.wait_ge(s.sd_made, norms * g + 1)
                v.reciprocal(SM[par][:, 7, :], SM[par][:, 6, :]).then_inc(s.ln_steps, k.one())
                hold(v, s.ln_steps, k.all())
                for j in range(GT):
                    last = v.tensor_scalar(XN_ST[par][:, j, :],
                                           X[:, bass.ds(g * GT + j, 1), :].rearrange("p a d -> p (a d)"),
                                           SM[par][:, 0, j:j + 1], SM[par][:, 7, j:j + 1],
                                           ALU.subtract, ALU.mult)
                last.then_inc(s.xn_made, 1)
                if la == 0:
                    sm = SM[par][:, 8:16, :]
                    v.wait_ge(s.xn_made, g + 1)
                    moments(lambda j: XN_ST[par][:, j, :], ST2[par], sm, 1)
                    v.wait_ge(s.sd_made, 2 * g + 2)
                    v.reciprocal(sm[:, 7, :], sm[:, 6, :]).then_inc(s.ln_steps, k.one())
                    hold(v, s.ln_steps, k.all())
                    for j in range(GT):
                        last = v.tensor_scalar(XN2[:, bass.ds(g * GT + j, 1), :].rearrange("p a d -> p (a d)"),
                                               XN_ST[par][:, j, :], sm[:, 0, j:j + 1], sm[:, 7, j:j + 1],
                                               ALU.subtract, ALU.mult)
                    last.then_inc(s.ln_steps, k.one())

            def logits(g, par):
                hold(v, s.logits_made, g + CREDIT + 1)
                ps = PS[:, 2 + par, 0:GT * E].rearrange("p (t e) -> p t e", e=E)
                if la == 0:
                    v.tensor_copy(grp(LG, g), ps).then_inc(s.lg_kept, 1)
                else:
                    v.tensor_tensor(grp(LG, g), ps, GB[:].unsqueeze(1).to_broadcast([P, GT, E]), ALU.add
                                    ).then_inc(s.lg_kept, 1)

            def body(g, par, use):
                norm(g, par, use)
                logits(g - 1, 1 - par)
            norm(0, 0, 0)
            pairs(v, 1, G - 2, body)
            body(G - 1, (G - 1) % 2, (G - 1) // 2)
            logits(G - 1, (G - 1) % 2)

        def dve_route(v, la):
            c, r = CHOICES[la], RT[la]
            k = Steps(r.rt_steps)

            def step(ins):
                ins.then_inc(r.rt_steps, k.one())
                v.wait_ge(r.rt_steps, k.all())

            ie = IE8[:].unsqueeze(1).to_broadcast([P, NT, E])
            wide = lambda ap: ap.unsqueeze(2).to_broadcast([P, NT, E])
            for i in range(c):
                step(v.tensor_reduce(MX[:, i, :], LG, AX.X, ALU.max))
                step(v.tensor_tensor(RA, LG, wide(MX[:, i, :]), ALU.is_equal))
                step(v.scalar_tensor_tensor(out=RB, in0=RA, scalar=float(-E), in1=ie, op0=ALU.mult, op1=ALU.add))
                step(v.tensor_reduce(IDX[:], RB, AX.X, ALU.min))
                step(v.tensor_scalar(IDX[:], IDX[:], float(E), None, ALU.add))
                step(v.tensor_tensor(OH[i], ie, wide(IDX[:]), ALU.is_equal))
                if i + 1 < c:
                    step(v.scalar_tensor_tensor(out=LG, in0=OH[i], scalar=-HUGE, in1=LG,
                                                op0=ALU.mult, op1=ALU.add))
            if c == 1:
                v.tensor_copy(RA, OH[0]).then_inc(r.onehot_made, 1)
            else:
                v.tensor_tensor(RA, OH[0], OH[1], ALU.add).then_inc(r.onehot_made, 1)
                v.tensor_tensor(WTS[:, 2, :], MX[:, 1, :], MX[:, 0, :], ALU.subtract).then_inc(r.w_exp, 1)
                v.wait_ge(r.w_exp, 2)
                step(v.tensor_scalar(WTS[:, 0, :], WTS[:, 2, :], 1.0, None, ALU.add))
                step(v.reciprocal(WTS[:, 0, :], WTS[:, 0, :]))
                step(v.tensor_tensor(WTS[:, 1, :], WTS[:, 2, :], WTS[:, 0, :], ALU.mult))
            v.wait_ge(r.ranks_made, 1)
            step(v.memset(RONE, 1.0))
            step(v.tensor_copy(RB.rearrange("p t e -> p (t e)"), PS[:, 5, :]))
            for e in range(E):
                last = v.tensor_tensor_scan(RC[:, :, e], RONE, RB[:, :, e], 0.0, ALU.mult, ALU.add)
            step(last)
            step(v.tensor_copy(CNT[:, 0, :], RC[:, NT - 1, :]))
            step(v.tensor_tensor(RTH, CNT[:, 0, :].unsqueeze(2).to_broadcast([P, E, THR]),
                                 ITHR[:].unsqueeze(1).to_broadcast([P, E, THR]), ALU.is_gt))
            step(v.tensor_reduce(CNT[:, 1, :], RTH, AX.X, ALU.add))
            step(v.tensor_tensor_scan(CNT[:, 2, :], RONE[:, 0:E], CNT[:, 1, :], 0.0, ALU.mult, ALU.add))
            step(v.tensor_tensor(CNT[:, 3, :], CNT[:, 2, :], CNT[:, 1, :], ALU.subtract))
            step(v.tensor_scalar(CNT[:, 3, :], CNT[:, 3, :], float(SLOT), None, ALU.mult))
            step(v.tensor_tensor(RTT, ITILE[:].unsqueeze(2).to_broadcast([P, MAXT, E]),
                                 CNT[:, 2, :].unsqueeze(1).to_broadcast([P, MAXT, E]), ALU.is_ge))
            step(v.tensor_reduce(TEF[:], RTT, AX.X, ALU.add))
            step(v.tensor_scalar(TEF[:], TEF[:], float(E - 1), None, ALU.min))
            step(v.tensor_copy(TE[:], TEF[:]))
            step(v.tensor_tensor(RC, RC, RB, ALU.subtract))
            step(v.tensor_tensor(RC, PS[:, 4, :].rearrange("p (t e) -> p t e", e=E), RC, ALU.add))
            step(v.tensor_tensor(RC, RC, CNT[:, 3, :].unsqueeze(1).to_broadcast([P, NT, E]), ALU.add))
            for i in range(c):
                step(v.tensor_tensor(RD, RC, OH[i], ALU.mult))
                step(v.tensor_reduce(POSF[:], RD, AX.X, ALU.add))
                step(v.tensor_copy(POS[:, i, :], POSF[:]))

        def dve_linear_attention(v):
            kp, ko = Steps(AT.phi_steps, 2), Steps(AT.out_steps, 1)
            for par in range(2):
                v.memset(A_VA[par][:, :, D:2 * D], 1.0)

            def phi(g, par):
                kp.at(g)
                kv = PS[:, 2:4, :].rearrange("p b (j c d) -> p (b j) c d", c=2, d=D)
                v.wait_ge(AT.ek_made, g + 1)
                v.tensor_scalar(A_E, A_E, 1.0, None, ALU.min).then_inc(AT.phi_steps, kp.one())
                v.wait_ge(AT.eq_made, g + 1)
                v.tensor_scalar(A_E2, A_E2, 1.0, None, ALU.min).then_inc(AT.phi_steps, kp.one())
                v.wait_ge(AT.phi_steps, kp.all() - 1)
                v.scalar_tensor_tensor(out=A_KF[par], in0=kv[:, :, 0, :], scalar=0.0, in1=A_E,
                                       op0=ALU.max, op1=ALU.add)
                v.wait_ge(AT.phi_steps, kp.all())
                v.scalar_tensor_tensor(out=A_QF[par], in0=PS[:, 1, :], scalar=0.0,
                                       in1=A_E2.rearrange("p a b -> p (a b)"), op0=ALU.max, op1=ALU.add
                                       ).then_inc(AT.phi_made, 1)

            def mask(g):
                v.wait_ge(AT.aug_made, g + 1)
                v.wait_ge(AT.num_made, g)
                v.tensor_tensor(A_M.rearrange("p s (i d) -> p (s i) d", d=D),
                                PS[:, 4, :].rearrange("p (a d) -> p a d", d=D),
                                BLOCK[:].unsqueeze(1).to_broadcast([P, GT, D]), ALU.mult).then_inc(AT.masked, 1)

            def divide(g, par):
                ko.at(g)
                v.wait_ge(AT.dd_made, g + 1)
                v.reciprocal(A_DD, A_DD).then_inc(AT.out_steps, ko.one())
                v.wait_ge(AT.out_steps, ko.all())
                v.wait_ge(AT.s_made, g + 1)
                v.tensor_tensor(A_OT[par], PS[:, 5, :], A_DD, ALU.mult).then_inc(AT.out_made, 1)

            def body(g, par, use, first=False, final_group=False):
                mask(g)
                if not final_group:
                    phi(g + 1, 1 - par)
                divide(g, par)
            phi(0, 0)
            body(0, 0, 0, first=True)
            pairs(v, 1, G - 2, body)
            body(G - 1, (G - 1) % 2, (G - 1) // 2, final_group=True)

        def dve_experts(v, la):
            f, n = FF[la], TILES[la]
            v.wait_ge(b2_in, 16 * (la + 1))
            v.sem_inc(f.xf_made, CREDIT)
            v.sem_inc(f.y_kept, CREDIT)

            def inputs(t, par):
                e = v.value_load(TE[0:1, bass.ds(t, 1)], min_val=0, max_val=E - 1)
                hold(v, f.hid_made, t + 1)
                if la == 0:
                    v.tensor_copy(F_PAR[par][:, FC:FC + 1], COLS[:, bass.ds(e + C_LNG, 1)])
                    v.tensor_copy(F_PAR[par][:, FC + 1:FC + 2], COLS[:, bass.ds(e + C_LNB, 1)])
                v.tensor_copy(F_PAR[par][:, 0:FC], COLS[:, bass.ds(e * FC + C_B1[la], FC)]
                              ).then_inc(f.par_made, 1)
                v.wait_ge(f.turned, t + CREDIT + 1)
                v.wait_ge(f.h_made, t + 1)
                v.wait_ge(f.par_made, t + 1)
                ps = PS[:, par, 0:SLOT]
                if la == 0:
                    v.tensor_scalar(F_X[par], ps, F_PAR[par][:, FC:FC + 1], F_PAR[par][:, FC + 1:FC + 2],
                                    ALU.mult, ALU.add).then_inc(f.xf_made, 1)
                else:
                    v.tensor_copy(F_X[par], ps).then_inc(f.xf_made, 1)
                return e

            def out_bias(e, t, par):
                hold(v, f.y_kept, t + 1)
                v.tensor_copy(F_B2[par], B2[:, bass.ds(e, 1), :].rearrange("p e d -> p (e d)")
                              ).then_inc(f.b2_made, 1)

            def result(t, par, use, first=False):
                v.wait_ge(f.y_made, t + CREDIT + 1)
                v.wait_ge(f.b2_made, t + 1)
                if not first:
                    v.wait_ge((f.y_out0, f.y_out1)[par], 16 * use)
                ps = PS[:, 6 + par, 0:SLOT].rearrange("p (h d) -> p h d", d=D)
                v.tensor_tensor(F_Y[par], ps, F_B2[par].unsqueeze(1).to_broadcast([P, HALVES, D]), ALU.add
                                ).then_inc(f.y_kept, 1)

            def body(t, par, use, first=False):
                e = inputs(t + 1, 1 - par)
                result(t - 1, 1 - par, use + par - 1, first)
                out_bias(e, t + 1, 1 - par)
            for t in range(2):
                out_bias(inputs(t, t), t, t)
            body(1, 1, 0, first=True)
            body(2, 0, 1, first=True)
            pairs(v, 3, n - 4, body)
            result(n - 2, 0, n // 2 - 1)
            result(n - 1, 1, n // 2 - 1)

        def dve_combine(v, la):
            b, c = CB[la], CHOICES[la]
            ku = Steps(b.u_steps, 2 if la else 0)
            kp = Steps(b.post_steps, 1)
            v.sem_inc(b.x_made, CREDIT)
            dst = lambda g, par: grp(X, g) if la == 0 else C_O[par]

            def total(g, par, use):
                ku.at(g)
                v.wait_ge((b.got0, b.got1)[par], 16 * GT * c * (use + 1))
                if not (isinstance(g, int) and g < 2):
                    hold(v, b.silu_made, g - 1)
                if la == 0:
                    v.tensor_tensor(C_U[par], C_Y[par][:, 0:GT, :], grp(XN, g), ALU.add).then_inc(b.u_made, 1)
                else:
                    w = lambda i: WTS[:, i, bass.ds(g * GT, GT)].unsqueeze(2).to_broadcast([P, GT, D])
                    v.tensor_tensor(C_U[par], C_Y[par][:, 0:GT, :], w(0), ALU.mult
                                    ).then_inc(b.u_steps, ku.one())
                    v.tensor_tensor(C_Y[par][:, GT:2 * GT, :], C_Y[par][:, GT:2 * GT, :], w(1), ALU.mult
                                    ).then_inc(b.u_steps, ku.one())
                    v.wait_ge(b.u_steps, ku.all())
                    v.tensor_tensor(C_U[par], C_U[par], C_Y[par][:, GT:2 * GT, :], ALU.add).then_inc(b.u_made, 1)

            def post(g, par, use):
                kp.at(g)
                hold(v, b.silu_made, g + 1)
                v.tensor_tensor(C_T, C_S[par], grp(S, g), ALU.mult).then_inc(b.post_steps, kp.one())
                if la == 1 and not (isinstance(g, int) and g < 2):
                    v.wait_ge(out_done[par], 16 * use)
                hold(v, b.post_steps, kp.all())
                v.tensor_tensor(dst(g, par), C_T, grp(X, g), ALU.add).then_inc(b.x_made, 1)
                v.wait_ge(b.x_made, CREDIT + g + 1)
                v.sem_inc(passed, 1)

            def body(g, par, use):
                total(g, par, use)
                post(g - 1, 1 - par, use + par - 1)
            total(0, 0, 0)
            total(1, 1, 0)
            post(0, 0, 0)
            body(2, 0, 1)
            pairs(v, 3, G - 4, body)
            body(G - 1, (G - 1) % 2, (G - 1) // 2)
            post(G - 1, (G - 1) % 2, (G - 1) // 2)

        def dve_recurrence(v):
            km = Steps(RW.mix_steps, 1)
            kc = Steps(RW.gn_steps, 2)
            for par in range(2):
                last = v.memset(R_XT[par][:, :, 0:1], 0.0)
            last.then_inc(RW.pad_zeroed, 1)
            v.wait_ge(RW.pad_zeroed, 1)
            v.sem_inc(RW.prod_made, CREDIT)

            def mixes(g, par):
                km.at(g)
                v.wait_ge(RW.xt_made, g + 1)
                v.wait_ge(RW.g_made, g)
                now, before = R_XT[par][:, :, 1:L + 1], R_XT[par][:, :, 0:L]
                xx = R_XX.rearrange("p (s t) -> p s t", s=2)
                v.tensor_tensor(xx, before, now, ALU.subtract).then_inc(RW.mix_steps, km.one())
                v.wait_ge(RW.mix_steps, km.all())
                for i in range(4):
                    last = v.scalar_tensor_tensor(out=R_MIX[:, i, :].rearrange("p (s t) -> p s t", s=2), in0=xx,
                                                  scalar=COLS[:, C_MAA + i:C_MAA + i + 1], in1=now,
                                                  op0=ALU.mult, op1=ALU.add)
                last.then_inc(RW.mixed, 1)

            def chunk(g, par, c):
                v.wait_ge(RW.chunk_steps, 4 * g + c + 1)
                if c == 0:
                    v.wait_ge(RW.r_kept, g + 1)
                prod = R_P.rearrange("p (a n m) -> p a n m", n=HN, m=HN)
                ps = PS[:, 4 + 2 * (c % 2):6 + 2 * (c % 2), :].rearrange("p b (a n m) -> p (b a) n m", n=HN, m=HN)
                r = R_R[par][:, c * P:(c + 1) * P].rearrange("p (a n) -> p a n", n=HN)
                v.tensor_tensor(prod, ps, r.unsqueeze(3).to_broadcast([P, HEADS, HN, HN]), ALU.mult
                                ).then_inc(RW.prod_made, 1)
                v.wait_ge(RW.prod_made, 4 * g + c + 1 + CREDIT)
                v.tensor_reduce(R_Y[:, c * P:(c + 1) * P].rearrange("p (a m) -> p a m", m=HN),
                                R_P.rearrange("p (a n m) -> p a m n", n=HN, m=HN), AX.X, ALU.add
                                ).then_inc(RW.red_made, 1)
                v.wait_ge(RW.red_made, 4 * g + c + 1)

            def group_norm(g):
                kc.at(g)
                y = R_Y.rearrange("p (a m) -> p a m", m=HN)
                yc = R_YC.rearrange("p (a m) -> p a m", m=HN)
                sq = R_SQ.rearrange("p (a m) -> p a m", m=HN)
                v.tensor_reduce(R_SM[:, 0, :], y, AX.X, ALU.add).then_inc(RW.gn_steps, kc.one())
                v.wait_ge(RW.gn_steps, kc.all())
                v.scalar_tensor_tensor(out=yc, in0=R_SM[:, 0, :].unsqueeze(2).to_broadcast([P, 64, HN]),
                                       scalar=-1.0 / HN, in1=y, op0=ALU.mult, op1=ALU.add).then_inc(RW.sq_in, 1)
                v.wait_ge(RW.sq_made, g + 1)
                v.tensor_reduce(R_SM[:, 1, :], sq, AX.X, ALU.add).then_inc(RW.sd_in, 1)
                v.wait_ge(RW.sd_made, g + 1)
                v.reciprocal(R_SM[:, 3, :], R_SM[:, 2, :]).then_inc(RW.gn_steps, kc.one())
                v.wait_ge(RW.gn_steps, kc.all())
                v.tensor_tensor(R_YN.rearrange("p t (h m) -> p h t m", m=HN),
                                R_YC.rearrange("p (h t m) -> p h t m", t=GT, m=HN),
                                R_SM[:, 3, :].rearrange("p (h t) -> p h t", t=GT).unsqueeze(3)
                                .to_broadcast([P, HEADS, GT, HN]), ALU.mult).then_inc(RW.yn_made, 1)

            def gate(g, par):
                v.wait_ge(RW.ya_made, g + 1)
                v.wait_ge(RW.g_kept, g + 1)
                v.tensor_tensor(R_SQ, R_YC, R_G[par], ALU.mult).then_inc(RW.yg_made, 1)

            def body(g, par, use, first=False, final_group=False):
                if not first:
                    gate(g - 1, 1 - par)
                chunk(g, par, 0)
                if not final_group:
                    mixes(g + 1, 1 - par)
                for c in range(1, 4):
                    chunk(g, par, c)
                if not first:
                    v.wait_ge(RW.s_made, g)
                group_norm(g)
            mixes(0, 0)
            body(0, 0, 0, first=True)
            pairs(v, 1, G - 2, body)
            body(G - 1, (G - 1) % 2, (G - 1) // 2, final_group=True)
            gate(G - 1, (G - 1) % 2)

        block = ctx.enter_context(nc.Block())

        @block.sync
        def _(sp):
            sp.dma_start(WA[:, 0, :], a["L0_attn_Wq"]).then_inc(params_in, 16)
            sp.dma_start(WA[:, 1, :], a["L0_attn_Wk"]).then_inc(params_in, 16)
            sp.dma_start(WA[:, 2, :], a["L0_attn_Wv"]).then_inc(params_in, 16)
            sp.dma_start(WA[:, 3, :], a["L0_attn_Wo"]).then_inc(params_in, 16)
            for i, n in enumerate(("w_k", "w_v", "w_r", "w_g", "w_o")):
                sp.dma_start(WNAT[:, i, :], a["L1_attn_" + n]).then_inc(params_in, 16)
            sp.dma_start(GWT[:], a["L1_ffn_gate_w"]).then_inc(params_in, 16)
            row = lambda n: a[n].rearrange("(o d) -> o d", o=1)
            sp.dma_start(GB[:], row("L1_ffn_gate_b").to_broadcast([P, E])).then_inc(params_in, 16)
            sp.dma_start(TD[:], row("L1_attn_time_decay").to_broadcast([P, HEADS])).then_inc(params_in, 16)
            sp.dma_start(TU[:], row("L1_attn_time_faaaa").to_broadcast([P, HEADS])).then_inc(params_in, 16)
            load_b2(sp, 0)
            sp.wait_ge(rows_zeroed, 1)
            for c, n, r in ((C_B1[0], "L0_ffn_b1", E * FC), (C_B1[1], "L1_ffn_b1", E * FC)):
                sp.dma_start(ROWS[c:c + r, :], a[n].rearrange("e (c f) -> (e c) f", f=P)).then_inc(params_in, 16)
            for c, n in ((C_LNG, "L0_ffn_ln_g"), (C_LNB, "L0_ffn_ln_b"), (C_CENT, "L0_ffn_centroids")):
                sp.dma_start(ROWS[c:c + E, :], a[n]).then_inc(params_in, 16)
            for c, n in ((C_MAA, "time_maa_k"), (C_MAA + 1, "time_maa_v"), (C_MAA + 2, "time_maa_r"),
                         (C_MAA + 3, "time_maa_g"), (C_GNG, "ln_g"), (C_GNB, "ln_b")):
                sp.dma_start(ROWS[c:c + 1, :], row("L1_attn_" + n)).then_inc(params_in, 16)

            def load_x(g, par, use):
                sp.wait_ge(x_in[par], 16 * use)
                sp.dma_start(grp(X, g), x_dram[:, bass.ds(g * GT, GT), :]).then_inc(x_in[par], 16)
            for g in range(2):
                sp.dma_start(grp(X, g), x_dram[:, g * GT:(g + 1) * GT, :]).then_inc(x_in[g], 16)
            pairs(sp, 2, G - 2, load_x)
            sp.wait_ge(s_zeroed, 1)
            fill = disp.rearrange("(c p r) d -> c p (r d)", p=P, r=16)
            for c in range(MAXT * SLOT // (P * 16)):
                sp.dma_start(fill[c], S[:, 0:16, :].rearrange("p a d -> p (a d)")).then_inc(zero_filled, 16)
            barrier(sp, 1)
            barrier(sp, 2)
            sp_attention_loads(sp, A_XS, (AT.xs_in0, AT.xs_in1), AT.turned)
            barrier(sp, 3)
            sp_experts(sp, 0)
            barrier(sp, 4)
            load_b2(sp, 1)
            barrier(sp, 5)
            barrier(sp, 6)
            barrier(sp, 7)
            sp_attention_loads(sp, R_XS, (RW.xs_in0, RW.xs_in1), RW.turned)
            barrier(sp, 8)
            sp_experts(sp, 1)
            barrier(sp, 9)

            def store(g, par, use):
                sp.wait_ge(CB[1].x_made, g + CREDIT + 1)
                sp.dma_start(out_dram[:, bass.ds(g * GT, GT), :], C_O[par]).then_inc(out_done[par], 16)
            pairs(sp, 0, G, store)
            for par in range(2):
                sp.wait_ge(out_done[par], 16 * G // 2)

        @block.gpsimd
        def _(pool):
            k = Steps(pool_steps)

            def made(ins):
                ins.then_inc(pool_steps, k.one())
                pool.wait_ge(pool_steps, k.all())

            made(pool.memset(ONES[:], 1.0))
            made(pool.affine_select(out=IDENT[:], in_=ONES[:], compare_op=ALU.is_equal, fill=0.0, base=0,
                                    pattern=[[1, P]], channel_multiplier=-1))
            made(pool.affine_select(out=UPPER[:], in_=ONES[:], compare_op=ALU.is_gt, fill=0.0, base=0,
                                    pattern=[[1, P]], channel_multiplier=-1))
            bv = BLOCK[:].rearrange("p (h n) -> p h n", n=HN)
            ov = ONES[:].rearrange("p (h n) -> p h n", n=HN)
            made(pool.affine_select(out=bv, in_=ov, compare_op=ALU.is_ge, fill=0.0, base=0,
                                    pattern=[[-HN, HEADS], [0, HN]], channel_multiplier=1))
            made(pool.affine_select(out=bv, in_=bv, compare_op=ALU.is_ge, fill=0.0, base=HN - 1,
                                    pattern=[[HN, HEADS], [0, HN]], channel_multiplier=-1))
            made(pool.iota(IE8[:], [[1, E]], base=-E, channel_multiplier=0, allow_small_or_imprecise_dtypes=True))
            made(pool.iota(ITHR[:], [[SLOT, THR]], base=0, channel_multiplier=0,
                           allow_small_or_imprecise_dtypes=True))
            made(pool.iota(ITILE[:], [[1, MAXT]], base=0, channel_multiplier=0,
                           allow_small_or_imprecise_dtypes=True))
            made(pool.iota(EXPO, [[1, 2 * P]], base=-1, channel_multiplier=-1,
                           allow_small_or_imprecise_dtypes=True))
            made(pool.affine_select(out=EXPO, in_=EXPO, compare_op=ALU.is_ge, fill=0.0, base=-1,
                                    pattern=[[1, 2 * P]], channel_multiplier=-1))
            for i, eps in enumerate((LN_EPS, DEN_EPS, GN_EPS)):
                made(pool.memset(EPSC[:, i:i + 1], eps))
            pool.memset(ZERO4[:], 0.0).then_inc(consts_made, 1)
            pool.wait_ge(exp_made, HEADS)
            for h in range(HEADS):
                d = TOEP[:, h, 0:P]
                pool.affine_select(out=d, in_=d, compare_op=ALU.is_ge, fill=0.0, base=-1,
                                   pattern=[[1, P]], channel_multiplier=-1).then_inc(toep_cut, 1)
            barrier(pool, 1)
            barrier(pool, 2)
            pool.wait_ge(zero_filled, 16 * (MAXT * SLOT // (P * 16)))
            pool_send(pool, 0, XN2, None)
            barrier(pool, 3)
            pool_store_y(pool, 0)
            barrier(pool, 4)
            pool_fetch_y(pool, 0)
            barrier(pool, 5)
            barrier(pool, 6)
            barrier(pool, 7)

            def kv_products(g, par, first):
                hold(pool, RW.v_kept, g + 1)
                if not first:
                    hold(pool, RW.chunk_steps, 4 * g - 4)
                pool.tensor_tensor(
                    KV[par].rearrange("p (a n m) -> p a n m", n=HN, m=HN),
                    R_K.rearrange("p (a n) -> p a n", n=HN).unsqueeze(3).to_broadcast([P, 64, HN, HN]),
                    R_V.rearrange("p (a m) -> p a m", m=HN).unsqueeze(2).to_broadcast([P, 64, HN, HN]),
                    ALU.mult).then_inc(RW.kv_made, 1)
            pool_send(pool, 1, XN, kv_products)
            barrier(pool, 8)
            pool_store_y(pool, 1)
            barrier(pool, 9)
            pool_fetch_y(pool, 1)

        @block.tensor
        def _(pe):
            pe.wait_ge(consts_made, 1)
            pe.wait_ge(params_in, PARAMS)
            pe.transpose(PS[:, 0, 0:P], ROWS, IDENT[:]).then_inc(cols_turned, 1)
            for i in range(5):
                pe.transpose(PS[:, 1 + i, 0:P], WNAT[:, i, :], IDENT[:]).then_inc(cols_turned, 1)
            pe.wait_ge(cols_kept, 6)
            pe_norm(pe, 0)
            barrier(pe, 1)
            pe_ranks(pe, 0)
            barrier(pe, 2)
            pe_linear_attention(pe)
            barrier(pe, 3)
            pe_experts(pe, 0)
            barrier(pe, 4)
            barrier(pe, 5)
            pe_norm(pe, 1)
            barrier(pe, 6)
            pe_ranks(pe, 1)
            barrier(pe, 7)
            pe_recurrence(pe)
            barrier(pe, 8)
            pe_experts(pe, 1)
            barrier(pe, 9)

        @block.scalar
        def _(act):
            act.wait_ge(cols_turned, 6)
            nc.scalar.activation(COLS[:], PS[:, 0, 0:P], ACT.Copy).then_inc(cols_kept, 1)
            for i in range(5):
                nc.scalar.activation(WT[:, i, :], PS[:, 1 + i, 0:P], ACT.Copy).then_inc(cols_kept, 1)
            act.wait_ge(params_in, PARAMS)
            nc.scalar.activation(LW[:], TD[:], ACT.Exp).then_inc(lw_made, 1)
            act.wait_ge(lw_made, 2)
            for h in range(HEADS):
                nc.scalar.activation(TOEP[:, h, :], EXPO, ACT.Exp, scale=LW[:, h:h + 1]).then_inc(exp_made, 1)
            act_norm(act, 0)
            barrier(act, 1)
            barrier(act, 2)
            act_linear_attention(act)
            barrier(act, 3)
            act_experts(act, 0, ACT.Relu)
            barrier(act, 4)
            act_combine(act, 0)
            barrier(act, 5)
            act_norm(act, 1)
            barrier(act, 6)
            act.wait_ge(RT[1].w_exp, 1)
            nc.scalar.activation(WTS[:, 2, :], WTS[:, 2, :], ACT.Exp).then_inc(RT[1].w_exp, 1)
            barrier(act, 7)
            act_recurrence(act)
            barrier(act, 8)
            act_experts(act, 1, ACT.Gelu)
            barrier(act, 9)
            act_combine(act, 1)

        @block.vector
        def _(v):
            v.memset(ROWS, 0.0).then_inc(rows_zeroed, 1)
            v.memset(S[:, 0:16, :], 0.0).then_inc(s_zeroed, 1)
            v.wait_ge(lw_made, 1)
            v.tensor_scalar(LW[:], LW[:], 1.0e4, -1.0, ALU.min, ALU.mult).then_inc(lw_made, 1)
            v.wait_ge(toep_cut, HEADS)
            for h in range(HEADS):
                v.scalar_tensor_tensor(out=TOEP[:, h, 0:P], in0=IDENT[:], scalar=TU[:, h:h + 1],
                                       in1=TOEP[:, h, 0:P], op0=ALU.mult, op1=ALU.add).then_inc(toep_made, 1)
            dve_norm(v, 0)
            barrier(v, 1)
            dve_route(v, 0)
            barrier(v, 2)
            dve_linear_attention(v)
            barrier(v, 3)
            dve_experts(v, 0)
            barrier(v, 4)
            dve_combine(v, 0)
            barrier(v, 5)
            dve_norm(v, 1)
            barrier(v, 6)
            dve_route(v, 1)
            barrier(v, 7)
            dve_recurrence(v)
            barrier(v, 8)
            dve_experts(v, 1)
            barrier(v, 9)
            dve_combine(v, 1)


_INS = ['L0_attn_x', 'L0_attn_Wq', 'L0_attn_Wk', 'L0_attn_Wv', 'L0_attn_Wo', 'L0_ffn_centroids', 'L0_ffn_ln_g',
        'L0_ffn_ln_b', 'L0_ffn_W1', 'L0_ffn_b1', 'L0_ffn_W2', 'L0_ffn_b2', 'L1_attn_w_r', 'L1_attn_w_k',
        'L1_attn_w_v', 'L1_attn_w_g', 'L1_attn_w_o', 'L1_attn_time_maa_k', 'L1_attn_time_maa_v',
        'L1_attn_time_maa_r', 'L1_attn_time_maa_g', 'L1_attn_time_decay', 'L1_attn_time_faaaa', 'L1_attn_ln_g',
        'L1_attn_ln_b', 'L1_ffn_gate_w', 'L1_ffn_gate_b', 'L1_ffn_w1', 'L1_ffn_b1', 'L1_ffn_w2', 'L1_ffn_b2']


def kernel(**inputs):
    import numpy as _np
    import concourse.bacc as _bacc
    from concourse import mybir as _mybir
    from concourse.bass_utils import run_bass_kernel_spmd as _run

    nc = _bacc.Bacc("TRN2", target_bir_lowering=False, num_devices=1)
    arrays, args = {}, {}
    for name in _INS:
        arr = _np.ascontiguousarray(inputs[name])
        arrays[f"in_{name}"] = arr
        args[name] = nc.dram_tensor(f"in_{name}", arr.shape, _mybir.dt.from_np(arr.dtype), kind="ExternalInput").ap()
    out = nc.dram_tensor("out_0", (B, L, D), _mybir.dt.float32, kind="ExternalOutput").ap()
    program(nc, args, out)
    r = _run(nc, [arrays], core_ids=[0])
    return r.results[0]["out_0"]
```

```python
from collections import namedtuple
from contextlib import ExitStack

import concourse.bass as bass
from concourse import mybir

ALU = mybir.AluOpType
ACT = mybir.ActivationFunctionType
F32 = mybir.dt.float32
I32 = mybir.dt.int32
U32 = mybir.dt.uint32
AX = mybir.AxisListType

P = 128
B, L, D = 32, 256, 128
TOK = B * L
NT = TOK // P
GT = 4
G = NT // GT
GW = GT * P
E, F = 8, 512
FC = F // P
HEADS, HN = 16, 8
SLOT = 256
HALVES = SLOT // P
CHOICES = (1, 2)
TILES = tuple((TOK * c // SLOT + E - 1 + 3) // 4 * 4 for c in CHOICES)
MAXT = max(TILES)
THR = TOK // SLOT
LN_EPS = 1e-5
DEN_EPS = 1e-6
GN_EPS = 1e-5 * 64
HUGE = 3.0e38
ENGINES = 5
WB = 4
PARAMS = 16 * 24
CREDIT = 2

WORDS = 11012
C_B1 = (0, E * FC)
C_LNG = 2 * E * FC
C_LNB = C_LNG + E
C_CENT = C_LNB + E
C_MAA = C_CENT + E
C_GNG = C_MAA + 4
C_GNB = C_GNG + 1


class Steps:

    def __init__(self, sem, per=0):
        self.sem, self.per, self.base, self.n = sem, per, 0, 0

    def at(self, i):
        assert self.n in (0, self.per), (self.n, self.per)
        self.base, self.n = i * self.per, 0

    def one(self):
        self.n += 1
        return 1

    def all(self):
        return self.base + self.n


def program(nc, a, out):
    with ExitStack() as ctx:
        def sb(name, shape, dt=F32):
            return ctx.enter_context(nc.sbuf_tensor(name, shape, dt))

        def sem(name):
            return ctx.enter_context(nc.semaphore(name))

        X = sb("X", [P, NT, D])
        XN = sb("XN", [P, NT, D])
        S = sb("S", [P, NT, D])
        XN2 = sb("XN2", [P, NT, D])
        KV = [XN2[:, par * NT // 2:(par + 1) * NT // 2, :].rearrange("p a b -> p (a b)") for par in range(2)]
        TOEP = sb("TOEP", [P, HEADS, 2 * P])
        COLS = sb("COLS", [P, P])
        IDENT = sb("IDENT", [P, P])
        UPPER = sb("UPPER", [P, P])
        ONES = sb("ONES", [P, P])
        BLOCK = sb("BLOCK", [P, P])
        ZERO4 = sb("ZERO4", [P, 1])
        EPSC = sb("EPSC", [P, 3])
        IE8 = sb("IE8", [P, E])
        ITHR = sb("ITHR", [P, THR])
        ITILE = sb("ITILE", [P, MAXT])
        TD = sb("TD", [P, HEADS])
        TU = sb("TU", [P, HEADS])
        LW = sb("LW", [P, HEADS])
        GB = sb("GB", [P, E])
        GWT = sb("GWT", [P, E])
        WA = sb("WA", [P, 4, D])
        WT = sb("WT", [P, 5, D])
        B2 = sb("B2", [P, E, D])
        MX = sb("MX", [P, 2, NT])
        IDX = sb("IDX", [P, NT])
        CNT = sb("CNT", [P, 4, E])
        TE = sb("TE", [P, MAXT], I32)
        TEF = sb("TEF", [P, MAXT])
        POSF = sb("POSF", [P, NT])
        POS = sb("POS", [P, 2, NT], U32)
        WTS = sb("WTS", [P, 3, NT])
        ARENA = sb("ARENA", [P, WORDS])

        def carve():
            at = [0]

            def take(*shape):
                n = 1
                for s in shape:
                    n *= s
                v = ARENA[:, at[0]:at[0] + n]
                at[0] += n
                assert at[0] <= WORDS, at[0]
                if len(shape) == 2:
                    v = v.rearrange("p (a b) -> p a b", a=shape[0])
                if len(shape) == 3:
                    v = v.rearrange("p (a b c) -> p a b c", a=shape[0], b=shape[1])
                return v
            return take

        PS = ctx.enter_context(nc.psum_tensor("PS", [P, 8, 512], F32))
        disp = nc.dram_tensor("disp", (MAXT * SLOT, D), F32, kind="Internal").ap()
        ybuf = nc.dram_tensor("ybuf", (MAXT * SLOT, D), F32, kind="Internal").ap()

        x_dram = a["L0_attn_x"].rearrange("b (h p) d -> p (b h) d", p=P)
        out_dram = out.rearrange("b (h p) d -> p (b h) d", p=P)

        phase_done = sem("phase_done")
        passed = sem("passed")
        params_in = sem("params_in")
        b2_in = sem("b2_in")
        rows_zeroed = sem("rows_zeroed")
        consts_made = sem("consts_made")
        pool_steps = sem("pool_steps")
        set_ready = sem("set_ready")
        cols_turned = sem("cols_turned")
        cols_kept = sem("cols_kept")
        zero_filled = sem("zero_filled")
        s_zeroed = sem("s_zeroed")
        lw_made = sem("lw_made")
        exp_made = sem("exp_made")
        toep_made = sem("toep_made")
        toep_cut = sem("toep_cut")
        x_in = [sem(f"x_in{i}") for i in range(2)]
        out_done = [sem(f"out_done{i}") for i in range(2)]

        def some(layer, names):
            names = names.split()
            return namedtuple("Sems", names)(*(sem(f"{n}_{layer}") for n in names))

        LNS = [some(la, "ln_steps var_made sd_made xn_made xn_kept xn_turned xt_made logits_made lg_kept")
               for la in range(2)]
        RT = [some(la, "rt_steps onehot_made ranks_made w_exp") for la in range(2)]
        SC = [some(la, "staged0 staged1 slots_staged sent0 sent1") for la in range(2)]
        FF = [some(la, "w_in0 w_in1 w_in2 w_in3 rows_in0 rows_in1 rows_in2 rows_in3 turned xf_made h_made "
                       "hid_made y_made b2_made par_made y_kept y_out0 y_out1") for la in range(2)]
        CB = [some(la, "pos_staged got0 got1 u_steps u_made silu_made post_steps x_made") for la in range(2)]
        AT = some("a0", "xs_in0 xs_in1 turned xt_made qkv_made ek_made eq_made v_made phi_steps phi_made "
                        "aug_made masked num_made dd_made out_steps out_made s_made s_kept")
        RW = some("a1", "xs_in0 xs_in1 turned xt_made mix_steps mixed kv_proj r_proj g_made k_kept v_kept r_kept "
                        "g_kept kv_made chunk_steps prod_made red_made gn_steps sq_in sq_made "
                        "sd_in sd_made yn_made yt_made ya_made yg_made s_made s_kept pad_zeroed")

        def rounds(eng, first, count, body, ways=2):
            with eng.Fori(0, count // ways) as it:
                for u in range(ways):
                    q = (first + u) % ways
                    body(it * ways + (first + u), q, it + (first + u) // ways)

        def hold(eng, s, value):
            eng.wait_ge(s, value)
            eng.sem_inc(passed, 1)

        def barrier(eng, n):
            eng.drain().then_inc(phase_done, 1)
            eng.wait_ge(phase_done, ENGINES * n)

        def grp(arr, g):
            return arr[:, bass.ds(g * GT, GT), :]

        t1 = carve()
        XN_ST = [t1(GT, D) for _ in range(2)]
        XT_ST = [t1(GT, P) for _ in range(2)]
        ST = [t1(GT, 6) for _ in range(2)]
        ST2 = [t1(GT, 6) for _ in range(2)]
        SM = [t1(16, GT) for _ in range(2)]
        ROWS = t1(P)
        WNAT = t1(5, D)
        EXPO = t1(2 * P)
        LG = ARENA[:, WORDS - NT * E:WORDS].rearrange("p (t e) -> p t e", e=E)

        t2 = carve()
        RA, RB, RC, RD = [t2(NT, E) for _ in range(4)]
        RTH = t2(E, THR)
        RTT = t2(MAXT, E)
        RONE = t2(NT)
        OH = [t2(NT, E) for _ in range(2)]

        t3 = carve()
        A_XS = [t3(GT, D) for _ in range(2)]
        A_XT = [t3(GT, P) for _ in range(2)]
        A_E = t3(GT, P)
        A_E2 = t3(GT, P)
        A_KF = [t3(GT, D) for _ in range(2)]
        A_VA = [t3(GT, 2 * D) for _ in range(2)]
        A_QF = [t3(GW) for _ in range(2)]
        A_M = t3(2, 2 * D)
        A_DD = t3(GW)
        A_OT = [t3(GW) for _ in range(2)]

        t4 = carve()
        F_W1 = [t4(F) for _ in range(WB)]
        F_W2 = [t4(FC, D) for _ in range(WB)]
        F_D = [t4(HALVES, D) for _ in range(WB)]
        F_X = [t4(SLOT) for _ in range(2)]
        F_H = [t4(FC, SLOT) for _ in range(2)]
        F_Y = [t4(HALVES, D) for _ in range(2)]
        F_PAR = [t4(FC + 2) for _ in range(2)]
        F_B2 = [t4(D) for _ in range(2)]

        t5 = carve()
        C_Y = [t5(2 * GT, D) for _ in range(2)]
        C_U = [t5(GT, D) for _ in range(2)]
        C_S = [t5(GT, D) for _ in range(2)]
        C_O = [t5(GT, D) for _ in range(2)]
        C_T = t5(GT, D)

        t6 = carve()
        R_XS = [t6(GT, D) for _ in range(2)]
        R_XT = [t6(2, L + 1) for _ in range(2)]
        R_MIX = t6(4, GW)
        R_K, R_V = [t6(GW) for _ in range(2)]
        R_R = [t6(GW) for _ in range(2)]
        R_G = [t6(GW) for _ in range(2)]
        R_P = t6(1024)
        R_Y = [t6(GW) for _ in range(2)]
        R_YC = t6(GW)
        R_SQ = t6(GW)
        R_YN = t6(GT, D)
        R_XX = R_YN.rearrange("p a b -> p (a b)")
        R_YA = R_YC
        R_YG = R_SQ
        R_SM = t6(4, 64)
        STAGE = [sb(f"STAGE{i}", [P, GT, D]) for i in range(2)]
        POS_ST = [sb(f"POS_ST{i}", [P, 2, GT], U32) for i in range(2)]

        def by_buffer(f):
            return (f.rows_in0, f.rows_in1, f.rows_in2, f.rows_in3), (f.w_in0, f.w_in1, f.w_in2, f.w_in3)

        def load_b2(sp, la):
            src = a[f"L{la}_ffn_b2"].rearrange("(o e) d -> o (e d)", o=1).to_broadcast([P, E * D])
            sp.dma_start(B2[:].rearrange("p e d -> p (e d)"), src).then_inc(b2_in, 16)

        def sp_attention_loads(sp, la, dst, sems, turned, src, ahead):
            sc = SC[la]
            n = 16 * GT * CHOICES[la]

            def load(i, par, use):
                hold(sp, turned, i + 1)
                sp.dma_start(dst[par], grp(XN, i)).then_inc(sems[par], 16)

            def stage(g, par, use, first=False):
                if not first:
                    hold(sp, (sc.sent0, sc.sent1)[par], n * use)
                sp.dma_start(STAGE[par][:], grp(src, g)).then_inc((sc.staged0, sc.staged1)[par], 16)

            def both(g, par, use):
                load(g + ahead, (par + ahead) % 2, use)
                stage(g, par, use)
            for i in range(ahead):
                load(i, i % 2, 0)
            for g in range(2):
                load(g + ahead, (g + ahead) % 2, 0)
                stage(g, g, 0, True)
            rounds(sp, 2, G - 2 - ahead, both)
            for g in range(G - ahead, G):
                stage(g, g % 2, g // 2)

        def sp_experts(sp, la):
            f = FF[la]
            rows_in, w_in = by_buffer(f)
            w1 = a[f"L{la}_ffn_W1" if la == 0 else "L1_ffn_w1"]
            w2 = a[f"L{la}_ffn_W2" if la == 0 else "L1_ffn_w2"]

            def load(t, q, use, first=False):
                e = sp.value_load(TE[0:1, bass.ds(t, 1)], min_val=0, max_val=E - 1)
                if not first:
                    sp.wait_ge(f.turned, t + CREDIT - WB + 1)
                sp.dma_start(F_D[q], disp.rearrange("(t h p) d -> p (t h) d", h=HALVES, p=P)
                             [:, bass.ds(t * HALVES, HALVES), :]).then_inc(rows_in[q], 16)
                if not first:
                    sp.wait_ge(f.h_made, t + CREDIT - WB + 1)
                sp.dma_start(F_W1[q], w1.rearrange("e d f -> d e f")[:, bass.ds(e, 1), :]
                             .rearrange("p e f -> p (e f)")).then_inc(w_in[q], 16)
                if not first:
                    sp.wait_ge(f.y_made, t + CREDIT - WB + 1)
                sp.dma_start(F_W2[q], w2.rearrange("e (c p) d -> p (e c) d", p=P)
                             [:, bass.ds(e * FC, FC), :]).then_inc(w_in[q], 16)
            for t in range(WB):
                load(t, t, 0, True)
            rounds(sp, WB, TILES[la] - WB, load, WB)

        def pool_send(pool, la, extra):
            c, s = CHOICES[la], SC[la]
            sent = (s.sent0, s.sent1)

            def send(g, par, use, first=False):
                if extra:
                    extra(g, par, first)
                if not first:
                    hold(pool, sent[par], use * 16 * GT * c)
                pool.tensor_copy(POS_ST[par][:, 0:c, :], POS[:, 0:c, bass.ds(g * GT, GT)]).then_inc(s.slots_staged, 1)
                hold(pool, s.slots_staged, g + 1)
                hold(pool, (s.staged0, s.staged1)[par], 16 * (use + 1))
                for j in range(GT):
                    for i in range(c):
                        pool.indirect_dma_start(
                            out=disp, out_offset=bass.IndirectOffsetOnAxis(ap=POS_ST[par][:, i, j:j + 1], axis=0),
                            in_=STAGE[par][:, j, :], in_offset=None).then_inc(sent[par], 16)
            send(0, 0, 0, True)
            send(1, 1, 0, True)
            rounds(pool, 2, G - 2, send)
            for par in range(2):
                pool.wait_ge(sent[par], G // 2 * 16 * GT * c)

        def pool_store_y(pool, la):
            f = FF[la]

            def store(t, par, use):
                hold(pool, f.y_kept, t + CREDIT + 1)
                pool.dma_start(ybuf.rearrange("(t h p) d -> p (t h) d", h=HALVES, p=P)
                               [:, bass.ds(t * HALVES, HALVES), :], F_Y[par]).then_inc((f.y_out0, f.y_out1)[par], 16)
            rounds(pool, 0, TILES[la], store)
            for s in (f.y_out0, f.y_out1):
                pool.wait_ge(s, 16 * TILES[la] // 2)

        def pool_fetch_y(pool, la):
            c, b = CHOICES[la], CB[la]
            got = (b.got0, b.got1)

            def fetch(g, par, use, first=False):
                if not first:
                    hold(pool, got[par], use * 16 * GT * c)
                    hold(pool, b.u_made, g - 1)
                pool.tensor_copy(POS_ST[par][:, 0:c, :], POS[:, 0:c, bass.ds(g * GT, GT)]).then_inc(b.pos_staged, 1)
                hold(pool, b.pos_staged, g + 1)
                for i in range(c):
                    for j in range(GT):
                        pool.indirect_dma_start(
                            out=C_Y[par][:, i * GT + j, :], out_offset=None, in_=ybuf[0:TILES[la] * SLOT, :],
                            in_offset=bass.IndirectOffsetOnAxis(ap=POS_ST[par][:, i, j:j + 1], axis=0)
                        ).then_inc(got[par], 16)
            fetch(0, 0, 0, True)
            fetch(1, 1, 0, True)
            rounds(pool, 2, G - 2, fetch)

        def pe_norm(pe, la):
            s = LNS[la]
            router = COLS[:, C_CENT:C_CENT + E] if la == 0 else GWT[:]
            pe.sem_inc(s.xn_turned, CREDIT)
            pe.sem_inc(s.logits_made, CREDIT)

            def body(g, par, use):
                pe.wait_ge(s.xn_made, g + 1)
                pe.wait_ge(s.xt_made, g + 1)
                for j in range(GT):
                    last = pe.transpose(PS[:, par, j * P:(j + 1) * P], XN_ST[par][:, j, :], IDENT[:])
                last.then_inc(s.xn_turned, 1)
                pe.wait_ge(s.xt_made, g + CREDIT + 1)
                pe.wait_ge(s.lg_kept, g + 1)
                for j in range(GT):
                    last = pe.matmul(PS[:, 2 + par, j * E:(j + 1) * E], XT_ST[par][:, j, :], router,
                                     start=True, stop=True)
                last.then_inc(s.logits_made, 1)
            rounds(pe, 0, G, body)

        def pe_ranks(pe, la):
            r = RT[la]
            pe.wait_ge(r.onehot_made, 1)
            oh = RA.rearrange("p t e -> p (t e)")
            pe.matmul(PS[:, 4, :], UPPER[:], oh, start=True, stop=True)
            pe.matmul(PS[:, 5, :], ONES[:], oh, start=True, stop=True).then_inc(r.ranks_made, 1)

        def pe_linear_attention(pe):
            xs_in = (AT.xs_in0, AT.xs_in1)
            pe.sem_inc(AT.turned, CREDIT)
            pe.sem_inc(AT.s_made, CREDIT)

            def turn(g, par, use):
                pe.wait_ge(xs_in[par], 16 * (use + 1))
                pe.wait_ge(AT.xt_made, g)
                for j in range(GT):
                    last = pe.transpose(PS[:, 0, j * P:(j + 1) * P], A_XS[par][:, j, :], IDENT[:])
                last.then_inc(AT.turned, 1)

            def project(g, par):
                pe.wait_ge(AT.xt_made, g + 1)
                pe.wait_ge(AT.phi_made, g)
                pe.wait_ge(AT.v_made, g)
                for j in range(GT):
                    pe.matmul(PS[:, 2 + j // 2, (j % 2) * 2 * D:(j % 2 + 1) * 2 * D], A_XT[par][:, j, :],
                              WA[:, 1:3, :].rearrange("p a d -> p (a d)"), start=True, stop=True)
                pe.matmul(PS[:, 1, :], WA[:, 0, :], A_XT[par].rearrange("p a b -> p (a b)"),
                          start=True, stop=True).then_inc(AT.qkv_made, 1)

            def sums(g, par):
                pe.wait_ge(AT.phi_made, g + 1)
                pe.wait_ge(AT.v_made, g + 1)
                pe.wait_ge(AT.masked, g)
                for s in range(2):
                    for h in range(2):
                        last = pe.matmul(PS[:, 4, s * 2 * D:(s + 1) * 2 * D], A_KF[par][:, 2 * s + h, :],
                                         A_VA[par][:, 2 * s + h, :], start=(h == 0), stop=(h == 1))
                last.then_inc(AT.aug_made, 1)

            def apply(g, par):
                pe.wait_ge(AT.masked, g + 1)
                pe.wait_ge(AT.out_made, g)
                for i in range(2):
                    for s in range(2):
                        last = pe.matmul(PS[:, 5 + i, s * L:(s + 1) * L], A_M[:, s, i * D:(i + 1) * D],
                                         A_QF[par][:, s * L:(s + 1) * L], start=True, stop=True)
                last.then_inc(AT.num_made, 1)

            def final(g, par):
                pe.wait_ge(AT.out_made, g + 1)
                pe.wait_ge(AT.s_kept, g)
                for j in range(GT):
                    last = pe.matmul(PS[:, 7, j * D:(j + 1) * D], A_OT[par][:, j * P:(j + 1) * P], WA[:, 3, :],
                                     start=True, stop=True)
                last.then_inc(AT.s_made, 1)

            def body(g, par, use, first=False, final_group=False):
                if not final_group:
                    turn(g + 1, 1 - par, use + par)
                sums(g, par)
                if not final_group:
                    project(g + 1, 1 - par)
                apply(g, par)
                if not first:
                    final(g - 1, 1 - par)
            turn(0, 0, 0)
            project(0, 0)
            body(0, 0, 0, first=True)
            rounds(pe, 1, G - 2, body)
            body(G - 1, (G - 1) % 2, (G - 1) // 2, final_group=True)
            final(G - 1, (G - 1) % 2)

        def pe_experts(pe, la):
            f, n = FF[la], TILES[la]
            pe.sem_inc(f.turned, CREDIT)
            pe.sem_inc(f.h_made, CREDIT)
            pe.sem_inc(f.y_made, CREDIT)

            rows_in, w_in = by_buffer(f)

            def turn(t, q, use):
                par = q % 2
                pe.wait_ge(rows_in[q], 16 * (use + 1))
                pe.wait_ge(f.xf_made, t + 1)
                for h in range(HALVES):
                    last = pe.transpose(PS[:, par, h * P:(h + 1) * P], F_D[q][:, h, :], IDENT[:])
                last.then_inc(f.turned, 1)

            def hidden(t, q, use):
                par = q % 2
                pe.wait_ge(w_in[q], 32 * (use + 1))
                pe.wait_ge(f.xf_made, t + CREDIT + 1)
                pe.wait_ge(f.hid_made, t + 1)
                for c in range(FC):
                    last = pe.matmul(PS[:, 2 + 2 * par + c // 2, (c % 2) * SLOT:(c % 2 + 1) * SLOT],
                                     F_W1[q][:, c * P:(c + 1) * P], F_X[par], start=True, stop=True)
                last.then_inc(f.h_made, 1)

            def result(t, q, use):
                par = q % 2
                pe.wait_ge(f.hid_made, t + CREDIT + 1)
                pe.wait_ge(f.y_kept, t + 1)
                for h in range(HALVES):
                    for c in range(FC):
                        last = pe.matmul(PS[:, 6 + par, h * D:(h + 1) * D], F_H[par][:, c, h * P:(h + 1) * P],
                                         F_W2[q][:, c, :], start=(c == 0), stop=(c == FC - 1))
                last.then_inc(f.y_made, 1)

            def body(t, q, use):
                turn(t + 1, (q + 1) % WB, use + (q + 1) // WB)
                hidden(t, q, use)
                result(t - 1, (q - 1) % WB, use + (q - 1) // WB)
            turn(0, 0, 0)
            turn(1, 1, 0)
            hidden(0, 0, 0)
            for t in (1, 2, 3):
                body(t, t, 0)
            rounds(pe, WB, n - 2 * WB, body, WB)
            for t in range(n - WB, n - 1):
                body(t, t % WB, t // WB)
            hidden(n - 1, WB - 1, n // WB - 1)
            result(n - 2, WB - 2, n // WB - 1)
            result(n - 1, WB - 1, n // WB - 1)

        def pe_recurrence(pe):
            xs_in = (RW.xs_in0, RW.xs_in1)
            pe.sem_inc(RW.turned, CREDIT)

            def turn(g, par, use):
                pe.wait_ge(xs_in[par], 16 * (use + 1))
                pe.wait_ge(RW.xt_made, g)
                if not (isinstance(g, int) and g < 2):
                    pe.wait_ge(RW.g_kept, g - 1)
                for j in range(GT):
                    last = pe.transpose(PS[:, 0, j * P:(j + 1) * P], R_XS[par][:, j, :], IDENT[:])
                last.then_inc(RW.turned, 1)

            def project_kvr(g, first=False):
                pe.wait_ge(RW.mixed, g + 1)
                pe.wait_ge(RW.r_kept, g)
                if not first:
                    pe.wait_ge(RW.ya_made, g - 2)
                    pe.wait_ge(RW.s_kept, g - 2)
                for i in range(3):
                    for j in range(GT):
                        last = pe.matmul(PS[:, 1 + i, j * D:(j + 1) * D], R_MIX[:, i, j * P:(j + 1) * P],
                                         WT[:, i, :], start=True, stop=True)
                    if i == 1:
                        last.then_inc(RW.kv_proj, 1)
                last.then_inc(RW.r_proj, 1)

            def project_g(g):
                pe.wait_ge(RW.xt_made, g + 2 if not isinstance(g, int) or g + 2 <= G else G)
                pe.matmul(PS[:, 0, :], WT[:, 3, :], R_MIX[:, 3, :], start=True, stop=True).then_inc(RW.g_made, 1)

            def chunk(g, par, c):
                if c == 0:
                    pe.wait_ge(RW.kv_made, g + 1)
                pe.wait_ge(RW.prod_made, 4 * g + c + 1)
                for h in range(4):
                    kv = KV[par].rearrange("p (h t q) -> p h t q", t=GT, q=64)[:, 4 * c + h, :, :]
                    ps = PS[:, 4 + 2 * (c % 2) + h // 2, (h % 2) * 256:(h % 2 + 1) * 256]
                    pv = ps.rearrange("p (t q) -> p t q", q=64)
                    pe.matmul(pv, TOEP[:, 4 * c + h, 0:P], kv, start=True, stop=False)
                    last = pe.matmul(pv[:, 1::2, :], TOEP[:, 4 * c + h, P:2 * P], kv[:, 0::2, :],
                                     start=False, stop=True)
                last.then_inc(RW.chunk_steps, 1)

            def turn_back(g):
                pe.wait_ge(RW.yn_made, g + 1)
                pe.wait_ge(RW.k_kept, g + 3 if not isinstance(g, int) or g + 3 <= G else G)
                for j in range(GT):
                    last = pe.transpose(PS[:, 1, j * P:(j + 1) * P], R_YN[:, j, :], IDENT[:])
                last.then_inc(RW.yt_made, 1)

            def final(g):
                pe.wait_ge(RW.yg_made, g + 1)
                for j in range(GT):
                    last = pe.matmul(PS[:, 2, j * D:(j + 1) * D], R_YG[:, j * P:(j + 1) * P], WT[:, 4, :],
                                     start=True, stop=True)
                last.then_inc(RW.s_made, 1)

            def body(g, par, use, has=(1, 1, 1, 1)):
                chunk(g, par, 0)
                if has[0]:
                    final(g - 2)
                chunk(g, par, 1)
                if has[2]:
                    project_kvr(g + 1, not has[0])
                chunk(g, par, 2)
                if has[3]:
                    turn(g + 2, par, use + 1)
                chunk(g, par, 3)
                if has[1]:
                    turn_back(g - 1)
                if has[2]:
                    project_g(g + 1)
            turn(0, 0, 0)
            turn(1, 1, 0)
            project_kvr(0, True)
            project_g(0)
            all_groups(pe, body)
            final(G - 2)
            turn_back(G - 1)
            final(G - 1)

        def all_groups(eng, body):
            body(0, 0, 0, (0, 0, 1, 1))
            body(1, 1, 0, (0, 1, 1, 1))
            rounds(eng, 2, G - 4, body)
            body(G - 2, (G - 2) % 2, (G - 2) // 2, (1, 1, 1, 0))
            body(G - 1, (G - 1) % 2, (G - 1) // 2, (1, 1, 0, 0))

        def act_norm(act, la):
            s = LNS[la]
            norms = 2 if la == 0 else 1
            act.sem_inc(s.xn_kept, CREDIT)
            act.sem_inc(s.xt_made, CREDIT)

            def body(g, par, use):
                for i in range(norms):
                    act.wait_ge(s.var_made, norms * g + i + 1)
                    nc.scalar.activation(SM[par][:, 8 * i + 6, :], SM[par][:, 8 * i + 5, :], ACT.Sqrt
                                         ).then_inc(s.sd_made, 1)
                    if i == 0:
                        hold(act, s.xn_made, g + 1)
                        nc.scalar.activation(grp(XN, g), XN_ST[par], ACT.Copy).then_inc(s.xn_kept, 1)
                act.wait_ge(s.xn_turned, g + CREDIT + 1)
                act.wait_ge(s.logits_made, g + 1)
                nc.scalar.activation(XT_ST[par].rearrange("p a b -> p (a b)"), PS[:, par, :], ACT.Copy
                                     ).then_inc(s.xt_made, 1)
            rounds(act, 0, G, body)

        def act_linear_attention(act):
            def keep_turned(g, par):
                act.wait_ge(AT.turned, g + CREDIT + 1)
                nc.scalar.activation(A_XT[par].rearrange("p a b -> p (a b)"), PS[:, 0, :], ACT.Copy
                                     ).then_inc(AT.xt_made, 1)

            def exps(g, par):
                act.wait_ge(AT.qkv_made, g + 1)
                kv = PS[:, 2:4, :].rearrange("p b (j c d) -> p (b j) c d", c=2, d=D)
                nc.scalar.activation(A_E, kv[:, :, 0, :], ACT.Exp).then_inc(AT.ek_made, 1)
                nc.scalar.activation(A_VA[par][:, :, 0:D], kv[:, :, 1, :], ACT.Copy).then_inc(AT.v_made, 1)
                nc.scalar.activation(A_E2.rearrange("p a b -> p (a b)"), PS[:, 1, :], ACT.Exp
                                     ).then_inc(AT.eq_made, 1)

            def dens(g):
                act.wait_ge(AT.num_made, g + 1)
                act.wait_ge(AT.out_made, g)
                nc.scalar.activation(A_DD, PS[:, 6, :], ACT.Identity, bias=EPSC[:, 1:2]).then_inc(AT.dd_made, 1)

            def keep_s(g):
                hold(act, AT.s_made, g + CREDIT + 1)
                nc.scalar.activation(grp(S, g), PS[:, 7, :].rearrange("p (a d) -> p a d", d=D), ACT.Copy
                                     ).then_inc(AT.s_kept, 1)

            def body(g, par, use, first=False, final_group=False):
                if not final_group:
                    keep_turned(g + 1, 1 - par)
                    exps(g + 1, 1 - par)
                dens(g)
                if not first:
                    keep_s(g - 1)
            keep_turned(0, 0)
            exps(0, 0)
            body(0, 0, 0, first=True)
            rounds(act, 1, G - 2, body)
            body(G - 1, (G - 1) % 2, (G - 1) // 2, final_group=True)
            keep_s(G - 1)

        def act_experts(act, la, func):
            f = FF[la]
            act.sem_inc(f.hid_made, CREDIT)

            def body(t, par, use):
                act.wait_ge(f.h_made, t + CREDIT + 1)
                act.wait_ge(f.par_made, t + 1)
                act.wait_ge(f.y_made, t + 1)
                for c in range(FC):
                    last = nc.scalar.activation(
                        F_H[par][:, c, :], PS[:, 2 + 2 * par + c // 2, (c % 2) * SLOT:(c % 2 + 1) * SLOT],
                        func, bias=F_PAR[par][:, c:c + 1])
                last.then_inc(f.hid_made, 1)
            rounds(act, 0, TILES[la], body)

        def act_combine(act, la):
            b = CB[la]

            def body(g, par, use):
                act.wait_ge(b.u_made, g + 1)
                act.wait_ge(b.x_made, g + 1)
                nc.scalar.activation(C_S[par], C_U[par], ACT.Silu).then_inc(b.silu_made, 1)
            rounds(act, 0, G, body)

        def act_recurrence(act):
            def keep_turned(g, par):
                act.wait_ge(RW.turned, g + CREDIT + 1)
                nc.scalar.activation(R_XT[par][:, :, 1:L + 1], PS[:, 0, :].rearrange("p (s t) -> p s t", s=2),
                                     ACT.Copy).then_inc(RW.xt_made, 1)

            def keep_kvr(g, par):
                act.wait_ge(RW.kv_proj, g + 1)
                act.wait_ge(RW.kv_made, g)
                for ps, dst, s in ((1, R_K, RW.k_kept), (2, R_V, RW.v_kept), (3, R_R[par], RW.r_kept)):
                    if ps == 3:
                        act.wait_ge(RW.r_proj, g + 1)
                    nc.scalar.activation(dst.rearrange("p (h t n) -> p t h n", t=GT, n=HN),
                                         PS[:, ps, :].rearrange("p (t h n) -> p t h n", t=GT, n=HN),
                                         ACT.Copy).then_inc(s, 1)

            def gates(g, par, first=False):
                act.wait_ge(RW.g_made, g + 1)
                if not first:
                    act.wait_ge(RW.yg_made, g - 1)
                nc.scalar.activation(R_G[par], PS[:, 0, :], ACT.Silu).then_inc(RW.g_kept, 1)

            def squares(g):
                act.wait_ge(RW.sq_in, g + 1)
                act.wait_ge(RW.s_made, g)
                nc.scalar.activation(R_SQ, R_YC, ACT.Square).then_inc(RW.sq_made, 1)

            def roots(g):
                act.wait_ge(RW.sd_in, g + 1)
                nc.scalar.activation(R_SM[:, 2, :], R_SM[:, 1, :], ACT.Sqrt, scale=1.0 / HN,
                                     bias=EPSC[:, 2:3]).then_inc(RW.sd_made, 1)

            def affine(g):
                act.wait_ge(RW.yt_made, g + 1)
                nc.scalar.activation(R_YA, PS[:, 1, :], ACT.Identity, scale=COLS[:, C_GNG:C_GNG + 1],
                                     bias=COLS[:, C_GNB:C_GNB + 1]).then_inc(RW.ya_made, 1)

            def keep_s(g):
                hold(act, RW.s_made, g + 1)
                nc.scalar.activation(grp(S, g), PS[:, 2, :].rearrange("p (a d) -> p a d", d=D), ACT.Copy
                                     ).then_inc(RW.s_kept, 1)

            def body(g, par, use, has=(1, 1, 1, 1)):
                if has[0]:
                    keep_s(g - 2)
                if has[1]:
                    squares(g - 1)
                if has[2]:
                    keep_kvr(g + 1, 1 - par)
                if has[1]:
                    roots(g - 1)
                if has[3]:
                    keep_turned(g + 2, par)
                if has[1]:
                    affine(g - 1)
                if has[2]:
                    gates(g + 1, 1 - par, not has[1])
            keep_turned(0, 0)
            keep_turned(1, 1)
            keep_kvr(0, 0)
            gates(0, 0, True)
            all_groups(act, body)
            keep_s(G - 2)
            squares(G - 1)
            roots(G - 1)
            affine(G - 1)
            keep_s(G - 1)

        def dve_norm(v, la):
            s = LNS[la]
            k = Steps(s.ln_steps, 17 if la == 0 else 8)
            v.sem_inc(s.lg_kept, CREDIT)

            def moments(src, st, sm, i):
                for j in range(GT):
                    last = v.bn_stats(st[:, j, :], src(j))
                last.then_inc(s.ln_steps, k.one())
                v.wait_ge(s.ln_steps, k.all())
                v.tensor_tensor(sm[:, 0, :], st[:, :, 1], st[:, :, 4], ALU.add).then_inc(s.ln_steps, k.one())
                v.tensor_tensor(sm[:, 1, :], st[:, :, 1], st[:, :, 4], ALU.subtract).then_inc(s.ln_steps, k.one())
                v.tensor_tensor(sm[:, 2, :], st[:, :, 2], st[:, :, 5], ALU.add).then_inc(s.ln_steps, k.one())
                v.wait_ge(s.ln_steps, k.all())
                v.scalar_tensor_tensor(out=sm[:, 3, :], in0=sm[:, 1, :], scalar=D / 4.0, in1=sm[:, 1, :],
                                       op0=ALU.mult, op1=ALU.mult).then_inc(s.ln_steps, k.one())
                v.tensor_scalar(sm[:, 0, :], sm[:, 0, :], 0.5, None, ALU.mult).then_inc(s.ln_steps, k.one())
                v.wait_ge(s.ln_steps, k.all())
                v.tensor_tensor(sm[:, 4, :], sm[:, 2, :], sm[:, 3, :], ALU.add).then_inc(s.ln_steps, k.one())
                v.wait_ge(s.ln_steps, k.all())
                v.tensor_scalar(sm[:, 5, :], sm[:, 4, :], 1.0 / D, LN_EPS, ALU.mult, ALU.add
                                ).then_inc(s.var_made, 1)

            def norm(g, par, use):
                k.at(g)
                if la == 0:
                    v.wait_ge(x_in[par], 16 * (use + 1))
                v.wait_ge(s.xn_kept, g + 1)
                v.wait_ge(s.xn_turned, g + 1)
                norms = 2 if la == 0 else 1
                moments(lambda j: X[:, bass.ds(g * GT + j, 1), :].rearrange("p a d -> p (a d)"), ST[par], SM[par], 0)
                v.wait_ge(s.sd_made, norms * g + 1)
                v.reciprocal(SM[par][:, 7, :], SM[par][:, 6, :]).then_inc(s.ln_steps, k.one())
                hold(v, s.ln_steps, k.all())
                for j in range(GT):
                    last = v.tensor_scalar(XN_ST[par][:, j, :],
                                           X[:, bass.ds(g * GT + j, 1), :].rearrange("p a d -> p (a d)"),
                                           SM[par][:, 0, j:j + 1], SM[par][:, 7, j:j + 1],
                                           ALU.subtract, ALU.mult)
                last.then_inc(s.xn_made, 1)
                if la == 0:
                    sm = SM[par][:, 8:16, :]
                    v.wait_ge(s.xn_made, g + 1)
                    moments(lambda j: XN_ST[par][:, j, :], ST2[par], sm, 1)
                    v.wait_ge(s.sd_made, 2 * g + 2)
                    v.reciprocal(sm[:, 7, :], sm[:, 6, :]).then_inc(s.ln_steps, k.one())
                    hold(v, s.ln_steps, k.all())
                    for j in range(GT):
                        last = v.tensor_scalar(XN2[:, bass.ds(g * GT + j, 1), :].rearrange("p a d -> p (a d)"),
                                               XN_ST[par][:, j, :], sm[:, 0, j:j + 1], sm[:, 7, j:j + 1],
                                               ALU.subtract, ALU.mult)
                    last.then_inc(s.ln_steps, k.one())

            def logits(g, par):
                hold(v, s.logits_made, g + CREDIT + 1)
                ps = PS[:, 2 + par, 0:GT * E].rearrange("p (t e) -> p t e", e=E)
                if la == 0:
                    v.tensor_copy(grp(LG, g), ps).then_inc(s.lg_kept, 1)
                else:
                    v.tensor_tensor(grp(LG, g), ps, GB[:].unsqueeze(1).to_broadcast([P, GT, E]), ALU.add
                                    ).then_inc(s.lg_kept, 1)

            def body(g, par, use):
                norm(g, par, use)
                logits(g - 1, 1 - par)
            norm(0, 0, 0)
            rounds(v, 1, G - 2, body)
            body(G - 1, (G - 1) % 2, (G - 1) // 2)
            logits(G - 1, (G - 1) % 2)

        def dve_route(v, la):
            c, r = CHOICES[la], RT[la]
            k = Steps(r.rt_steps)

            def step(ins):
                ins.then_inc(r.rt_steps, k.one())
                v.wait_ge(r.rt_steps, k.all())

            ie = IE8[:].unsqueeze(1).to_broadcast([P, NT, E])
            wide = lambda ap: ap.unsqueeze(2).to_broadcast([P, NT, E])
            for i in range(c):
                step(v.tensor_reduce(MX[:, i, :], LG, AX.X, ALU.max))
                step(v.tensor_tensor(RA, LG, wide(MX[:, i, :]), ALU.is_equal))
                step(v.scalar_tensor_tensor(out=RB, in0=RA, scalar=float(-E), in1=ie, op0=ALU.mult, op1=ALU.add))
                step(v.tensor_reduce(IDX[:], RB, AX.X, ALU.min))
                step(v.tensor_scalar(IDX[:], IDX[:], float(E), None, ALU.add))
                step(v.tensor_tensor(OH[i], ie, wide(IDX[:]), ALU.is_equal))
                if i + 1 < c:
                    step(v.scalar_tensor_tensor(out=LG, in0=OH[i], scalar=-HUGE, in1=LG,
                                                op0=ALU.mult, op1=ALU.add))
            if c == 1:
                v.tensor_copy(RA, OH[0]).then_inc(r.onehot_made, 1)
            else:
                v.tensor_tensor(RA, OH[0], OH[1], ALU.add).then_inc(r.onehot_made, 1)
                v.tensor_tensor(WTS[:, 2, :], MX[:, 1, :], MX[:, 0, :], ALU.subtract).then_inc(r.w_exp, 1)
                v.wait_ge(r.w_exp, 2)
                step(v.tensor_scalar(WTS[:, 0, :], WTS[:, 2, :], 1.0, None, ALU.add))
                step(v.reciprocal(WTS[:, 0, :], WTS[:, 0, :]))
                step(v.tensor_tensor(WTS[:, 1, :], WTS[:, 2, :], WTS[:, 0, :], ALU.mult))
            v.wait_ge(r.ranks_made, 1)
            step(v.memset(RONE, 1.0))
            step(v.tensor_copy(RB.rearrange("p t e -> p (t e)"), PS[:, 5, :]))
            for e in range(E):
                last = v.tensor_tensor_scan(RC[:, :, e], RONE, RB[:, :, e], 0.0, ALU.mult, ALU.add)
            step(last)
            step(v.tensor_copy(CNT[:, 0, :], RC[:, NT - 1, :]))
            step(v.tensor_tensor(RTH, CNT[:, 0, :].unsqueeze(2).to_broadcast([P, E, THR]),
                                 ITHR[:].unsqueeze(1).to_broadcast([P, E, THR]), ALU.is_gt))
            step(v.tensor_reduce(CNT[:, 1, :], RTH, AX.X, ALU.add))
            step(v.tensor_tensor_scan(CNT[:, 2, :], RONE[:, 0:E], CNT[:, 1, :], 0.0, ALU.mult, ALU.add))
            step(v.tensor_tensor(CNT[:, 3, :], CNT[:, 2, :], CNT[:, 1, :], ALU.subtract))
            step(v.tensor_scalar(CNT[:, 3, :], CNT[:, 3, :], float(SLOT), None, ALU.mult))
            step(v.tensor_tensor(RTT, ITILE[:].unsqueeze(2).to_broadcast([P, MAXT, E]),
                                 CNT[:, 2, :].unsqueeze(1).to_broadcast([P, MAXT, E]), ALU.is_ge))
            step(v.tensor_reduce(TEF[:], RTT, AX.X, ALU.add))
            step(v.tensor_scalar(TEF[:], TEF[:], float(E - 1), None, ALU.min))
            step(v.tensor_copy(TE[:], TEF[:]))
            step(v.tensor_tensor(RC, RC, RB, ALU.subtract))
            step(v.tensor_tensor(RC, PS[:, 4, :].rearrange("p (t e) -> p t e", e=E), RC, ALU.add))
            step(v.tensor_tensor(RC, RC, CNT[:, 3, :].unsqueeze(1).to_broadcast([P, NT, E]), ALU.add))
            for i in range(c):
                step(v.tensor_tensor(RD, RC, OH[i], ALU.mult))
                step(v.tensor_reduce(POSF[:], RD, AX.X, ALU.add))
                step(v.tensor_copy(POS[:, i, :], POSF[:]))

        def dve_linear_attention(v):
            kp, ko = Steps(AT.phi_steps, 2), Steps(AT.out_steps, 1)
            for par in range(2):
                v.memset(A_VA[par][:, :, D:2 * D], 1.0)

            def phi(g, par):
                kp.at(g)
                kv = PS[:, 2:4, :].rearrange("p b (j c d) -> p (b j) c d", c=2, d=D)
                v.wait_ge(AT.ek_made, g + 1)
                v.tensor_scalar(A_E, A_E, 1.0, None, ALU.min).then_inc(AT.phi_steps, kp.one())
                v.wait_ge(AT.eq_made, g + 1)
                v.tensor_scalar(A_E2, A_E2, 1.0, None, ALU.min).then_inc(AT.phi_steps, kp.one())
                v.wait_ge(AT.phi_steps, kp.all() - 1)
                v.scalar_tensor_tensor(out=A_KF[par], in0=kv[:, :, 0, :], scalar=0.0, in1=A_E,
                                       op0=ALU.max, op1=ALU.add)
                v.wait_ge(AT.phi_steps, kp.all())
                v.scalar_tensor_tensor(out=A_QF[par], in0=PS[:, 1, :], scalar=0.0,
                                       in1=A_E2.rearrange("p a b -> p (a b)"), op0=ALU.max, op1=ALU.add
                                       ).then_inc(AT.phi_made, 1)

            def mask(g):
                v.wait_ge(AT.aug_made, g + 1)
                v.wait_ge(AT.num_made, g)
                v.tensor_tensor(A_M.rearrange("p s (i d) -> p (s i) d", d=D),
                                PS[:, 4, :].rearrange("p (a d) -> p a d", d=D),
                                BLOCK[:].unsqueeze(1).to_broadcast([P, GT, D]), ALU.mult).then_inc(AT.masked, 1)

            def divide(g, par):
                ko.at(g)
                v.wait_ge(AT.dd_made, g + 1)
                v.reciprocal(A_DD, A_DD).then_inc(AT.out_steps, ko.one())
                v.wait_ge(AT.out_steps, ko.all())
                v.wait_ge(AT.s_made, g + 1)
                v.tensor_tensor(A_OT[par], PS[:, 5, :], A_DD, ALU.mult).then_inc(AT.out_made, 1)

            def body(g, par, use, first=False, final_group=False):
                mask(g)
                if not final_group:
                    phi(g + 1, 1 - par)
                divide(g, par)
            phi(0, 0)
            body(0, 0, 0, first=True)
            rounds(v, 1, G - 2, body)
            body(G - 1, (G - 1) % 2, (G - 1) // 2, final_group=True)

        def dve_experts(v, la):
            f, n = FF[la], TILES[la]
            v.wait_ge(b2_in, 16 * (la + 1))
            v.sem_inc(f.xf_made, CREDIT)
            v.sem_inc(f.y_kept, CREDIT)

            def inputs(t, par):
                e = v.value_load(TE[0:1, bass.ds(t, 1)], min_val=0, max_val=E - 1)
                hold(v, f.hid_made, t + 1)
                if la == 0:
                    v.tensor_copy(F_PAR[par][:, FC:FC + 1], COLS[:, bass.ds(e + C_LNG, 1)])
                    v.tensor_copy(F_PAR[par][:, FC + 1:FC + 2], COLS[:, bass.ds(e + C_LNB, 1)])
                v.tensor_copy(F_PAR[par][:, 0:FC], COLS[:, bass.ds(e * FC + C_B1[la], FC)]
                              ).then_inc(f.par_made, 1)
                v.wait_ge(f.turned, t + CREDIT + 1)
                v.wait_ge(f.h_made, t + 1)
                v.wait_ge(f.par_made, t + 1)
                ps = PS[:, par, 0:SLOT]
                if la == 0:
                    v.tensor_scalar(F_X[par], ps, F_PAR[par][:, FC:FC + 1], F_PAR[par][:, FC + 1:FC + 2],
                                    ALU.mult, ALU.add).then_inc(f.xf_made, 1)
                else:
                    v.tensor_copy(F_X[par], ps).then_inc(f.xf_made, 1)
                return e

            def out_bias(e, t, par):
                hold(v, f.y_kept, t + 1)
                v.tensor_copy(F_B2[par], B2[:, bass.ds(e, 1), :].rearrange("p e d -> p (e d)")
                              ).then_inc(f.b2_made, 1)

            def result(t, par, use, first=False):
                v.wait_ge(f.y_made, t + CREDIT + 1)
                v.wait_ge(f.b2_made, t + 1)
                if not first:
                    v.wait_ge((f.y_out0, f.y_out1)[par], 16 * use)
                ps = PS[:, 6 + par, 0:SLOT].rearrange("p (h d) -> p h d", d=D)
                v.tensor_tensor(F_Y[par], ps, F_B2[par].unsqueeze(1).to_broadcast([P, HALVES, D]), ALU.add
                                ).then_inc(f.y_kept, 1)

            def body(t, par, use, first=False):
                e = inputs(t + 1, 1 - par)
                result(t - 1, 1 - par, use + par - 1, first)
                out_bias(e, t + 1, 1 - par)
            for t in range(2):
                out_bias(inputs(t, t), t, t)
            body(1, 1, 0, first=True)
            body(2, 0, 1, first=True)
            rounds(v, 3, n - 4, body)
            result(n - 2, 0, n // 2 - 1)
            result(n - 1, 1, n // 2 - 1)

        def dve_combine(v, la):
            b, c = CB[la], CHOICES[la]
            ku = Steps(b.u_steps, 2 if la else 0)
            kp = Steps(b.post_steps, 1)
            v.sem_inc(b.x_made, CREDIT)
            dst = lambda g, par: grp(X, g) if la == 0 else C_O[par]

            def total(g, par, use):
                ku.at(g)
                v.wait_ge((b.got0, b.got1)[par], 16 * GT * c * (use + 1))
                if not (isinstance(g, int) and g < 2):
                    hold(v, b.silu_made, g - 1)
                if la == 0:
                    v.tensor_tensor(C_U[par], C_Y[par][:, 0:GT, :], grp(XN, g), ALU.add).then_inc(b.u_made, 1)
                else:
                    w = lambda i: WTS[:, i, bass.ds(g * GT, GT)].unsqueeze(2).to_broadcast([P, GT, D])
                    v.tensor_tensor(C_U[par], C_Y[par][:, 0:GT, :], w(0), ALU.mult
                                    ).then_inc(b.u_steps, ku.one())
                    v.tensor_tensor(C_Y[par][:, GT:2 * GT, :], C_Y[par][:, GT:2 * GT, :], w(1), ALU.mult
                                    ).then_inc(b.u_steps, ku.one())
                    v.wait_ge(b.u_steps, ku.all())
                    v.tensor_tensor(C_U[par], C_U[par], C_Y[par][:, GT:2 * GT, :], ALU.add).then_inc(b.u_made, 1)

            def post(g, par, use):
                kp.at(g)
                hold(v, b.silu_made, g + 1)
                v.tensor_tensor(C_T, C_S[par], grp(S, g), ALU.mult).then_inc(b.post_steps, kp.one())
                if la == 1 and not (isinstance(g, int) and g < 2):
                    v.wait_ge(out_done[par], 16 * use)
                hold(v, b.post_steps, kp.all())
                v.tensor_tensor(dst(g, par), C_T, grp(X, g), ALU.add).then_inc(b.x_made, 1)
                v.wait_ge(b.x_made, CREDIT + g + 1)
                v.sem_inc(passed, 1)

            def body(g, par, use):
                total(g, par, use)
                post(g - 1, 1 - par, use + par - 1)
            total(0, 0, 0)
            total(1, 1, 0)
            post(0, 0, 0)
            body(2, 0, 1)
            rounds(v, 3, G - 4, body)
            body(G - 1, (G - 1) % 2, (G - 1) // 2)
            post(G - 1, (G - 1) % 2, (G - 1) // 2)

        def dve_recurrence(v):
            km = Steps(RW.mix_steps, 1)
            kc = Steps(RW.gn_steps, 2)
            for par in range(2):
                last = v.memset(R_XT[par][:, :, 0:1], 0.0)
            last.then_inc(RW.pad_zeroed, 1)
            v.wait_ge(RW.pad_zeroed, 1)
            v.sem_inc(RW.prod_made, CREDIT)

            def mixes(g, par):
                km.at(g)
                v.wait_ge(RW.xt_made, g + 1)
                v.wait_ge(RW.g_made, g)
                now, before = R_XT[par][:, :, 1:L + 1], R_XT[par][:, :, 0:L]
                xx = R_XX.rearrange("p (s t) -> p s t", s=2)
                v.tensor_tensor(xx, before, now, ALU.subtract).then_inc(RW.mix_steps, km.one())
                v.wait_ge(RW.mix_steps, km.all())
                for i in range(4):
                    last = v.scalar_tensor_tensor(out=R_MIX[:, i, :].rearrange("p (s t) -> p s t", s=2), in0=xx,
                                                  scalar=COLS[:, C_MAA + i:C_MAA + i + 1], in1=now,
                                                  op0=ALU.mult, op1=ALU.add)
                last.then_inc(RW.mixed, 1)

            def chunk(g, par, c):
                v.wait_ge(RW.chunk_steps, 4 * g + c + 1)
                if c == 0:
                    v.wait_ge(RW.r_kept, g + 1)
                prod = R_P.rearrange("p (a n m) -> p a n m", n=HN, m=HN)
                ps = PS[:, 4 + 2 * (c % 2):6 + 2 * (c % 2), :].rearrange("p b (a n m) -> p (b a) n m", n=HN, m=HN)
                r = R_R[par][:, c * P:(c + 1) * P].rearrange("p (a n) -> p a n", n=HN)
                v.tensor_tensor(prod, ps, r.unsqueeze(3).to_broadcast([P, HEADS, HN, HN]), ALU.mult
                                ).then_inc(RW.prod_made, 1)
                v.wait_ge(RW.prod_made, 4 * g + c + 1 + CREDIT)
                v.tensor_reduce(R_Y[par][:, c * P:(c + 1) * P].rearrange("p (a m) -> p a m", m=HN),
                                R_P.rearrange("p (a n m) -> p a m n", n=HN, m=HN), AX.X, ALU.add
                                ).then_inc(RW.red_made, 1)
                v.wait_ge(RW.red_made, 4 * g + c + 1)

            def center(g, par):
                kc.at(g)
                v.wait_ge(RW.yg_made, g)
                y = R_Y[par].rearrange("p (a m) -> p a m", m=HN)
                v.tensor_reduce(R_SM[:, 0, :], y, AX.X, ALU.add).then_inc(RW.gn_steps, kc.one())
                v.wait_ge(RW.gn_steps, kc.all())
                v.scalar_tensor_tensor(out=R_YC.rearrange("p (a m) -> p a m", m=HN),
                                       in0=R_SM[:, 0, :].unsqueeze(2).to_broadcast([P, 64, HN]),
                                       scalar=-1.0 / HN, in1=y, op0=ALU.mult, op1=ALU.add).then_inc(RW.sq_in, 1)

            def sum_squares(g):
                v.wait_ge(RW.sq_made, g + 1)
                v.tensor_reduce(R_SM[:, 1, :], R_SQ.rearrange("p (a m) -> p a m", m=HN), AX.X, ALU.add
                                ).then_inc(RW.sd_in, 1)

            def normalize(g):
                v.wait_ge(RW.sd_made, g + 1)
                v.reciprocal(R_SM[:, 3, :], R_SM[:, 2, :]).then_inc(RW.gn_steps, kc.one())
                v.wait_ge(RW.gn_steps, kc.all())
                v.tensor_tensor(R_YN.rearrange("p t (h m) -> p h t m", m=HN),
                                R_YC.rearrange("p (h t m) -> p h t m", t=GT, m=HN),
                                R_SM[:, 3, :].rearrange("p (h t) -> p h t", t=GT).unsqueeze(3)
                                .to_broadcast([P, HEADS, GT, HN]), ALU.mult).then_inc(RW.yn_made, 1)

            def gate(g, par):
                v.wait_ge(RW.ya_made, g + 1)
                v.wait_ge(RW.g_kept, g + 1)
                v.tensor_tensor(R_YG, R_YA, R_G[par], ALU.mult).then_inc(RW.yg_made, 1)

            def body(g, par, use, has=(1, 1, 1, 1)):
                if has[2]:
                    mixes(g + 1, 1 - par)
                chunk(g, par, 0)
                if has[1]:
                    center(g - 1, 1 - par)
                chunk(g, par, 1)
                if has[1]:
                    sum_squares(g - 1)
                chunk(g, par, 2)
                if has[1]:
                    normalize(g - 1)
                chunk(g, par, 3)
                if has[1]:
                    gate(g - 1, 1 - par)
            mixes(0, 0)
            all_groups(v, body)
            center(G - 1, (G - 1) % 2)
            sum_squares(G - 1)
            normalize(G - 1)
            gate(G - 1, (G - 1) % 2)

        block = ctx.enter_context(nc.Block())

        @block.sync
        def _(sp):
            sp.dma_start(WA[:, 0, :], a["L0_attn_Wq"]).then_inc(params_in, 16)
            sp.dma_start(WA[:, 1, :], a["L0_attn_Wk"]).then_inc(params_in, 16)
            sp.dma_start(WA[:, 2, :], a["L0_attn_Wv"]).then_inc(params_in, 16)
            sp.dma_start(WA[:, 3, :], a["L0_attn_Wo"]).then_inc(params_in, 16)
            for i, n in enumerate(("w_k", "w_v", "w_r", "w_g", "w_o")):
                sp.dma_start(WNAT[:, i, :], a["L1_attn_" + n]).then_inc(params_in, 16)
            sp.dma_start(GWT[:], a["L1_ffn_gate_w"]).then_inc(params_in, 16)
            row = lambda n: a[n].rearrange("(o d) -> o d", o=1)
            sp.dma_start(GB[:], row("L1_ffn_gate_b").to_broadcast([P, E])).then_inc(params_in, 16)
            sp.dma_start(TD[:], row("L1_attn_time_decay").to_broadcast([P, HEADS])).then_inc(params_in, 16)
            sp.dma_start(TU[:], row("L1_attn_time_faaaa").to_broadcast([P, HEADS])).then_inc(params_in, 16)
            load_b2(sp, 0)
            sp.wait_ge(rows_zeroed, 1)
            for c, n, r in ((C_B1[0], "L0_ffn_b1", E * FC), (C_B1[1], "L1_ffn_b1", E * FC)):
                sp.dma_start(ROWS[c:c + r, :], a[n].rearrange("e (c f) -> (e c) f", f=P)).then_inc(params_in, 16)
            for c, n in ((C_LNG, "L0_ffn_ln_g"), (C_LNB, "L0_ffn_ln_b"), (C_CENT, "L0_ffn_centroids")):
                sp.dma_start(ROWS[c:c + E, :], a[n]).then_inc(params_in, 16)
            for c, n in ((C_MAA, "time_maa_k"), (C_MAA + 1, "time_maa_v"), (C_MAA + 2, "time_maa_r"),
                         (C_MAA + 3, "time_maa_g"), (C_GNG, "ln_g"), (C_GNB, "ln_b")):
                sp.dma_start(ROWS[c:c + 1, :], row("L1_attn_" + n)).then_inc(params_in, 16)

            def load_x(g, par, use):
                sp.wait_ge(x_in[par], 16 * use)
                sp.dma_start(grp(X, g), x_dram[:, bass.ds(g * GT, GT), :]).then_inc(x_in[par], 16)
            for g in range(2):
                sp.dma_start(grp(X, g), x_dram[:, g * GT:(g + 1) * GT, :]).then_inc(x_in[g], 16)
            rounds(sp, 2, G - 2, load_x)
            sp.wait_ge(s_zeroed, 1)
            fill = disp.rearrange("(c p r) d -> c p (r d)", p=P, r=16)
            for c in range(MAXT * SLOT // (P * 16)):
                sp.dma_start(fill[c], S[:, 0:16, :].rearrange("p a d -> p (a d)")).then_inc(zero_filled, 16)
            barrier(sp, 1)
            barrier(sp, 2)
            sp_attention_loads(sp, 0, A_XS, (AT.xs_in0, AT.xs_in1), AT.turned, XN2, 0)
            barrier(sp, 3)
            sp_experts(sp, 0)
            barrier(sp, 4)
            load_b2(sp, 1)
            barrier(sp, 5)
            barrier(sp, 6)
            barrier(sp, 7)
            sp_attention_loads(sp, 1, R_XS, (RW.xs_in0, RW.xs_in1), RW.turned, XN, 2)
            barrier(sp, 8)
            sp_experts(sp, 1)
            barrier(sp, 9)

            def store(g, par, use):
                sp.wait_ge(CB[1].x_made, g + CREDIT + 1)
                sp.dma_start(out_dram[:, bass.ds(g * GT, GT), :], C_O[par]).then_inc(out_done[par], 16)
            rounds(sp, 0, G, store)
            for par in range(2):
                sp.wait_ge(out_done[par], 16 * G // 2)

        @block.gpsimd
        def _(pool):
            k = Steps(pool_steps)

            def made(ins):
                ins.then_inc(pool_steps, k.one())
                pool.wait_ge(pool_steps, k.all())

            made(pool.memset(ONES[:], 1.0))
            made(pool.affine_select(out=IDENT[:], in_=ONES[:], compare_op=ALU.is_equal, fill=0.0, base=0,
                                    pattern=[[1, P]], channel_multiplier=-1))
            made(pool.affine_select(out=UPPER[:], in_=ONES[:], compare_op=ALU.is_gt, fill=0.0, base=0,
                                    pattern=[[1, P]], channel_multiplier=-1))
            bv = BLOCK[:].rearrange("p (h n) -> p h n", n=HN)
            ov = ONES[:].rearrange("p (h n) -> p h n", n=HN)
            made(pool.affine_select(out=bv, in_=ov, compare_op=ALU.is_ge, fill=0.0, base=0,
                                    pattern=[[-HN, HEADS], [0, HN]], channel_multiplier=1))
            made(pool.affine_select(out=bv, in_=bv, compare_op=ALU.is_ge, fill=0.0, base=HN - 1,
                                    pattern=[[HN, HEADS], [0, HN]], channel_multiplier=-1))
            made(pool.iota(IE8[:], [[1, E]], base=-E, channel_multiplier=0, allow_small_or_imprecise_dtypes=True))
            made(pool.iota(ITHR[:], [[SLOT, THR]], base=0, channel_multiplier=0,
                           allow_small_or_imprecise_dtypes=True))
            made(pool.iota(ITILE[:], [[1, MAXT]], base=0, channel_multiplier=0,
                           allow_small_or_imprecise_dtypes=True))
            made(pool.iota(EXPO, [[1, 2 * P]], base=-1, channel_multiplier=-1,
                           allow_small_or_imprecise_dtypes=True))
            made(pool.affine_select(out=EXPO, in_=EXPO, compare_op=ALU.is_ge, fill=0.0, base=-1,
                                    pattern=[[1, 2 * P]], channel_multiplier=-1))
            for i, eps in enumerate((LN_EPS, DEN_EPS, GN_EPS)):
                made(pool.memset(EPSC[:, i:i + 1], eps))
            pool.memset(ZERO4[:], 0.0).then_inc(consts_made, 1)
            pool.wait_ge(exp_made, HEADS)
            for h in range(HEADS):
                d = TOEP[:, h, 0:P]
                pool.affine_select(out=d, in_=d, compare_op=ALU.is_ge, fill=0.0, base=-1,
                                   pattern=[[1, P]], channel_multiplier=-1).then_inc(toep_cut, 1)
            barrier(pool, 1)
            barrier(pool, 2)
            pool.wait_ge(zero_filled, 16 * (MAXT * SLOT // (P * 16)))
            pool_send(pool, 0, None)
            barrier(pool, 3)
            pool_store_y(pool, 0)
            barrier(pool, 4)
            pool_fetch_y(pool, 0)
            barrier(pool, 5)
            barrier(pool, 6)
            barrier(pool, 7)

            def kv_products(g, par, first):
                hold(pool, RW.v_kept, g + 1)
                if not first:
                    hold(pool, RW.chunk_steps, 4 * g - 4)
                pool.tensor_tensor(
                    KV[par].rearrange("p (a n m) -> p a n m", n=HN, m=HN),
                    R_K.rearrange("p (a n) -> p a n", n=HN).unsqueeze(3).to_broadcast([P, 64, HN, HN]),
                    R_V.rearrange("p (a m) -> p a m", m=HN).unsqueeze(2).to_broadcast([P, 64, HN, HN]),
                    ALU.mult).then_inc(RW.kv_made, 1)
            pool_send(pool, 1, kv_products)
            barrier(pool, 8)
            pool_store_y(pool, 1)
            barrier(pool, 9)
            pool_fetch_y(pool, 1)

        @block.tensor
        def _(pe):
            pe.wait_ge(consts_made, 1)
            pe.wait_ge(params_in, PARAMS)
            pe.transpose(PS[:, 0, 0:P], ROWS, IDENT[:]).then_inc(cols_turned, 1)
            for i in range(5):
                pe.transpose(PS[:, 1 + i, 0:P], WNAT[:, i, :], IDENT[:]).then_inc(cols_turned, 1)
            pe.wait_ge(cols_kept, 6)
            pe_norm(pe, 0)
            barrier(pe, 1)
            pe_ranks(pe, 0)
            barrier(pe, 2)
            pe_linear_attention(pe)
            barrier(pe, 3)
            pe_experts(pe, 0)
            barrier(pe, 4)
            barrier(pe, 5)
            pe_norm(pe, 1)
            barrier(pe, 6)
            pe_ranks(pe, 1)
            barrier(pe, 7)
            pe_recurrence(pe)
            barrier(pe, 8)
            pe_experts(pe, 1)
            barrier(pe, 9)

        @block.scalar
        def _(act):
            act.wait_ge(cols_turned, 6)
            nc.scalar.activation(COLS[:], PS[:, 0, 0:P], ACT.Copy).then_inc(cols_kept, 1)
            for i in range(5):
                nc.scalar.activation(WT[:, i, :], PS[:, 1 + i, 0:P], ACT.Copy).then_inc(cols_kept, 1)
            act.wait_ge(params_in, PARAMS)
            nc.scalar.activation(LW[:], TD[:], ACT.Exp).then_inc(lw_made, 1)
            act.wait_ge(lw_made, 2)
            for h in range(HEADS):
                nc.scalar.activation(TOEP[:, h, :], EXPO, ACT.Exp, scale=LW[:, h:h + 1]).then_inc(exp_made, 1)
            act_norm(act, 0)
            barrier(act, 1)
            barrier(act, 2)
            act_linear_attention(act)
            barrier(act, 3)
            act_experts(act, 0, ACT.Relu)
            barrier(act, 4)
            act_combine(act, 0)
            barrier(act, 5)
            act_norm(act, 1)
            barrier(act, 6)
            act.wait_ge(RT[1].w_exp, 1)
            nc.scalar.activation(WTS[:, 2, :], WTS[:, 2, :], ACT.Exp).then_inc(RT[1].w_exp, 1)
            barrier(act, 7)
            act_recurrence(act)
            barrier(act, 8)
            act_experts(act, 1, ACT.Gelu)
            barrier(act, 9)
            act_combine(act, 1)

        @block.vector
        def _(v):
            v.memset(ROWS, 0.0).then_inc(rows_zeroed, 1)
            v.memset(S[:, 0:16, :], 0.0).then_inc(s_zeroed, 1)
            v.wait_ge(lw_made, 1)
            v.tensor_scalar(LW[:], LW[:], 1.0e4, -1.0, ALU.min, ALU.mult).then_inc(lw_made, 1)
            v.wait_ge(toep_cut, HEADS)
            for h in range(HEADS):
                v.scalar_tensor_tensor(out=TOEP[:, h, 0:P], in0=IDENT[:], scalar=TU[:, h:h + 1],
                                       in1=TOEP[:, h, 0:P], op0=ALU.mult, op1=ALU.add).then_inc(toep_made, 1)
            dve_norm(v, 0)
            barrier(v, 1)
            dve_route(v, 0)
            barrier(v, 2)
            dve_linear_attention(v)
            barrier(v, 3)
            dve_experts(v, 0)
            barrier(v, 4)
            dve_combine(v, 0)
            barrier(v, 5)
            dve_norm(v, 1)
            barrier(v, 6)
            dve_route(v, 1)
            barrier(v, 7)
            dve_recurrence(v)
            barrier(v, 8)
            dve_experts(v, 1)
            barrier(v, 9)
            dve_combine(v, 1)


_INS = ['L0_attn_x', 'L0_attn_Wq', 'L0_attn_Wk', 'L0_attn_Wv', 'L0_attn_Wo', 'L0_ffn_centroids', 'L0_ffn_ln_g',
        'L0_ffn_ln_b', 'L0_ffn_W1', 'L0_ffn_b1', 'L0_ffn_W2', 'L0_ffn_b2', 'L1_attn_w_r', 'L1_attn_w_k',
        'L1_attn_w_v', 'L1_attn_w_g', 'L1_attn_w_o', 'L1_attn_time_maa_k', 'L1_attn_time_maa_v',
        'L1_attn_time_maa_r', 'L1_attn_time_maa_g', 'L1_attn_time_decay', 'L1_attn_time_faaaa', 'L1_attn_ln_g',
        'L1_attn_ln_b', 'L1_ffn_gate_w', 'L1_ffn_gate_b', 'L1_ffn_w1', 'L1_ffn_b1', 'L1_ffn_w2', 'L1_ffn_b2']


def kernel(**inputs):
    import numpy as _np
    import concourse.bacc as _bacc
    from concourse import mybir as _mybir
    from concourse.bass_utils import run_bass_kernel_spmd as _run

    nc = _bacc.Bacc("TRN2", target_bir_lowering=False, num_devices=1)
    arrays, args = {}, {}
    for name in _INS:
        arr = _np.ascontiguousarray(inputs[name])
        arrays[f"in_{name}"] = arr
        args[name] = nc.dram_tensor(f"in_{name}", arr.shape, _mybir.dt.from_np(arr.dtype), kind="ExternalInput").ap()
    out = nc.dram_tensor("out_0", (B, L, D), _mybir.dt.float32, kind="ExternalOutput").ap()
    program(nc, args, out)
    r = _run(nc, [arrays], core_ids=[0])
    return r.results[0]["out_0"]
```

```python
from collections import namedtuple
from contextlib import ExitStack

import concourse.bass as bass
from concourse import mybir

ALU = mybir.AluOpType
ACT = mybir.ActivationFunctionType
F32 = mybir.dt.float32
I32 = mybir.dt.int32
U32 = mybir.dt.uint32
AX = mybir.AxisListType

P = 128
B, L, D = 32, 256, 128
TOK = B * L
NT = TOK // P
GT = 4
G = NT // GT
GW = GT * P
E, F = 8, 512
FC = F // P
HEADS, HN = 16, 8
SLOT = 256
HALVES = SLOT // P
CHOICES = (1, 2)
TILES = tuple(TOK * c // SLOT + E - 1 for c in CHOICES)
MAXT = max(TILES)
THR = TOK // SLOT
ROW = D + 2
NO_TOKEN = 2 * TOK
FILL = 16
FILLS = tuple(-(-t * SLOT // (P * FILL)) for t in TILES)
YB = 4
DVE_TILES = 2
PT, PAIRS = 2 * GT, G // 2
GOT_BEFORE = (16 * PAIRS // 2,) * 2 + (0,) * 2
CHOSEN_EARLY = NT - 2 * PT
LN_EPS = 1e-5
DEN_EPS = 1e-6
GN_EPS = 1e-5 * 64
HUGE = 3.0e38
ENGINES = 5
WB = 4
COL_PARAMS = 16 * 11
PARAMS = 16 * 12
LOADS_BEFORE = ((0,) * WB, tuple((TILES[0] + WB - 1 - q) // WB for q in range(WB)))
CREDIT = 2

WORDS = 11012
C_B1 = (0, E * FC)
C_LNG = 2 * E * FC
C_LNB = C_LNG + E
C_CENT = C_LNB + E
C_MAA = C_CENT + E
C_GNG = C_MAA + 4
C_GNB = C_GNG + 1


class Steps:

    def __init__(self, sem, per=0):
        self.sem, self.per, self.base, self.n = sem, per, 0, 0

    def at(self, i):
        assert self.n in (0, self.per), (self.n, self.per)
        self.base, self.n = i * self.per, 0

    def one(self):
        self.n += 1
        return 1

    def all(self):
        return self.base + self.n


def program(nc, a, out):
    with ExitStack() as ctx:
        def sb(name, shape, dt=F32):
            return ctx.enter_context(nc.sbuf_tensor(name, shape, dt))

        def sem(name):
            return ctx.enter_context(nc.semaphore(name))

        X = sb("X", [P, NT, D])
        XN = sb("XN", [P, NT, D])
        S = sb("S", [P, NT, D])
        XN2 = sb("XN2", [P, NT, D])
        KV = [XN2[:, par * NT // 2:(par + 1) * NT // 2, :].rearrange("p a b -> p (a b)") for par in range(2)]
        TOEP = sb("TOEP", [P, HEADS, 2 * P])
        COLS = sb("COLS", [P, P])
        IDENT = sb("IDENT", [P, P])
        UPPER = sb("UPPER", [P, P])
        ONES = sb("ONES", [P, P])
        BLOCK = sb("BLOCK", [P, D + HEADS])
        ZERO4 = sb("ZERO4", [P, 1])
        EPSC = sb("EPSC", [P, 3])
        IE8 = sb("IE8", [P, E])
        ITHR = sb("ITHR", [P, THR])
        ITILE = sb("ITILE", [P, MAXT])
        TAG = sb("TAG", [P, NT, 2])
        DST = sb("DST", [P, WB, HALVES], U32)
        TD = sb("TD", [P, HEADS])
        TU = sb("TU", [P, HEADS])
        LW = sb("LW", [P, HEADS])
        GB = sb("GB", [P, E])
        GWT = sb("GWT", [P, E])
        WA = sb("WA", [P, 4, D])
        WT = sb("WT", [P, 5, D])
        B2 = sb("B2", [P, E, D])
        MX = sb("MX", [P, 2, NT])
        IDX = sb("IDX", [P, NT])
        CNT = sb("CNT", [P, 4, E])
        TE = sb("TE", [P, MAXT], I32)
        TEF = sb("TEF", [P, MAXT])
        POSF = sb("POSF", [P, NT])
        POS = sb("POS", [P, 2, NT], U32)
        WTS = sb("WTS", [P, 3, NT])
        ARENA = sb("ARENA", [P, WORDS])

        def carve(space=None, begin=0):
            space = ARENA if space is None else space
            at, words = [begin], space.shape[-1]

            def take(*shape):
                n = 1
                for s in shape:
                    n *= s
                v = space[:, at[0]:at[0] + n]
                at[0] += n
                assert at[0] <= words, at[0]
                if len(shape) == 2:
                    v = v.rearrange("p (a b) -> p a b", a=shape[0])
                if len(shape) == 3:
                    v = v.rearrange("p (a b c) -> p a b c", a=shape[0], b=shape[1])
                return v
            return take

        PS = ctx.enter_context(nc.psum_tensor("PS", [P, 8, 512], F32))
        disp = [nc.dram_tensor(f"disp{la}", (FILLS[la] * P * FILL, ROW), F32, kind="Internal").ap() for la in range(2)]
        ybuf = nc.dram_tensor("ybuf", (3 * TOK + P * FILL, D), F32, kind="Internal").ap()

        x_dram = a["L0_attn_x"].rearrange("b (h p) d -> p (b h) d", p=P)
        out_dram = out.rearrange("b (h p) d -> p (b h) d", p=P)

        phase_done = sem("phase_done")
        passed = sem("passed")
        td_in = sem("td_in")
        cols_in = sem("cols_in")
        params_in = sem("params_in")
        wt_turned = sem("wt_turned")
        b2_in = sem("b2_in")
        rows_zeroed = sem("rows_zeroed")
        consts_made = sem("consts_made")
        pool_steps = sem("pool_steps")
        cols_turned = sem("cols_turned")
        cols_kept = sem("cols_kept")
        zero_filled = [sem(f"zero_filled{i}") for i in range(2)]
        ranks_kept = sem("ranks_kept")
        slots_made = sem("slots_made")
        lw_made = sem("lw_made")
        exp_made = sem("exp_made")
        toep_cut = sem("toep_cut")
        x_in = [sem(f"x_in{i}") for i in range(2)]
        out_done = sem("out_done")

        def some(layer, names):
            names = names.split()
            return namedtuple("Sems", names)(*(sem(f"{n}_{layer}") for n in names))

        LNS = [some(la, "ln_steps var_made sd_made rs_made xn_made xn_kept xn_turned xt_made logits_made lg_kept")
               for la in range(2)]
        w1_made = sem("w1_made")
        xp_made = sem("xp_made")
        nb_made, xn2_kept = sem("nb_made"), sem("xn2_kept")
        RT = [some(la, "rt_steps onehot_made ranks_made w_exp") for la in range(2)]
        SC = [some(la, "staged0 staged1 slots_staged sent0 sent1") for la in range(2)]
        w_in = [sem(f"w_in{q}") for q in range(WB)]
        rows_in = [sem(f"rows_in{q}") for q in range(WB)]
        got = [sem(f"got{q}") for q in range(YB)]
        FF = [some(la, "turned xf_made h_made "
                       "hid_made y_made dst_steps b2_made par_made y_kept y_out0 y_out1") for la in range(2)]
        CB = [some(la, "u_steps u_made silu_made post_steps x_made") for la in range(2)]
        AT = some("a0", "xs_in0 xs_in1 turned xt_made qkv_made ek_made eq_made v_made phi_steps phi_made "
                        "aug_made masked num_made out_steps out_made o_turned ot_kept s_made s_kept")
        RW = some("a1", "xs_in0 xs_in1 turned xt_made mix_steps mixed kv_proj r_proj g_made k_kept v_kept r_kept "
                        "g_kept kv_made chunk_steps prod_made red_made gn_steps sq_in sq_made "
                        "sd_in sd_made yn_made yt_made ya_made yg_made s_made s_kept pad_zeroed")

        def rounds(eng, first, count, body, ways=2, turns=1):
            with eng.Fori(0, count // (ways * turns)) as it:
                for u in range(ways * turns):
                    q = (first + u) % ways
                    body(it * (ways * turns) + (first + u), q, it * turns + (first + u) // ways)

        def tile_rounds(eng, first, end, body):
            start = first
            while start < WB or (end - start) % WB:
                body(start, start % WB, start // WB)
                start += 1
            rounds(eng, start, end - start, body, WB)

        def hold(eng, s, value):
            eng.wait_ge(s, value)
            eng.sem_inc(passed, 1)

        def barrier(eng, n):
            eng.drain().then_inc(phase_done, 1)
            eng.wait_ge(phase_done, ENGINES * n)

        def row(arr, g, j):
            return arr[:, bass.ds(g * GT + j, 1), :].rearrange("p a d -> p (a d)")

        def grp(arr, g):
            return arr[:, bass.ds(g * GT, GT), :]

        t1 = carve()
        XN_ST = [t1(GT, D) for _ in range(2)]
        XT_ST = [t1(GT, P) for _ in range(2)]
        ST = [t1(2 * GT, 6) for _ in range(2)]
        SM = [t1(9, 2 * GT) for _ in range(2)]
        X_COLS, N_COLS, BOTH_COLS = slice(0, GT), slice(GT, 2 * GT), slice(0, 2 * GT)
        EMPTY = S[:].rearrange("p a d -> p (a d)")[:, 0:FILL * ROW]
        ROWS = t1(P)
        WNAT = t1(5, D)
        EXPO = S[:].rearrange("p a d -> p (a d)")[:, 24 * D:26 * D]

        t2 = carve(S[:].rearrange("p a d -> p (a d)"), NT * D // 2 - 512)
        LG = t2(NT, E)
        RA, RB, RC, RD = [t2(NT, E) for _ in range(4)]
        RTH = t2(E, THR)
        RTT = t2(MAXT, E)
        RONE = t2(NT)
        OH = [t2(NT, E) for _ in range(2)]

        t3 = carve()
        A_XS = [t3(GT, D) for _ in range(2)]
        A_XT = [t3(GT, P) for _ in range(2)]
        A_E = t3(GT, P)
        A_E2 = t3(GT, P)
        A_KF = [t3(GT, D) for _ in range(2)]
        A_VA = [t3(GT, D + HEADS) for _ in range(2)]
        A_QF = [t3(GW) for _ in range(2)]
        A_M = t3(2, D + HEADS)
        A_DD = t3(GT, HEADS)
        A_O = t3(GT, D)
        A_OT = t3(GW)
        A_ND = PS[:, 5:7, :].rearrange("p b (j c) -> p (b j) c", j=2)
        A_NUM, A_DEN = A_ND[:, :, 0:D], A_ND[:, :, D:D + HEADS]

        t4 = carve()
        F_W1 = [t4(F) for _ in range(WB)]
        F_W2 = [t4(FC, D) for _ in range(WB)]
        F_D = [t4(HALVES, ROW) for _ in range(WB)]
        F_C = [t4(HALVES) for _ in range(2)]
        F_X = [t4(SLOT) for _ in range(2)]
        F_H = [t4(FC, SLOT) for _ in range(2)]
        F_Y = [t4(HALVES, D) for _ in range(2)]
        F_PAR = [t4(FC + 2) for _ in range(2)]
        F_B2 = [t4(D) for _ in range(2)]

        t7 = carve()
        M_Y = [t7(PT, D) for _ in range(2)]
        M_W = [t7(PT, D) for _ in range(2)]
        M_N = [t7(PT, D) for _ in range(2)]
        M_T = [t7(PT, P) for _ in range(2)]
        M_ST = [t7(PT, 6) for _ in range(2)]
        M_SM = [t7(8, PT) for _ in range(2)]

        t5 = carve()
        C_Y = [t5(2 * GT, D) for _ in range(YB)]
        C_U = [t5(GT, D) for _ in range(2)]
        C_S = [t5(GT, D) for _ in range(2)]
        C_T = [t5(GT, D) for _ in range(2)]

        t6 = carve()
        R_XS = [t6(GT, D) for _ in range(2)]
        R_XT = [t6(2, L + 1) for _ in range(2)]
        R_MIX = t6(4, GW)
        R_K, R_V = [t6(GW) for _ in range(2)]
        R_R = [t6(GW) for _ in range(2)]
        R_G = [t6(GW) for _ in range(2)]
        R_P = [t6(1024), B2[:].rearrange("p e d -> p (e d)")]
        R_Y = [t6(GW) for _ in range(2)]
        R_YC = t6(GW)
        R_SQ = t6(GW)
        R_YN = t6(GT, D)
        R_XX = R_YN.rearrange("p a b -> p (a b)")
        R_YA = R_YC
        R_YG = WA[:].rearrange("p a d -> p (a d)")
        R_SM = t6(4, 64)
        STAGE = [sb(f"STAGE{i}", [P, GT, ROW]) for i in range(2)]
        POS_ST = [sb(f"POS_ST{i}", [P, 2, GT], U32) for i in range(2)]

        def load_b2(sp, la):
            src = a[f"L{la}_ffn_b2"].rearrange("(o e) d -> o (e d)", o=1).to_broadcast([P, E * D])
            sp.dma_start(B2[:].rearrange("p e d -> p (e d)"), src).then_inc(b2_in, 16)

        def sp_attention_loads(sp, la, dst, sems, turned, src, ahead):
            sc = SC[la]
            n = 16 * GT * CHOICES[la]

            def load(i, par, use):
                hold(sp, turned, i + 1)
                sp.dma_start(dst[par], grp(XN, i)).then_inc(sems[par], 16)

            def stage(g, par, use, first=False):
                if not first:
                    hold(sp, (sc.sent0, sc.sent1)[par], n * use)
                sp.dma_start(STAGE[par][:, :, 0:D], grp(src, g)).then_inc((sc.staged0, sc.staged1)[par], 16)

            def both(g, par, use):
                load(g + ahead, (par + ahead) % 2, use)
                stage(g, par, use)
            for i in range(ahead):
                load(i, i % 2, 0)
            for g in range(2):
                load(g + ahead, (g + ahead) % 2, 0)
                stage(g, g, 0, True)
            rounds(sp, 2, G - 2 - ahead, both)
            for g in range(G - ahead, G):
                stage(g, g % 2, g // 2)

        def sp_experts(sp, la):
            f = FF[la]
            w1 = a[f"L{la}_ffn_W1" if la == 0 else "L1_ffn_w1"]
            w2 = a[f"L{la}_ffn_W2" if la == 0 else "L1_ffn_w2"]

            def load(t, q, use, first=False):
                e = sp.value_load(TE[0:1, bass.ds(t, 1)], min_val=0, max_val=E - 1)
                if not first:
                    sp.wait_ge(f.xf_made, t + CREDIT - WB + 1)
                sp.dma_start(F_D[q], disp[la].rearrange("(t h p) d -> p (t h) d", h=HALVES, p=P)
                             [:, bass.ds(t * HALVES, HALVES), :]).then_inc(rows_in[q], 16)
                if not first:
                    sp.wait_ge(f.h_made, t + CREDIT - WB + 1)
                sp.dma_start(F_W1[q], w1.rearrange("e d f -> d e f")[:, bass.ds(e, 1), :]
                             .rearrange("p e f -> p (e f)")).then_inc(w_in[q], 16)
                if not first:
                    sp.wait_ge(f.y_made, t + CREDIT - WB + 1)
                sp.dma_start(F_W2[q], w2.rearrange("e (c p) d -> p (e c) d", p=P)
                             [:, bass.ds(e * FC, FC), :]).then_inc(w_in[q], 16)
            for t in range(WB):
                load(t, t, 0, True)
            tile_rounds(sp, WB, TILES[la], load)

        def pool_send(pool, la, ahead):
            c, s = CHOICES[la], SC[la]
            sent = (s.sent0, s.sent1)

            def send(g, par, use, first=False):
                if ahead and not (isinstance(g, int) and g == G - 1):
                    ahead(g + 1, 1 - par)
                if isinstance(g, int) and g == 0:
                    pool.wait_ge(slots_made, la + 1)
                if not first:
                    hold(pool, sent[par], use * 16 * GT * c)
                pool.tensor_copy(POS_ST[par][:, 0:c, :], POS[:, 0:c, bass.ds(g * GT, GT)]).then_inc(s.slots_staged, 1)
                pool.tensor_copy(STAGE[par][:, :, D:ROW], grp(TAG, g)).then_inc(s.slots_staged, 1)
                hold(pool, s.slots_staged, 2 * g + 2)
                hold(pool, (s.staged0, s.staged1)[par], 16 * (use + 1))
                for j in range(GT):
                    for i in range(c):
                        pool.indirect_dma_start(
                            out=disp[la], out_offset=bass.IndirectOffsetOnAxis(ap=POS_ST[par][:, i, j:j + 1], axis=0),
                            in_=STAGE[par][:, j, :], in_offset=None).then_inc(sent[par], 16)
            if ahead:
                ahead(0, 0)
            send(0, 0, 0, True)
            send(1, 1, 0, True)
            rounds(pool, 2, G - 4, send)
            for g in (G - 2, G - 1):
                send(g, g % 2, g // 2)
            for par in range(2):
                pool.wait_ge(sent[par], G // 2 * 16 * GT * c)

        def pool_store_y(pool, la):
            f = FF[la]

            def store(t, q, use):
                hold(pool, f.y_kept, t + CREDIT + 1)
                for h in range(HALVES):
                    pool.indirect_dma_start(
                        out=ybuf, out_offset=bass.IndirectOffsetOnAxis(ap=DST[:, q, h:h + 1], axis=0),
                        in_=F_Y[q % 2][:, h, :], in_offset=None).then_inc((f.y_out0, f.y_out1)[q % 2], 16)
            tile_rounds(pool, 0, TILES[la], store)
            pool.wait_ge(f.y_out0, 16 * HALVES * ((TILES[la] + 1) // 2))
            pool.wait_ge(f.y_out1, 16 * HALVES * (TILES[la] // 2))

        def weight(i, g):
            return WTS[:, i, bass.ds(g * GT, GT)].unsqueeze(2).to_broadcast([P, GT, D])

        def pool_combine(pool):
            def second_choice(g, q, use):
                hold(pool, got[q], GOT_BEFORE[q] + 16 * CHOICES[1] * (use + 1))
                y = C_Y[q][:, GT:2 * GT, :]
                pool.tensor_tensor(y, y, weight(1, g), ALU.mult).then_inc(w1_made, 1)


            def result(g, par):
                hold(pool, CB[1].post_steps, g + 1)
                pool.tensor_tensor(grp(X, g), C_T[par], grp(X, g), ALU.add).then_inc(CB[1].x_made, 1)

            def body(g, q, use):
                second_choice(g, q, use)
                result(g - 2, q % 2)
            second_choice(0, 0, 0)
            second_choice(1, 1, 0)
            body(2, 2, 0)
            rounds(pool, 3, G - YB, body, YB)
            body(G - 1, YB - 1, G // YB - 1)
            for g in (G - 2, G - 1):
                result(g, g % 2)

        def sp_fetch_y(sp):
            def fetch(g, q, use, first=False):
                if not first:
                    hold(sp, CB[1].u_made, g - YB + 1)
                for i in range(CHOICES[1]):
                    rows = ybuf[i * TOK:(i + 1) * TOK, :].rearrange("(n p) d -> p n d", p=P)
                    sp.dma_start(C_Y[q][:, i * GT:(i + 1) * GT, :], rows[:, bass.ds(g * GT, GT), :]
                                 ).then_inc(got[q], 16)

            def store(g):
                hold(sp, CB[1].x_made, g + CREDIT + 1)
                sp.dma_start(out_dram[:, bass.ds(g * GT, GT), :], grp(X, g)).then_inc(out_done, 16)

            def body(g, q, use):
                fetch(g, q, use)
                store(g - YB - 1)
            for g in range(YB):
                fetch(g, g, 0, True)
            fetch(YB, 0, 1)
            rounds(sp, YB + 1, G - 2 * YB, body, YB)
            for g in range(G - YB + 1, G):
                body(g, g % YB, g // YB)
            for g in range(G - YB - 1, G):
                store(g)
            sp.wait_ge(out_done, 16 * G)

        def sp_fetch_pairs(sp):
            rows = ybuf[0:TOK, :].rearrange("(n p) d -> p n d", p=P)

            def fetch(i, par, use, first=False):
                if not first:
                    hold(sp, CB[0].silu_made, i - 1)
                sp.dma_start(M_Y[par], rows[:, bass.ds(i * PT, PT), :]).then_inc(got[par], 16)
            for i in range(2):
                fetch(i, i, 0, True)
            rounds(sp, 2, PAIRS - 2, fetch)

        def pair(arr, i):
            return arr[:, bass.ds(i * PT, PT), :]

        def pool_norm(pool):
            s = LNS[0]

            def apply(i, par, use):
                hold(pool, s.rs_made, i + 1)
                hold(pool, s.xn_kept, i + 1)
                hold(pool, s.xn_turned, i + 1)
                n = GT - DVE_TILES
                out = XN_ST[par][:, DVE_TILES:GT, :]
                of_rows = lambda k: SM[par][:, k, DVE_TILES:GT].unsqueeze(2).to_broadcast([P, n, D])
                x = X[:, bass.ds((use + par * (G // 2)) * GT + DVE_TILES, n), :]
                pool.tensor_tensor(out, x, of_rows(0), ALU.subtract).then_inc(xp_made, 1)
                hold(pool, xp_made, 2 * i + 1)
                pool.tensor_tensor(out, out, of_rows(7), ALU.mult).then_inc(xp_made, 1)
            rounds(pool, 0, G, apply, turns=2)

        def pool_merge(pool):
            def add(i, par, use):
                hold(pool, got[par], 16 * (use + 1))
                pool.tensor_tensor(M_Y[par], M_Y[par], pair(XN, i), ALU.add).then_inc(CB[0].u_made, 1)

            def result(i, par):
                hold(pool, CB[0].post_steps, i + 1)
                pool.tensor_tensor(pair(X, i), pair(X, i), M_W[par], ALU.add).then_inc(CB[0].x_made, 1)

            def body(i, par, use):
                result(i - 1, 1 - par)
                add(i + 2, par, use + 1)
            add(0, 0, 0)
            add(1, 1, 0)
            add(2, 0, 1)
            body(1, 1, 0)
            rounds(pool, 2, PAIRS - 4, body)
            for i in range(PAIRS - 3, PAIRS):
                result(i, i % 2)

        def pe_norm(pe, la):
            s = LNS[la]
            router = GWT[:] if la else COLS[:, C_CENT:C_CENT + E]
            norm, turned, n = (M_N, M_T, PT) if la else (XN_ST, XT_ST, GT)
            steps, banks = NT // n, n // GT
            pe.sem_inc(s.xn_turned, CREDIT)
            pe.sem_inc(s.logits_made, CREDIT)

            def turn(i, par):
                pe.wait_ge(s.xn_made, i + 1)
                if la == 0:
                    pe.wait_ge(xp_made, 2 * i + 2)
                pe.wait_ge(s.xt_made, i + 1)
                for j in range(n):
                    last = pe.transpose(PS[:, banks * par + j // GT, j % GT * P:(j % GT + 1) * P],
                                        norm[par][:, j, :], IDENT[:])
                last.then_inc(s.xn_turned, 1)

            def logits(i, par):
                pe.wait_ge(s.xt_made, i + CREDIT + 1)
                pe.wait_ge(s.lg_kept, i + 1)
                for j in range(n):
                    last = pe.matmul(PS[:, 4 + par, j * E:(j + 1) * E], turned[par][:, j, :], router,
                                     start=True, stop=True)
                last.then_inc(s.logits_made, 1)

            def body(i, par, use):
                turn(i, par)
                logits(i - 1, 1 - par)
            turn(0, 0)
            rounds(pe, 1, steps - 2, body)
            body(steps - 1, 1, steps // 2 - 1)
            logits(steps - 1, 1)

        def pe_ranks(pe, la):
            r = RT[la]
            pe.wait_ge(r.onehot_made, 1)
            oh = RA.rearrange("p t e -> p (t e)")
            pe.matmul(PS[:, 4, :], UPPER[:], oh, start=True, stop=True)
            pe.matmul(PS[:, 5, :], ONES[:], oh, start=True, stop=True).then_inc(r.ranks_made, 1)

        def pe_linear_attention(pe):
            xs_in = (AT.xs_in0, AT.xs_in1)
            pe.sem_inc(AT.turned, CREDIT)
            pe.sem_inc(AT.s_made, CREDIT)

            def turn(g, par, use):
                pe.wait_ge(xs_in[par], 16 * (use + 1))
                pe.wait_ge(AT.xt_made, g)
                for j in range(GT):
                    last = pe.transpose(PS[:, 0, j * P:(j + 1) * P], A_XS[par][:, j, :], IDENT[:])
                last.then_inc(AT.turned, 1)

            def project(g, par):
                pe.wait_ge(AT.xt_made, g + 1)
                pe.wait_ge(AT.phi_made, g)
                pe.wait_ge(AT.v_made, g)
                for j in range(GT):
                    pe.matmul(PS[:, 2 + j // 2, (j % 2) * 2 * D:(j % 2 + 1) * 2 * D], A_XT[par][:, j, :],
                              WA[:, 1:3, :].rearrange("p a d -> p (a d)"), start=True, stop=True)
                pe.matmul(PS[:, 1, :], WA[:, 0, :], A_XT[par].rearrange("p a b -> p (a b)"),
                          start=True, stop=True).then_inc(AT.qkv_made, 1)

            def sums(g, par):
                pe.wait_ge(AT.phi_made, g + 1)
                pe.wait_ge(AT.v_made, g + 1)
                pe.wait_ge(AT.masked, g)
                for s in range(2):
                    for h in range(2):
                        last = pe.matmul(PS[:, 4, s * 256:s * 256 + D + HEADS], A_KF[par][:, 2 * s + h, :],
                                         A_VA[par][:, 2 * s + h, :], start=(h == 0), stop=(h == 1))
                last.then_inc(AT.aug_made, 1)

            def apply(g, par):
                pe.wait_ge(AT.masked, g + 1)
                pe.wait_ge(AT.out_made, g)
                for j in range(GT):
                    last = pe.matmul(A_ND[:, j, 0:D + HEADS], A_QF[par][:, j * P:(j + 1) * P],
                                     A_M[:, j // 2, :], start=True, stop=True)
                last.then_inc(AT.num_made, 1)

            def turn_back(g):
                pe.wait_ge(AT.out_made, g + 1)
                pe.wait_ge(AT.s_kept, g)
                for j in range(GT):
                    last = pe.transpose(PS[:, 7, j * P:(j + 1) * P], A_O[:, j, :], IDENT[:])
                last.then_inc(AT.o_turned, 1)

            def final(g):
                pe.wait_ge(AT.ot_kept, g + 1)
                for j in range(GT):
                    last = pe.matmul(PS[:, 7, j * D:(j + 1) * D], A_OT[:, j * P:(j + 1) * P], WA[:, 3, :],
                                     start=True, stop=True)
                last.then_inc(AT.s_made, 1)

            def body(g, par, use, first=False, left=2):
                if left > 0:
                    project(g + 1, 1 - par)
                if first:
                    pe.wait_ge(ranks_kept, 1)
                sums(g, par)
                if not first:
                    turn_back(g - 1)
                if left > 1:
                    turn(g + 2, par, use + 1)
                apply(g, par)
                if not first:
                    final(g - 1)
            turn(0, 0, 0)
            project(0, 0)
            turn(1, 1, 0)
            pe_ranks(pe, 0)
            body(0, 0, 0, first=True)
            body(1, 1, 0)
            rounds(pe, 2, G - 4, body, turns=2)
            body(G - 2, 0, G // 2 - 1, left=1)
            body(G - 1, 1, G // 2 - 1, left=0)
            turn_back(G - 1)
            final(G - 1)

        def pe_experts(pe, la):
            f, n = FF[la], TILES[la]
            pe.sem_inc(f.turned, CREDIT)
            pe.sem_inc(f.h_made, CREDIT)
            pe.sem_inc(f.y_made, CREDIT)
            loads = LOADS_BEFORE[la]

            def turn(t, q, use):
                par = q % 2
                pe.wait_ge(rows_in[q], 16 * (loads[q] + use + 1))
                pe.wait_ge(f.xf_made, t + 1)
                for h in range(HALVES):
                    last = pe.transpose(PS[:, par, h * P:(h + 1) * P], F_D[q][:, h, 0:D], IDENT[:])
                last.then_inc(f.turned, 1)

            def hidden(t, q, use):
                par = q % 2
                pe.wait_ge(w_in[q], 32 * (loads[q] + use + 1))
                pe.wait_ge(f.xf_made, t + CREDIT + 1)
                pe.wait_ge(f.hid_made, t + 1)
                for c in range(FC):
                    last = pe.matmul(PS[:, 2 + 2 * par + c // 2, (c % 2) * SLOT:(c % 2 + 1) * SLOT],
                                     F_W1[q][:, c * P:(c + 1) * P], F_X[par], start=True, stop=True)
                last.then_inc(f.h_made, 1)

            def result(t, q, use):
                par = q % 2
                pe.wait_ge(f.hid_made, t + CREDIT + 1)
                pe.wait_ge(f.y_kept, t + 1)
                for h in range(HALVES):
                    for c in range(FC):
                        last = pe.matmul(PS[:, 6 + par, h * D:(h + 1) * D], F_H[par][:, c, h * P:(h + 1) * P],
                                         F_W2[q][:, c, :], start=(c == 0), stop=(c == FC - 1))
                last.then_inc(f.y_made, 1)

            def body(t, q, use):
                turn(t + 1, (q + 1) % WB, use + (q + 1) // WB)
                hidden(t, q, use)
                result(t - 1, (q - 1) % WB, use + (q - 1) // WB)
            turn(0, 0, 0)
            turn(1, 1, 0)
            hidden(0, 0, 0)
            tile_rounds(pe, 1, n - 1, body)
            hidden(n - 1, (n - 1) % WB, (n - 1) // WB)
            for t in (n - 2, n - 1):
                result(t, t % WB, t // WB)

        def pe_recurrence(pe):
            xs_in = (RW.xs_in0, RW.xs_in1)
            pe.sem_inc(RW.turned, CREDIT)

            def turn(g, par, use):
                pe.wait_ge(xs_in[par], 16 * (use + 1))
                pe.wait_ge(RW.xt_made, g)
                if not (isinstance(g, int) and g < 2):
                    pe.wait_ge(RW.g_kept, g - 1)
                for j in range(GT):
                    last = pe.transpose(PS[:, 0, j * P:(j + 1) * P], R_XS[par][:, j, :], IDENT[:])
                last.then_inc(RW.turned, 1)

            def project_kvr(g, first=False):
                pe.wait_ge(RW.mixed, g + 1)
                pe.wait_ge(RW.r_kept, g)
                if not first:
                    pe.wait_ge(RW.ya_made, g - 2)
                    pe.wait_ge(RW.s_kept, g - 3 + CREDIT)
                for i in range(3):
                    for j in range(GT):
                        last = pe.matmul(PS[:, 1 + i, j * D:(j + 1) * D], R_MIX[:, i, j * P:(j + 1) * P],
                                         WT[:, i, :], start=True, stop=True)
                    if i == 1:
                        last.then_inc(RW.kv_proj, 1)
                last.then_inc(RW.r_proj, 1)

            def project_g(g):
                pe.wait_ge(RW.xt_made, g + 2 if not isinstance(g, int) or g + 2 <= G else G)
                pe.matmul(PS[:, 0, :], WT[:, 3, :], R_MIX[:, 3, :], start=True, stop=True).then_inc(RW.g_made, 1)

            def chunk(g, par, c):
                if c == 0:
                    pe.wait_ge(RW.kv_made, g + 1)
                pe.wait_ge(RW.prod_made, 4 * g + c + 1)
                for h in range(4):
                    kv = KV[par].rearrange("p (h t q) -> p h t q", t=GT, q=64)[:, 4 * c + h, :, :]
                    ps = PS[:, 4 + 2 * (c % 2) + h // 2, (h % 2) * 256:(h % 2 + 1) * 256]
                    pv = ps.rearrange("p (t q) -> p t q", q=64)
                    pe.matmul(pv, TOEP[:, 4 * c + h, 0:P], kv, start=True, stop=False)
                    last = pe.matmul(pv[:, 1::2, :], TOEP[:, 4 * c + h, P:2 * P], kv[:, 0::2, :],
                                     start=False, stop=True)
                last.then_inc(RW.chunk_steps, 1)

            def turn_back(g):
                pe.wait_ge(RW.yn_made, g + 1)
                pe.wait_ge(RW.k_kept, g + 3 if not isinstance(g, int) or g + 3 <= G else G)
                for j in range(GT):
                    last = pe.transpose(PS[:, 1, j * P:(j + 1) * P], R_YN[:, j, :], IDENT[:])
                last.then_inc(RW.yt_made, 1)

            def final(g):
                pe.wait_ge(RW.yg_made, g + 1)
                pe.wait_ge(RW.v_kept, g + 4 if not isinstance(g, int) or g + 4 <= G else G)
                for j in range(GT):
                    last = pe.matmul(PS[:, 2, j * D:(j + 1) * D], R_YG[:, j * P:(j + 1) * P], WT[:, 4, :],
                                     start=True, stop=True)
                last.then_inc(RW.s_made, 1)

            def body(g, par, use, has=(1, 1, 1, 1)):
                chunk(g, par, 0)
                chunk(g, par, 1)
                if has[2] and has[1]:
                    project_kvr(g + 1, not has[0])
                chunk(g, par, 2)
                if has[0]:
                    final(g - 2)
                if has[3]:
                    turn(g + 2, par, use + 1)
                chunk(g, par, 3)
                if has[2]:
                    project_g(g + 1)
                if has[1]:
                    turn_back(g - 1)
            turn(0, 0, 0)
            turn(1, 1, 0)
            pe_ranks(pe, 1)
            project_kvr(0, True)
            project_g(0)
            pe.wait_ge(ranks_kept, 2)
            project_kvr(1, True)
            all_groups(pe, body)
            final(G - 2)
            turn_back(G - 1)
            final(G - 1)

        def all_groups(eng, body):
            body(0, 0, 0, (0, 0, 1, 1))
            body(1, 1, 0, (0, 1, 1, 1))
            rounds(eng, 2, G - 4, body, turns=2)
            body(G - 2, (G - 2) % 2, (G - 2) // 2, (1, 1, 1, 0))
            body(G - 1, (G - 1) % 2, (G - 1) // 2, (1, 1, 0, 0))

        def act_norm(act):
            s = LNS[0]
            act.sem_inc(s.xn_kept, CREDIT)
            act.sem_inc(s.xt_made, CREDIT)
            act.sem_inc(xn2_kept, CREDIT)

            def root(i, par, cols):
                act.wait_ge(s.var_made, i + 1)
                nc.scalar.activation(SM[par][:, 6, cols], SM[par][:, 5, cols], ACT.Sqrt).then_inc(s.sd_made, 1)

            def keep(i, par, use):
                hold(act, s.xn_made, i + 1)
                hold(act, xp_made, 2 * i + 2)
                nc.scalar.activation(grp(XN, use + par * (G // 2)), XN_ST[par], ACT.Copy).then_inc(s.xn_kept, 1)
                act.wait_ge(s.xn_turned, i + CREDIT + 1)
                act.wait_ge(s.logits_made, i + 1)
                nc.scalar.activation(XT_ST[par].rearrange("p a b -> p (a b)"), PS[:, par, :], ACT.Copy
                                     ).then_inc(s.xt_made, 1)

            def second(i, par, use):
                act.wait_ge(nb_made, i - 1)
                for j in range(GT):
                    last = nc.scalar.activation(
                        row(XN2, use - 1 + par * (G // 2), j), row(XN, use - 1 + par * (G // 2), j), ACT.Identity,
                        bias=SM[par][:, 8, GT + j:GT + j + 1], scale=SM[par][:, 7, GT + j:GT + j + 1])
                last.then_inc(xn2_kept, 1)

            def body(i, par, use):
                root(i, par, BOTH_COLS)
                second(i - 1, 1 - par, use + par - 1)
                keep(i - 1, 1 - par, use + par - 1)
            root(0, 0, X_COLS)
            act.wait_ge(cols_turned, 1)
            nc.scalar.activation(COLS[:], PS[:, 0, 0:P], ACT.Copy).then_inc(cols_kept, 1)
            root(1, 1, X_COLS)
            keep(0, 0, 0)
            root(2, 0, BOTH_COLS)
            keep(1, 1, 0)
            rounds(act, 3, G - 4, body, turns=2)
            body(G - 1, 1, G // 2 - 1)
            root(G, 0, N_COLS)
            second(G - 1, 1, G // 2 - 1)
            keep(G - 1, 1, G // 2 - 1)
            root(G + 1, 1, N_COLS)
            second(G, 0, G // 2)
            second(G + 1, 1, G // 2)

        def act_merge(act):
            b, s = CB[0], LNS[1]
            act.sem_inc(b.x_made, CREDIT)
            act.sem_inc(s.xn_kept, CREDIT)
            act.sem_inc(s.xt_made, CREDIT)

            def silu(i, par):
                act.wait_ge(b.u_made, i + 1)
                act.wait_ge(b.x_made, i + 1)
                nc.scalar.activation(M_W[par], M_Y[par], ACT.Silu).then_inc(b.silu_made, 1)

            def root(i, par):
                act.wait_ge(s.var_made, i + 1)
                nc.scalar.activation(M_SM[par][:, 6, :], M_SM[par][:, 5, :], ACT.Sqrt).then_inc(s.sd_made, 1)

            def keep(i, par):
                hold(act, s.xn_made, i + 1)
                nc.scalar.activation(pair(XN, i), M_N[par], ACT.Copy).then_inc(s.xn_kept, 1)
                act.wait_ge(s.xn_turned, i + CREDIT + 1)
                act.wait_ge(s.logits_made, i + 1)
                nc.scalar.activation(M_T[par].rearrange("p (b a) c -> p b (a c)", b=2),
                                     PS[:, 2 * par:2 * par + 2, :], ACT.Copy).then_inc(s.xt_made, 1)

            def body(i, par, use):
                silu(i + 1, 1 - par)
                keep(i - 3, 1 - par)
                root(i - 1, 1 - par)
            silu(0, 0)
            silu(1, 1)
            for i in (1, 2):
                silu(i + 1, (i + 1) % 2)
                root(i - 1, (i - 1) % 2)
            rounds(act, 3, PAIRS - 4, body)
            keep(PAIRS - 4, 0)
            root(PAIRS - 2, 0)
            keep(PAIRS - 3, 1)
            root(PAIRS - 1, 1)
            keep(PAIRS - 2, 0)
            keep(PAIRS - 1, 1)

        def act_linear_attention(act):
            def keep_turned(g, par):
                act.wait_ge(AT.turned, g + CREDIT + 1)
                nc.scalar.activation(A_XT[par].rearrange("p a b -> p (a b)"), PS[:, 0, :], ACT.Copy
                                     ).then_inc(AT.xt_made, 1)

            def exps(g, par):
                act.wait_ge(AT.qkv_made, g + 1)
                kv = PS[:, 2:4, :].rearrange("p b (j c d) -> p (b j) c d", c=2, d=D)
                nc.scalar.activation(A_E, kv[:, :, 0, :], ACT.Exp).then_inc(AT.ek_made, 1)
                nc.scalar.activation(A_VA[par][:, :, 0:D], kv[:, :, 1, :], ACT.Copy).then_inc(AT.v_made, 1)
                nc.scalar.activation(A_E2.rearrange("p a b -> p (a b)"), PS[:, 1, :], ACT.Exp
                                     ).then_inc(AT.eq_made, 1)

            def keep_out(g):
                act.wait_ge(AT.o_turned, g + 1)
                nc.scalar.activation(A_OT, PS[:, 7, :], ACT.Copy).then_inc(AT.ot_kept, 1)

            def keep_s(g):
                hold(act, AT.s_made, g + CREDIT + 1)
                nc.scalar.activation(grp(S, g), PS[:, 7, :].rearrange("p (a d) -> p a d", d=D), ACT.Copy
                                     ).then_inc(AT.s_kept, 1)

            def body(g, par, use, first=False, left=2):
                if left > 0:
                    exps(g + 1, 1 - par)
                if not first:
                    keep_out(g - 1)
                if left > 1:
                    keep_turned(g + 2, par)
                if not first:
                    keep_s(g - 1)

            def decays(heads):
                act.wait_ge(lw_made, 2)
                for h in heads:
                    nc.scalar.activation(TOEP[:, h, :], EXPO, ACT.Exp, scale=LW[:, h:h + 1]).then_inc(exp_made, 1)
            keep_turned(0, 0)
            exps(0, 0)
            keep_turned(1, 1)
            decays(range(12))
            act.wait_ge(zero_filled[1], 16 * FILLS[1])
            body(0, 0, 0, first=True)
            decays(range(12, HEADS))
            body(1, 1, 0)
            rounds(act, 2, G - 4, body, turns=2)
            body(G - 2, 0, G // 2 - 1, left=1)
            body(G - 1, 1, G // 2 - 1, left=0)
            keep_out(G - 1)
            keep_s(G - 1)

        def act_experts(act, la, func):
            f = FF[la]
            act.sem_inc(f.hid_made, CREDIT)

            def body(t, q, use):
                par = q % 2
                act.wait_ge(f.h_made, t + CREDIT + 1)
                act.wait_ge(f.par_made, t + 1)
                act.wait_ge(f.y_made, t + 1)
                for c in range(FC):
                    last = nc.scalar.activation(
                        F_H[par][:, c, :], PS[:, 2 + 2 * par + c // 2, (c % 2) * SLOT:(c % 2 + 1) * SLOT],
                        func, bias=F_PAR[par][:, c:c + 1])
                last.then_inc(f.hid_made, 1)
            tile_rounds(act, 0, TILES[la], body)

        def act_combine(act):
            b = CB[1]

            def body(g, par, use):
                act.wait_ge(b.u_made, g + 1)
                act.wait_ge(b.x_made, g + 1)
                nc.scalar.activation(C_S[par], C_U[par], ACT.Silu).then_inc(b.silu_made, 1)
            rounds(act, 0, G, body)

        def act_recurrence(act):
            def keep_turned(g, par):
                act.wait_ge(RW.turned, g + CREDIT + 1)
                nc.scalar.activation(R_XT[par][:, :, 1:L + 1], PS[:, 0, :].rearrange("p (s t) -> p s t", s=2),
                                     ACT.Copy).then_inc(RW.xt_made, 1)

            def keep_kvr(g, par):
                act.wait_ge(RW.kv_proj, g + 1)
                act.wait_ge(RW.kv_made, g)
                for ps, dst, s in ((1, R_K, RW.k_kept), (2, R_V, RW.v_kept), (3, R_R[par], RW.r_kept)):
                    if ps == 3:
                        act.wait_ge(RW.r_proj, g + 1)
                    nc.scalar.activation(dst.rearrange("p (h t n) -> p t h n", t=GT, n=HN),
                                         PS[:, ps, :].rearrange("p (t h n) -> p t h n", t=GT, n=HN),
                                         ACT.Copy).then_inc(s, 1)

            def gates(g, par, first=False):
                act.wait_ge(RW.g_made, g + 1)
                if not first:
                    act.wait_ge(RW.yg_made, g - 1)
                nc.scalar.activation(R_G[par], PS[:, 0, :], ACT.Silu).then_inc(RW.g_kept, 1)

            def squares(g):
                act.wait_ge(RW.sq_in, g + 1)
                nc.scalar.activation(R_SQ, R_YC, ACT.Square).then_inc(RW.sq_made, 1)

            def roots(g):
                act.wait_ge(RW.sd_in, g + 1)
                nc.scalar.activation(R_SM[:, 2, :], R_SM[:, 1, :], ACT.Sqrt, scale=1.0 / HN,
                                     bias=EPSC[:, 2:3]).then_inc(RW.sd_made, 1)

            def affine(g):
                act.wait_ge(RW.yt_made, g + 1)
                nc.scalar.activation(R_YA, PS[:, 1, :], ACT.Identity, scale=COLS[:, C_GNG:C_GNG + 1],
                                     bias=COLS[:, C_GNB:C_GNB + 1]).then_inc(RW.ya_made, 1)

            def keep_s(g):
                hold(act, RW.s_made, g + 1)
                nc.scalar.activation(grp(S, g), PS[:, 2, :].rearrange("p (a d) -> p a d", d=D), ACT.Copy
                                     ).then_inc(RW.s_kept, 1)

            def body(g, par, use, has=(1, 1, 1, 1)):
                if has[2]:
                    keep_kvr(g + 1, 1 - par)
                if has[1]:
                    squares(g - 1)
                    roots(g - 1)
                if has[0]:
                    keep_s(g - 2)
                if has[3]:
                    keep_turned(g + 2, par)
                if has[1]:
                    affine(g - 1)
                if has[2]:
                    gates(g + 1, 1 - par, not has[1])
            act.sem_inc(RW.s_kept, CREDIT)
            keep_turned(0, 0)
            keep_turned(1, 1)
            act.wait_ge(RT[1].w_exp, 1)
            nc.scalar.activation(WTS[:, 2, :], WTS[:, 2, :], ACT.Exp).then_inc(RT[1].w_exp, 1)
            keep_kvr(0, 0)
            gates(0, 0, True)
            all_groups(act, body)
            keep_s(G - 2)
            squares(G - 1)
            roots(G - 1)
            affine(G - 1)
            keep_s(G - 1)

        def variance_stages(v, s, k, st, sm):
            def sums():
                v.wait_ge(s.ln_steps, k.all())
                v.tensor_tensor(sm[:, 0, :], st[:, :, 1], st[:, :, 4], ALU.add).then_inc(s.ln_steps, k.one())
                v.tensor_tensor(sm[:, 1, :], st[:, :, 1], st[:, :, 4], ALU.subtract)
                v.tensor_tensor(sm[:, 2, :], st[:, :, 2], st[:, :, 5], ALU.add).then_inc(s.ln_steps, k.one())

            def squares():
                v.wait_ge(s.ln_steps, k.all())
                v.scalar_tensor_tensor(out=sm[:, 3, :], in0=sm[:, 1, :], scalar=D / 4.0, in1=sm[:, 1, :],
                                       op0=ALU.mult, op1=ALU.mult).then_inc(s.ln_steps, k.one())
                v.tensor_scalar(sm[:, 0, :], sm[:, 0, :], 0.5, None, ALU.mult).then_inc(s.ln_steps, k.one())

            def both():
                v.wait_ge(s.ln_steps, k.all())
                v.tensor_tensor(sm[:, 4, :], sm[:, 2, :], sm[:, 3, :], ALU.add).then_inc(s.ln_steps, k.one())

            def variance():
                v.wait_ge(s.ln_steps, k.all())
                v.tensor_scalar(sm[:, 5, :], sm[:, 4, :], 1.0 / D, LN_EPS, ALU.mult, ALU.add
                                ).then_inc(s.var_made, 1)
            return sums, squares, both, variance

        def dve_norm(v):
            s = LNS[0]
            k = Steps(s.ln_steps, 6)
            v.sem_inc(s.lg_kept, CREDIT)

            def moments(i, par, use, cols):
                k.at(i)
                if not (isinstance(i, int) and i < 2):
                    hold(v, s.xn_made, i - 1)
                    hold(v, xp_made, 2 * i - 2)
                if cols.start == 0:
                    v.wait_ge(x_in[par], 16 * (use + 1))
                    for j in range(GT):
                        last = v.bn_stats(ST[par][:, j, :], row(X, use + par * (G // 2), j))
                if cols.stop == 2 * GT:
                    for j in range(GT):
                        last = v.bn_stats(ST[par][:, GT + j, :], XN_ST[par][:, j, :])
                last.then_inc(s.ln_steps, k.one())

            def inverses(i, par, cols):
                if not (isinstance(i, int) and i < 2):
                    hold(v, xn2_kept, CREDIT + i - 3)
                v.wait_ge(s.sd_made, i + 1)
                v.reciprocal(SM[par][:, 7, cols], SM[par][:, 6, cols]).then_inc(s.rs_made, 1)

            def second_bias(i, par):
                hold(v, s.rs_made, i + 1)
                v.scalar_tensor_tensor(out=SM[par][:, 8, N_COLS], in0=SM[par][:, 0, N_COLS], scalar=-1.0,
                                       in1=SM[par][:, 7, N_COLS], op0=ALU.mult, op1=ALU.mult
                                       ).then_inc(nb_made, 1)

            def apply(i, par, use, j):
                if j == 0:
                    hold(v, s.rs_made, i + 1)
                    hold(v, s.xn_kept, i + 1)
                    hold(v, s.xn_turned, i + 1)
                ins = v.tensor_scalar(XN_ST[par][:, j, :], row(X, use + par * (G // 2), j),
                                      SM[par][:, 0, j:j + 1], SM[par][:, 7, j:j + 1], ALU.subtract, ALU.mult)
                if j == DVE_TILES - 1:
                    ins.then_inc(s.xn_made, 1)

            def step(of_stats=None, of_norm=None):
                stages = (None,) * GT
                if of_stats:
                    i, par, use, cols = of_stats
                    moments(i, par, use, cols)
                    stages = variance_stages(v, s, k, ST[par][:, cols, :], SM[par][:, :, cols])
                if of_norm:
                    i, par, use, cols = of_norm
                    inverses(i, par, cols)
                for j in range(GT):
                    if stages[j]:
                        stages[j]()
                    if of_norm and j == 0 and cols.stop == 2 * GT:
                        second_bias(i, par)
                    if of_norm and cols.start == 0 and j < DVE_TILES:
                        apply(i, par, use, j)

            def logits(i, par, use):
                hold(v, s.logits_made, i + CREDIT + 1)
                v.tensor_copy(grp(LG, use + par * (G // 2)),
                              PS[:, 4 + par, 0:GT * E].rearrange("p (t e) -> p t e", e=E)).then_inc(s.lg_kept, 1)

            def body(i, par, use):
                step((i, par, use, BOTH_COLS), (i - 1, 1 - par, use + par - 1, BOTH_COLS))
                logits(i - 3, 1 - par, use + par - 2)
            half = G // 2
            step((0, 0, 0, X_COLS))
            step((1, 1, 0, X_COLS), (0, 0, 0, X_COLS))
            step((2, 0, 1, BOTH_COLS), (1, 1, 0, X_COLS))
            rounds(v, 3, G - 4, body, turns=2)
            body(G - 1, 1, half - 1)
            step((G, 0, half, N_COLS), (G - 1, 1, half - 1, BOTH_COLS))
            step((G + 1, 1, half, N_COLS), (G, 0, half, N_COLS))
            step(None, (G + 1, 1, half, N_COLS))
            for i in (G - 3, G - 2, G - 1):
                logits(i, i % 2, i // 2)

        def dve_merge(v, choose):
            b, s = CB[0], LNS[1]
            k = Steps(s.ln_steps, 6)
            v.sem_inc(s.lg_kept, CREDIT)

            def gated(i, par):
                hold(v, b.silu_made, i + 1)
                v.tensor_tensor(M_W[par], M_W[par], pair(S, i), ALU.mult).then_inc(b.post_steps, 1)

            def moments(i, par):
                k.at(i)
                if not (isinstance(i, int) and i < 2):
                    hold(v, s.xn_made, i - 1)
                hold(v, b.x_made, i + CREDIT + 1)
                for j in range(PT):
                    last = v.bn_stats(M_ST[par][:, j, :], row(X, 2 * i, j))
                last.then_inc(s.ln_steps, k.one())

            def inverses(i, par):
                v.wait_ge(s.sd_made, i + 1)
                v.reciprocal(M_SM[par][:, 7, :], M_SM[par][:, 6, :]).then_inc(s.rs_made, 1)

            def apply(i, par, j):
                if j == 0:
                    hold(v, s.rs_made, i + 1)
                    hold(v, s.xn_kept, i + 1)
                    hold(v, s.xn_turned, i + 1)
                ins = v.tensor_scalar(M_N[par][:, j, :], row(X, 2 * i, j), M_SM[par][:, 0, j:j + 1],
                                      M_SM[par][:, 7, j:j + 1], ALU.subtract, ALU.mult)
                if j == PT - 1:
                    ins.then_inc(s.xn_made, 1)

            def logits(i, par):
                hold(v, s.logits_made, i + CREDIT + 1)
                v.tensor_tensor(pair(LG, i), PS[:, 4 + par, 0:PT * E].rearrange("p (t e) -> p t e", e=E),
                                GB[:].unsqueeze(1).to_broadcast([P, PT, E]), ALU.add).then_inc(s.lg_kept, 1)

            def body(i, par, use, has=(1, 1, 1, 1)):
                other = 1 - par
                stages = (None,) * 4
                if has[0]:
                    gated(i, par)
                if has[1]:
                    moments(i - 1, other)
                    stages = variance_stages(v, s, k, M_ST[other], M_SM[other])
                if has[2]:
                    inverses(i - 2, par)
                for j in range(4):
                    if stages[j]:
                        stages[j]()
                    if has[2]:
                        apply(i - 2, par, 2 * j)
                        apply(i - 2, par, 2 * j + 1)
                if has[3]:
                    logits(i - 4, par)
            body(0, 0, 0, (1, 0, 0, 0))
            body(1, 1, 0, (1, 1, 0, 0))
            body(2, 0, 1, (1, 1, 1, 0))
            body(3, 1, 1, (1, 1, 1, 0))
            rounds(v, 4, PAIRS - 4, body)
            body(PAIRS, 0, 0, (0, 1, 1, 1))
            body(PAIRS + 1, 1, 0, (0, 0, 1, 1))
            v.wait_ge(s.lg_kept, CREDIT + CHOSEN_EARLY // PT)
            choose(0, CHOSEN_EARLY)
            logits(PAIRS - 2, 0)
            logits(PAIRS - 1, 1)

        def dve_route(v, la):
            c, r = CHOICES[la], RT[la]
            k = Steps(r.rt_steps)

            def step(ins):
                ins.then_inc(r.rt_steps, k.one())
                v.wait_ge(r.rt_steps, k.all())

            def choose(first, n):
                cut = lambda ap: ap[:, first:first + n]
                ie = IE8[:].unsqueeze(1).to_broadcast([P, n, E])
                wide = lambda ap: cut(ap).unsqueeze(2).to_broadcast([P, n, E])
                for i in range(c):
                    step(v.tensor_reduce(cut(MX[:, i, :]), cut(LG), AX.X, ALU.max))
                    step(v.tensor_tensor(cut(RA), cut(LG), wide(MX[:, i, :]), ALU.is_equal))
                    step(v.scalar_tensor_tensor(out=cut(RB), in0=cut(RA), scalar=float(-E), in1=ie,
                                                op0=ALU.mult, op1=ALU.add))
                    step(v.tensor_reduce(cut(IDX), cut(RB), AX.X, ALU.min))
                    step(v.tensor_scalar(cut(IDX), cut(IDX), float(E), None, ALU.add))
                    if i == 0:
                        v.tensor_scalar(cut(TAG[:, :, 1]), cut(IDX), float(E), None, ALU.add)
                    step(v.tensor_tensor(cut(OH[i]), ie, wide(IDX), ALU.is_equal))
                    if i + 1 < c:
                        step(v.scalar_tensor_tensor(out=cut(LG), in0=cut(OH[i]), scalar=-HUGE, in1=cut(LG),
                                                    op0=ALU.mult, op1=ALU.add))

            def chosen():
                if c == 1:
                    v.tensor_copy(RA, OH[0]).then_inc(r.onehot_made, 1)
                else:
                    v.tensor_tensor(RA, OH[0], OH[1], ALU.add).then_inc(r.onehot_made, 1)
                    v.tensor_tensor(WTS[:, 2, :], MX[:, 1, :], MX[:, 0, :], ALU.subtract).then_inc(r.w_exp, 1)
                step(v.memset(RONE, 1.0))

            def weights():
                v.wait_ge(r.w_exp, 2)
                step(v.tensor_scalar(WTS[:, 0, :], WTS[:, 2, :], 1.0, None, ALU.add))
                step(v.reciprocal(WTS[:, 0, :], WTS[:, 0, :]))
                step(v.tensor_tensor(WTS[:, 1, :], WTS[:, 2, :], WTS[:, 0, :], ALU.mult))

            def keep_ranks():
                v.wait_ge(r.ranks_made, 1)
                v.tensor_copy(RD.rearrange("p t e -> p (t e)"), PS[:, 4, :])
                ins = v.tensor_copy(RB.rearrange("p t e -> p (t e)"), PS[:, 5, :])
                ins.then_inc(ranks_kept, 1)
                v.wait_ge(ranks_kept, la + 1)

            def running_totals():
                for e in range(E):
                    last = v.tensor_tensor_scan(RC[:, :, e], RONE, RB[:, :, e], 0.0, ALU.mult, ALU.add)
                step(last)

            def begins():
                step(v.tensor_copy(CNT[:, 0, :], RC[:, NT - 1, :]))
                step(v.tensor_tensor(RTH, CNT[:, 0, :].unsqueeze(2).to_broadcast([P, E, THR]),
                                     ITHR[:].unsqueeze(1).to_broadcast([P, E, THR]), ALU.is_gt))
                step(v.tensor_reduce(CNT[:, 1, :], RTH, AX.X, ALU.add))
                step(v.tensor_tensor_scan(CNT[:, 2, :], RONE[:, 0:E], CNT[:, 1, :], 0.0, ALU.mult, ALU.add))
                step(v.tensor_tensor(CNT[:, 3, :], CNT[:, 2, :], CNT[:, 1, :], ALU.subtract))
                step(v.tensor_scalar(CNT[:, 3, :], CNT[:, 3, :], float(SLOT), None, ALU.mult))

            def slots():
                step(v.tensor_tensor(RC, RC, RB, ALU.subtract))
                step(v.tensor_tensor(RC, RD, RC, ALU.add))
                step(v.tensor_tensor(RC, RC, CNT[:, 3, :].unsqueeze(1).to_broadcast([P, NT, E]), ALU.add))
                for i in range(c):
                    step(v.tensor_tensor(RD, RC, OH[i], ALU.mult))
                    step(v.tensor_reduce(POSF[:], RD, AX.X, ALU.add))
                    if i + 1 < c:
                        step(v.tensor_copy(POS[:, i, :], POSF[:]))
                    else:
                        v.tensor_copy(POS[:, i, :], POSF[:]).then_inc(slots_made, 1)

            def tiles():
                step(v.tensor_tensor(RTT, ITILE[:].unsqueeze(2).to_broadcast([P, MAXT, E]),
                                     CNT[:, 2, :].unsqueeze(1).to_broadcast([P, MAXT, E]), ALU.is_ge))
                step(v.tensor_reduce(TEF[:], RTT, AX.X, ALU.add))
                step(v.tensor_scalar(TEF[:], TEF[:], float(E - 1), None, ALU.min))
                step(v.tensor_copy(TE[:], TEF[:]))
            return choose, chosen, weights, keep_ranks, running_totals, begins, slots, tiles

        def dve_linear_attention(v):
            kp, ko = Steps(AT.phi_steps, 2), Steps(AT.out_steps, 2)
            for par in range(2):
                v.memset(A_VA[par][:, :, D:D + HEADS], 1.0)
            choose, chosen, _, keep_ranks, running_totals, begins, slots, tiles = dve_route(v, 0)
            choose(0, NT)
            chosen()

            def phi(g, par):
                kp.at(g)
                kv = PS[:, 2:4, :].rearrange("p b (j c d) -> p (b j) c d", c=2, d=D)
                v.wait_ge(AT.ek_made, g + 1)
                v.tensor_scalar(A_E, A_E, 1.0, None, ALU.min).then_inc(AT.phi_steps, kp.one())
                v.wait_ge(AT.eq_made, g + 1)
                v.tensor_scalar(A_E2, A_E2, 1.0, None, ALU.min).then_inc(AT.phi_steps, kp.one())
                v.wait_ge(AT.phi_steps, kp.all() - 1)
                v.scalar_tensor_tensor(out=A_KF[par], in0=kv[:, :, 0, :], scalar=0.0, in1=A_E,
                                       op0=ALU.max, op1=ALU.add)
                v.wait_ge(AT.phi_steps, kp.all())
                v.scalar_tensor_tensor(out=A_QF[par], in0=PS[:, 1, :], scalar=0.0,
                                       in1=A_E2.rearrange("p a b -> p (a b)"), op0=ALU.max, op1=ALU.add
                                       ).then_inc(AT.phi_made, 1)

            def mask(g):
                v.wait_ge(AT.aug_made, g + 1)
                v.tensor_tensor(A_M, PS[:, 4, :].rearrange("p (s c) -> p s c", s=2)[:, :, 0:D + HEADS],
                                BLOCK[:].unsqueeze(1).to_broadcast([P, 2, D + HEADS]), ALU.mult
                                ).then_inc(AT.masked, 1)

            def divide(g):
                ko.at(g)
                v.wait_ge(AT.num_made, g + 1)
                v.tensor_scalar(A_DD, A_DEN, DEN_EPS, None, ALU.add).then_inc(AT.out_steps, ko.one())
                v.wait_ge(AT.out_steps, ko.all())
                v.reciprocal(A_DD, A_DD).then_inc(AT.out_steps, ko.one())
                v.wait_ge(AT.out_steps, ko.all())
                v.tensor_tensor(A_O.rearrange("p t (h m) -> p t h m", m=HN),
                                A_NUM.rearrange("p t (h m) -> p t h m", m=HN),
                                A_DD.unsqueeze(3).to_broadcast([P, GT, HEADS, HN]), ALU.mult
                                ).then_inc(AT.out_made, 1)

            def body(g, par, use, final_group=False):
                mask(g)
                if not final_group:
                    phi(g + 1, 1 - par)
                divide(g)
            phi(0, 0)
            keep_ranks()
            body(0, 0, 0)
            running_totals()
            body(1, 1, 0)
            begins()
            body(2, 0, 1)
            slots()
            body(3, 1, 1)
            tiles()
            v.wait_ge(toep_cut, HEADS)
            for g in (4, 5):
                body(g, g % 2, g // 2)
                for h in range((g - 4) * HEADS // 2, (g - 3) * HEADS // 2):
                    v.scalar_tensor_tensor(out=TOEP[:, h, 0:P], in0=IDENT[:], scalar=TU[:, h:h + 1],
                                           in1=TOEP[:, h, 0:P], op0=ALU.mult, op1=ALU.add)
            rounds(v, 6, G - 8, body, turns=2)
            body(G - 2, 0, G // 2 - 1)
            body(G - 1, 1, G // 2 - 1, final_group=True)

        def dve_experts(v, la):
            f, n = FF[la], TILES[la]
            kd = Steps(f.dst_steps, 3 if la else 1)
            v.sem_inc(f.xf_made, CREDIT)
            v.sem_inc(f.y_kept, CREDIT)

            def destinations(t, q, use):
                kd.at(t)
                v.wait_ge(rows_in[q], 16 * (LOADS_BEFORE[la][q] + use + 1))
                if not (isinstance(t, int) and t < WB):
                    v.wait_ge((f.y_out0, f.y_out1)[q % 2], 16 * HALVES * (2 * use + q // 2 - 1))
                number, first = F_D[q][:, :, D], F_D[q][:, :, D + 1]
                if la == 0:
                    v.tensor_copy(DST[:, q, :], number).then_inc(f.dst_steps, kd.one())
                    return
                c = F_C[q % 2]
                v.tensor_tensor(c, first, TEF[:, bass.ds(t, 1)].to_broadcast([P, HALVES]), ALU.not_equal
                                ).then_inc(f.dst_steps, kd.one())
                v.wait_ge(f.dst_steps, kd.all())
                v.scalar_tensor_tensor(out=c, in0=c, scalar=float(TOK), in1=number, op0=ALU.mult, op1=ALU.add
                                       ).then_inc(f.dst_steps, kd.one())
                v.wait_ge(f.dst_steps, kd.all())
                v.tensor_copy(DST[:, q, :], c).then_inc(f.dst_steps, kd.one())

            def inputs(t, q, use):
                par = q % 2
                e = v.value_load(TE[0:1, bass.ds(t, 1)], min_val=0, max_val=E - 1)
                hold(v, f.hid_made, t + 1)
                if la == 0:
                    v.tensor_copy(F_PAR[par][:, FC:FC + 1], COLS[:, bass.ds(e + C_LNG, 1)])
                    v.tensor_copy(F_PAR[par][:, FC + 1:FC + 2], COLS[:, bass.ds(e + C_LNB, 1)])
                v.tensor_copy(F_PAR[par][:, 0:FC], COLS[:, bass.ds(e * FC + C_B1[la], FC)]
                              ).then_inc(f.par_made, 1)
                destinations(t, q, use)
                v.wait_ge(f.turned, t + CREDIT + 1)
                v.wait_ge(f.h_made, t + 1)
                v.wait_ge(f.par_made, t + 1)
                ps = PS[:, par, 0:SLOT]
                if la == 0:
                    v.tensor_scalar(F_X[par], ps, F_PAR[par][:, FC:FC + 1], F_PAR[par][:, FC + 1:FC + 2],
                                    ALU.mult, ALU.add).then_inc(f.xf_made, 1)
                else:
                    v.tensor_copy(F_X[par], ps).then_inc(f.xf_made, 1)
                return e

            def out_bias(e, t, par):
                if isinstance(t, int) and t == 0:
                    v.wait_ge(b2_in, 16 * (la + 1))
                hold(v, f.y_kept, t + 1)
                v.tensor_copy(F_B2[par], B2[:, bass.ds(e, 1), :].rearrange("p e d -> p (e d)")
                              ).then_inc(f.b2_made, 1)

            def result(t, q, use):
                par = q % 2
                v.wait_ge(f.y_made, t + CREDIT + 1)
                v.wait_ge(f.b2_made, t + 1)
                v.wait_ge(f.dst_steps, kd.per * (t + 1))
                if not (isinstance(t, int) and t < 2):
                    v.wait_ge((f.y_out0, f.y_out1)[par], 16 * HALVES * (2 * use + q // 2))
                ps = PS[:, 6 + par, 0:SLOT].rearrange("p (h d) -> p h d", d=D)
                v.tensor_tensor(F_Y[par], ps, F_B2[par].unsqueeze(1).to_broadcast([P, HALVES, D]), ALU.add
                                ).then_inc(f.y_kept, 1)

            def body(t, q, use):
                e = inputs(t + 1, (q + 1) % WB, use + (q + 1) // WB)
                result(t - 1, (q - 1) % WB, use + (q - 1) // WB)
                out_bias(e, t + 1, (q + 1) % 2)
            for t in range(2):
                out_bias(inputs(t, t, 0), t, t)
            tile_rounds(v, 1, n - 1, body)
            for t in (n - 2, n - 1):
                result(t, t % WB, t // WB)

        def dve_combine(v):
            b = CB[1]
            ku = Steps(b.u_steps, 1)
            v.sem_inc(b.x_made, CREDIT)

            def first_choice(g, q, use):
                ku.at(g)
                v.wait_ge(got[q], GOT_BEFORE[q] + 16 * CHOICES[1] * (use + 1))
                if not (isinstance(g, int) and g < 2):
                    hold(v, b.silu_made, g - 1)
                v.tensor_tensor(C_U[q % 2], C_Y[q][:, 0:GT, :], weight(0, g), ALU.mult
                                ).then_inc(b.u_steps, ku.one())

            def total(g, q):
                v.wait_ge(b.u_steps, ku.all())
                v.wait_ge(w1_made, g + 1)
                v.tensor_tensor(C_U[q % 2], C_U[q % 2], C_Y[q][:, GT:2 * GT, :], ALU.add).then_inc(b.u_made, 1)

            def gated(g, par):
                hold(v, b.silu_made, g + 1)
                if not (isinstance(g, int) and g < 2):
                    hold(v, b.x_made, CREDIT + g - 1)
                v.tensor_tensor(C_T[par], C_S[par], grp(S, g), ALU.mult).then_inc(b.post_steps, 1)

            def body(g, q, use, first=False, final_group=False):
                if not final_group:
                    first_choice(g, q, use)
                if not first:
                    gated(g - 1, (q - 1) % 2)
                if not final_group:
                    total(g, q)
            body(0, 0, 0, first=True)
            body(1, 1, 0)
            body(2, 2, 0)
            rounds(v, 3, G - YB, body, YB)
            body(G - 1, YB - 1, G // YB - 1)
            body(G, 0, G // YB, final_group=True)

        def dve_recurrence(v, route):
            kc = Steps(RW.gn_steps, 2)
            for par in range(2):
                last = v.memset(R_XT[par][:, :, 0:1], 0.0)
            last.then_inc(RW.pad_zeroed, 1)
            v.wait_ge(RW.pad_zeroed, 1)
            v.sem_inc(RW.prod_made, CREDIT)

            def differences(g, par):
                v.wait_ge(RW.xt_made, g + 1)
                v.wait_ge(RW.mixed, g)
                v.tensor_tensor(R_XX.rearrange("p (s t) -> p s t", s=2), R_XT[par][:, :, 0:L],
                                R_XT[par][:, :, 1:L + 1], ALU.subtract).then_inc(RW.mix_steps, 1)

            def mixes(g, par):
                v.wait_ge(RW.g_made, g)
                v.wait_ge(RW.mix_steps, g + 1)
                for i in range(4):
                    last = v.scalar_tensor_tensor(out=R_MIX[:, i, :].rearrange("p (s t) -> p s t", s=2),
                                                  in0=R_XX.rearrange("p (s t) -> p s t", s=2),
                                                  scalar=COLS[:, C_MAA + i:C_MAA + i + 1],
                                                  in1=R_XT[par][:, :, 1:L + 1], op0=ALU.mult, op1=ALU.add)
                last.then_inc(RW.mixed, 1)

            def products(g, par, c):
                v.wait_ge(RW.chunk_steps, 4 * g + c + 1)
                if c == 0:
                    v.wait_ge(RW.r_kept, g + 1)
                if not (isinstance(g, int) and 4 * g + c < 2):
                    v.wait_ge(RW.red_made, 4 * g + c - 1)
                prod = R_P[c % 2].rearrange("p (a n m) -> p a n m", n=HN, m=HN)
                ps = PS[:, 4 + 2 * (c % 2):6 + 2 * (c % 2), :].rearrange("p b (a n m) -> p (b a) n m", n=HN, m=HN)
                r = R_R[par][:, c * P:(c + 1) * P].rearrange("p (a n) -> p a n", n=HN)
                v.tensor_tensor(prod, ps, r.unsqueeze(3).to_broadcast([P, HEADS, HN, HN]), ALU.mult
                                ).then_inc(RW.prod_made, 1)

            def total(g, par, c):
                v.wait_ge(RW.prod_made, 4 * g + c + 1 + CREDIT)
                v.tensor_reduce(R_Y[par][:, c * P:(c + 1) * P].rearrange("p (a m) -> p a m", m=HN),
                                R_P[c % 2].rearrange("p (a n m) -> p a m n", n=HN, m=HN), AX.X, ALU.add
                                ).then_inc(RW.red_made, 1)

            def means(g, par):
                kc.at(g)
                v.wait_ge(RW.red_made, 4 * g + 4)
                v.tensor_reduce(R_SM[:, 0, :], R_Y[par].rearrange("p (a m) -> p a m", m=HN), AX.X, ALU.add
                                ).then_inc(RW.gn_steps, kc.one())

            def center(g, par):
                v.wait_ge(RW.gn_steps, kc.all())
                v.wait_ge(RW.yg_made, g)
                v.scalar_tensor_tensor(out=R_YC.rearrange("p (a m) -> p a m", m=HN),
                                       in0=R_SM[:, 0, :].unsqueeze(2).to_broadcast([P, 64, HN]),
                                       scalar=-1.0 / HN, in1=R_Y[par].rearrange("p (a m) -> p a m", m=HN),
                                       op0=ALU.mult, op1=ALU.add).then_inc(RW.sq_in, 1)

            def sum_squares(g):
                v.wait_ge(RW.sq_made, g + 1)
                v.tensor_reduce(R_SM[:, 1, :], R_SQ.rearrange("p (a m) -> p a m", m=HN), AX.X, ALU.add
                                ).then_inc(RW.sd_in, 1)

            def inverses(g):
                v.wait_ge(RW.sd_made, g + 1)
                v.reciprocal(R_SM[:, 3, :], R_SM[:, 2, :]).then_inc(RW.gn_steps, kc.one())

            def normalize(g):
                v.wait_ge(RW.gn_steps, kc.all())
                v.tensor_tensor(R_YN.rearrange("p t (h m) -> p h t m", m=HN),
                                R_YC.rearrange("p (h t m) -> p h t m", t=GT, m=HN),
                                R_SM[:, 3, :].rearrange("p (h t) -> p h t", t=GT).unsqueeze(3)
                                .to_broadcast([P, HEADS, GT, HN]), ALU.mult).then_inc(RW.yn_made, 1)

            def gate(g, par):
                v.wait_ge(RW.ya_made, g + 1)
                v.wait_ge(RW.g_kept, g + 1)
                v.wait_ge(RW.s_made, g)
                v.tensor_tensor(R_YG, R_YA, R_G[par], ALU.mult).then_inc(RW.yg_made, 1)

            def body(g, par, use, has=(1, 1, 1, 1)):
                before, other = has[1], 1 - par
                if has[2] and before:
                    mixes(g + 1, other)
                if before:
                    means(g - 1, other)
                products(g, par, 0)
                if before:
                    center(g - 1, other)
                total(g, par, 0)
                products(g, par, 1)
                if before:
                    sum_squares(g - 1)
                total(g, par, 1)
                products(g, par, 2)
                if before:
                    inverses(g - 1)
                total(g, par, 2)
                if before:
                    normalize(g - 1)
                products(g, par, 3)
                total(g, par, 3)
                if before:
                    gate(g - 1, other)
                if has[3]:
                    differences(g + 2, par)
            choose, chosen, weights, keep_ranks, running_totals, begins, slots, tiles = route
            choose(CHOSEN_EARLY, NT - CHOSEN_EARLY)
            chosen()
            differences(0, 0)
            mixes(0, 0)
            differences(1, 1)
            weights()
            keep_ranks()
            mixes(1, 1)
            running_totals()
            begins()
            slots()
            tiles()
            all_groups(v, body)
            means(G - 1, (G - 1) % 2)
            center(G - 1, (G - 1) % 2)
            sum_squares(G - 1)
            inverses(G - 1)
            normalize(G - 1)
            gate(G - 1, (G - 1) % 2)

        block = ctx.enter_context(nc.Block())

        @block.sync
        def _(sp):
            row = lambda n: a[n].rearrange("(o d) -> o d", o=1)
            sp.dma_start(TD[:], row("L1_attn_time_decay").to_broadcast([P, HEADS])).then_inc(td_in, 16)
            for par in range(2):
                g = par * (G // 2)
                sp.dma_start(grp(X, g), x_dram[:, g * GT:(g + 1) * GT, :]).then_inc(x_in[par], 16)
            sp.wait_ge(rows_zeroed, 1)
            for c, n, r in ((C_B1[0], "L0_ffn_b1", E * FC), (C_B1[1], "L1_ffn_b1", E * FC)):
                sp.dma_start(ROWS[c:c + r, :], a[n].rearrange("e (c f) -> (e c) f", f=P)).then_inc(cols_in, 16)
            for c, n in ((C_LNG, "L0_ffn_ln_g"), (C_LNB, "L0_ffn_ln_b"), (C_CENT, "L0_ffn_centroids")):
                sp.dma_start(ROWS[c:c + E, :], a[n]).then_inc(cols_in, 16)
            for c, n in ((C_MAA, "time_maa_k"), (C_MAA + 1, "time_maa_v"), (C_MAA + 2, "time_maa_r"),
                         (C_MAA + 3, "time_maa_g"), (C_GNG, "ln_g"), (C_GNB, "ln_b")):
                sp.dma_start(ROWS[c:c + 1, :], row("L1_attn_" + n)).then_inc(cols_in, 16)

            def load_x(i, par, use):
                sp.wait_ge(x_in[par], 16 * use)
                g = use + par * (G // 2)
                sp.dma_start(grp(X, g), x_dram[:, bass.ds(g * GT, GT), :]).then_inc(x_in[par], 16)
            rounds(sp, 2, G - 2, load_x)
            for i, n in enumerate(("w_k", "w_v", "w_r", "w_g", "w_o")):
                sp.dma_start(WNAT[:, i, :], a["L1_attn_" + n]).then_inc(params_in, 16)
            for i, n in enumerate(("Wq", "Wk", "Wv", "Wo")):
                sp.dma_start(WA[:, i, :], a["L0_attn_" + n]).then_inc(params_in, 16)
            sp.dma_start(GWT[:], a["L1_ffn_gate_w"]).then_inc(params_in, 16)
            sp.dma_start(GB[:], row("L1_ffn_gate_b").to_broadcast([P, E])).then_inc(params_in, 16)
            sp.dma_start(TU[:], row("L1_attn_time_faaaa").to_broadcast([P, HEADS])).then_inc(params_in, 16)
            load_b2(sp, 0)
            sp.wait_ge(rows_zeroed, 3)
            for la in range(2):
                fill = disp[la].rearrange("(c p r) d -> c p (r d)", p=P, r=FILL)
                for c in range(FILLS[la]):
                    sp.dma_start(fill[c], EMPTY).then_inc(zero_filled[la], 16)
            sp.wait_ge(zero_filled[0], 16 * FILLS[0])
            barrier(sp, 1)
            sp_attention_loads(sp, 0, A_XS, (AT.xs_in0, AT.xs_in1), AT.turned, XN2, 4)
            barrier(sp, 2)
            sp_experts(sp, 0)
            barrier(sp, 3)
            sp_fetch_pairs(sp)
            barrier(sp, 4)
            sp_attention_loads(sp, 1, R_XS, (RW.xs_in0, RW.xs_in1), RW.turned, XN, 2)
            barrier(sp, 5)
            load_b2(sp, 1)
            sp_experts(sp, 1)
            barrier(sp, 6)
            sp_fetch_y(sp)

        @block.gpsimd
        def _(pool):
            k = Steps(pool_steps)

            def made(ins):
                ins.then_inc(pool_steps, k.one())
                pool.wait_ge(pool_steps, k.all())

            made(pool.memset(ONES[:], 1.0))
            made(pool.affine_select(out=IDENT[:], in_=ONES[:], compare_op=ALU.is_equal, fill=0.0, base=0,
                                    pattern=[[1, P]], channel_multiplier=-1))
            made(pool.affine_select(out=UPPER[:], in_=ONES[:], compare_op=ALU.is_gt, fill=0.0, base=0,
                                    pattern=[[1, P]], channel_multiplier=-1))
            bv = BLOCK[:, 0:D].rearrange("p (h n) -> p h n", n=HN)
            ov = ONES[:].rearrange("p (h n) -> p h n", n=HN)
            made(pool.affine_select(out=bv, in_=ov, compare_op=ALU.is_ge, fill=0.0, base=0,
                                    pattern=[[-HN, HEADS], [0, HN]], channel_multiplier=1))
            made(pool.affine_select(out=bv, in_=bv, compare_op=ALU.is_ge, fill=0.0, base=HN - 1,
                                    pattern=[[HN, HEADS], [0, HN]], channel_multiplier=-1))
            made(pool.affine_select(out=BLOCK[:, D:D + HEADS], in_=ONES[:, 0:HEADS], compare_op=ALU.is_ge, fill=0.0,
                                    base=0, pattern=[[-HN, HEADS]], channel_multiplier=1))
            made(pool.affine_select(out=BLOCK[:, D:D + HEADS], in_=BLOCK[:, D:D + HEADS], compare_op=ALU.is_ge,
                                    fill=0.0, base=HN - 1, pattern=[[HN, HEADS]], channel_multiplier=-1))
            made(pool.iota(IE8[:], [[1, E]], base=-E, channel_multiplier=0, allow_small_or_imprecise_dtypes=True))
            made(pool.iota(ITHR[:], [[SLOT, THR]], base=0, channel_multiplier=0,
                           allow_small_or_imprecise_dtypes=True))
            made(pool.iota(ITILE[:], [[1, MAXT]], base=0, channel_multiplier=0,
                           allow_small_or_imprecise_dtypes=True))
            made(pool.iota(EXPO, [[1, 2 * P]], base=-1, channel_multiplier=-1,
                           allow_small_or_imprecise_dtypes=True))
            made(pool.affine_select(out=EXPO, in_=EXPO, compare_op=ALU.is_ge, fill=0.0, base=-1,
                                    pattern=[[1, 2 * P]], channel_multiplier=-1))
            made(pool.iota(TAG[:, :, 0], [[P, NT]], base=0, channel_multiplier=1,
                           allow_small_or_imprecise_dtypes=True))
            pool.wait_ge(rows_zeroed, 2)
            pool.iota(EMPTY.rearrange("p (r w) -> p r w", w=ROW)[:, :, D], [[1, FILL]], base=NO_TOKEN,
                      channel_multiplier=FILL, allow_small_or_imprecise_dtypes=True).then_inc(rows_zeroed, 1)
            for i, eps in enumerate((LN_EPS, DEN_EPS, GN_EPS)):
                made(pool.memset(EPSC[:, i:i + 1], eps))
            pool.memset(ZERO4[:], 0.0).then_inc(consts_made, 1)
            pool_norm(pool)
            barrier(pool, 1)
            pool.wait_ge(exp_made, HEADS)
            for h in range(HEADS):
                d = TOEP[:, h, 0:P]
                pool.affine_select(out=d, in_=d, compare_op=ALU.is_ge, fill=0.0, base=-1,
                                   pattern=[[1, P]], channel_multiplier=-1).then_inc(toep_cut, 1)
            pool_send(pool, 0, None)
            barrier(pool, 2)
            pool_store_y(pool, 0)
            barrier(pool, 3)
            pool_merge(pool)
            barrier(pool, 4)

            def kv_products(g, par):
                hold(pool, RW.v_kept, g + 1)
                if not (isinstance(g, int) and g < 2):
                    hold(pool, RW.chunk_steps, 4 * g - 4)
                pool.tensor_tensor(
                    KV[par].rearrange("p (a n m) -> p a n m", n=HN, m=HN),
                    R_K.rearrange("p (a n) -> p a n", n=HN).unsqueeze(3).to_broadcast([P, 64, HN, HN]),
                    R_V.rearrange("p (a m) -> p a m", m=HN).unsqueeze(2).to_broadcast([P, 64, HN, HN]),
                    ALU.mult).then_inc(RW.kv_made, 1)
            pool_send(pool, 1, kv_products)
            barrier(pool, 5)
            pool_store_y(pool, 1)
            barrier(pool, 6)
            pool_combine(pool)

        @block.tensor
        def _(pe):
            pe.wait_ge(consts_made, 1)
            pe.wait_ge(cols_in, COL_PARAMS)
            pe.transpose(PS[:, 0, 0:P], ROWS, IDENT[:]).then_inc(cols_turned, 1)
            pe.wait_ge(cols_kept, 1)
            pe_norm(pe, 0)
            pe.wait_ge(params_in, PARAMS)
            for i in range(5):
                last = pe.transpose(PS[:, 6 + i // 4, i % 4 * P:(i % 4 + 1) * P], WNAT[:, i, :], IDENT[:])
            last.then_inc(wt_turned, 1)
            barrier(pe, 1)
            pe_linear_attention(pe)
            barrier(pe, 2)
            pe_experts(pe, 0)
            barrier(pe, 3)
            pe_norm(pe, 1)
            barrier(pe, 4)
            pe_recurrence(pe)
            barrier(pe, 5)
            pe_experts(pe, 1)
            barrier(pe, 6)

        @block.scalar
        def _(act):
            act.wait_ge(td_in, 16)
            nc.scalar.activation(LW[:], TD[:], ACT.Exp).then_inc(lw_made, 1)
            act_norm(act)
            act.wait_ge(wt_turned, 1)
            wt = WT[:].rearrange("p a b -> p (a b)")
            nc.scalar.activation(wt[:, 0:GW], PS[:, 6, :], ACT.Copy)
            nc.scalar.activation(wt[:, GW:5 * D], PS[:, 7, 0:D], ACT.Copy)
            barrier(act, 1)
            act_linear_attention(act)
            barrier(act, 2)
            act_experts(act, 0, ACT.Relu)
            barrier(act, 3)
            act_merge(act)
            barrier(act, 4)
            act_recurrence(act)
            barrier(act, 5)
            act_experts(act, 1, ACT.Gelu)
            barrier(act, 6)
            act_combine(act)

        @block.vector
        def _(v):
            v.memset(ROWS, 0.0).then_inc(rows_zeroed, 1)
            v.memset(EMPTY, 0.0).then_inc(rows_zeroed, 1)
            v.wait_ge(lw_made, 1)
            v.tensor_scalar(LW[:], LW[:], 1.0e4, -1.0, ALU.min, ALU.mult).then_inc(lw_made, 1)
            dve_norm(v)
            barrier(v, 1)
            dve_linear_attention(v)
            barrier(v, 2)
            dve_experts(v, 0)
            barrier(v, 3)
            route = dve_route(v, 1)
            dve_merge(v, route[0])
            barrier(v, 4)
            dve_recurrence(v, route)
            barrier(v, 5)
            dve_experts(v, 1)
            barrier(v, 6)
            dve_combine(v)


_INS = ['L0_attn_x', 'L0_attn_Wq', 'L0_attn_Wk', 'L0_attn_Wv', 'L0_attn_Wo', 'L0_ffn_centroids', 'L0_ffn_ln_g',
        'L0_ffn_ln_b', 'L0_ffn_W1', 'L0_ffn_b1', 'L0_ffn_W2', 'L0_ffn_b2', 'L1_attn_w_r', 'L1_attn_w_k',
        'L1_attn_w_v', 'L1_attn_w_g', 'L1_attn_w_o', 'L1_attn_time_maa_k', 'L1_attn_time_maa_v',
        'L1_attn_time_maa_r', 'L1_attn_time_maa_g', 'L1_attn_time_decay', 'L1_attn_time_faaaa', 'L1_attn_ln_g',
        'L1_attn_ln_b', 'L1_ffn_gate_w', 'L1_ffn_gate_b', 'L1_ffn_w1', 'L1_ffn_b1', 'L1_ffn_w2', 'L1_ffn_b2']


def kernel(**inputs):
    import numpy as _np
    import concourse.bacc as _bacc
    from concourse import mybir as _mybir
    from concourse.bass_utils import run_bass_kernel_spmd as _run

    nc = _bacc.Bacc("TRN2", target_bir_lowering=False, num_devices=1)
    arrays, args = {}, {}
    for name in _INS:
        arr = _np.ascontiguousarray(inputs[name])
        arrays[f"in_{name}"] = arr
        args[name] = nc.dram_tensor(f"in_{name}", arr.shape, _mybir.dt.from_np(arr.dtype), kind="ExternalInput").ap()
    out = nc.dram_tensor("out_0", (B, L, D), _mybir.dt.float32, kind="ExternalOutput").ap()
    program(nc, args, out)
    r = _run(nc, [arrays], core_ids=[0])
    return r.results[0]["out_0"]
```
